# Optimizing a Trainium2 kernel written in Bass

```python
import numpy as np
import jax
import jax.numpy as jnp

def _softmax(x, axis=-1):
    return jax.nn.softmax(x, axis=axis)

def _gelu(x):
    return jax.nn.gelu(x, approximate=True)

def _silu(x):
    return jax.nn.silu(x)

def _sigmoid(x):
    return jax.nn.sigmoid(x)

def _layernorm(x, axis=-1, eps=1e-05):
    m = jnp.mean(x, axis=axis, keepdims=True)
    v = jnp.var(x, axis=axis, keepdims=True)
    return (x - m) / jnp.sqrt(v + eps)

def _scatter_add(tgt, idx, src, axis=0):
    return tgt.at[idx].add(src)

def _segment_sum(src, seg, n):
    return jax.ops.segment_sum(src, seg, n)
kernel_name = 'mk_adaln_d1_jaxref_r4_151434'

def setup_inputs(seed: int=0):
    np.random.seed(seed)
    _w = jnp.asarray

    def _L0_attn_setup():
        import jax, jax.numpy as jnp
        import numpy as np
        import math
        B, S, DIM, HEADS = (2, 512, 256, 16)

        def _alibi_slopes(n_heads):

            def pow2_slopes(n):
                start = 2 ** (-2 ** (-(math.log2(n) - 3)))
                return [start * start ** i for i in range(n)]
            if math.log2(n_heads).is_integer():
                slopes = pow2_slopes(n_heads)
            else:
                closest = 2 ** math.floor(math.log2(n_heads))
                slopes = pow2_slopes(closest)
                slopes += pow2_slopes(2 * closest)[0::2][:n_heads - closest]
            return np.asarray(slopes, dtype=np.float32).reshape(n_heads, 1, 1)
        key = jax.random.key(seed)
        k1, k2, k3 = jax.random.split(key, 3)
        x = jax.random.normal(k1, (B, S, DIM), dtype=jnp.float32)
        W_qkv = jax.random.normal(k2, (3 * DIM, DIM), dtype=jnp.float32) * 0.02
        W_o = jax.random.normal(k3, (DIM, DIM), dtype=jnp.float32) * 0.02
        return {'x': x, 'W_qkv': W_qkv, 'W_o': W_o}
    _L0_attn_in = _L0_attn_setup()

    def _L0_ffn_setup():
        import jax, jax.numpy as jnp
        import numpy as np
        D_MODEL = 256
        D_HIDDEN = 1024
        N_EXPERTS = 8
        B, S = (2, 512)
        key = jax.random.key(seed)
        ks = jax.random.split(key, 4)
        sd = 1.0 / np.sqrt(D_MODEL)
        sh = 1.0 / np.sqrt(D_HIDDEN)
        return {'x': jax.random.normal(ks[0], (B, S, D_MODEL), dtype=jnp.float32), 'Wg': jax.random.normal(ks[1], (D_MODEL, N_EXPERTS), dtype=jnp.float32) * sd, 'bg': jnp.zeros((N_EXPERTS,), dtype=jnp.float32), 'W1': jax.random.normal(ks[2], (N_EXPERTS, D_MODEL, D_HIDDEN), dtype=jnp.float32) * sd, 'b1': jnp.zeros((N_EXPERTS, D_HIDDEN), dtype=jnp.float32), 'W2': jax.random.normal(ks[3], (N_EXPERTS, D_HIDDEN, D_MODEL), dtype=jnp.float32) * sh, 'b2': jnp.zeros((N_EXPERTS, D_MODEL), dtype=jnp.float32)}
    _L0_ffn_in = _L0_ffn_setup()
    _L0_c = _w((lambda *s: np.random.randn(*s).astype(np.float32) * 0.05)(2, 256))
    _L0_wmod = _w((lambda *s: np.random.randn(*s).astype(np.float32) * 0.05)(256, 6 * 256) * 256 ** (-0.5))
    _d = {'L0_attn_x': _L0_attn_in['x'], 'L0_attn_W_qkv': _L0_attn_in['W_qkv'], 'L0_attn_W_o': _L0_attn_in['W_o'], 'L0_ffn_Wg': _L0_ffn_in['Wg'], 'L0_ffn_bg': _L0_ffn_in['bg'], 'L0_ffn_W1': _L0_ffn_in['W1'], 'L0_ffn_b1': _L0_ffn_in['b1'], 'L0_ffn_W2': _L0_ffn_in['W2'], 'L0_ffn_b2': _L0_ffn_in['b2'], 'L0_c': _L0_c, 'L0_wmod': _L0_wmod}
    _x0 = _d['L0_attn_x']
    _d['L0_attn_x'] = jax.random.normal(jax.random.fold_in(jax.random.key(seed), 1), (2, 2048, 256), dtype=_x0.dtype)
    del _x0
    return _d

def reference(L0_attn_x, L0_attn_W_qkv, L0_attn_W_o, L0_ffn_Wg, L0_ffn_bg, L0_ffn_W1, L0_ffn_b1, L0_ffn_W2, L0_ffn_b2, L0_c, L0_wmod):

    def _L0_attn_ref(x, W_qkv, W_o):
        import jax, jax.numpy as jnp
        import numpy as np
        import math
        B, S, DIM, HEADS = (2, 512, 256, 16)

        def _alibi_slopes(n_heads):

            def pow2_slopes(n):
                start = 2 ** (-2 ** (-(math.log2(n) - 3)))
                return [start * start ** i for i in range(n)]
            if math.log2(n_heads).is_integer():
                slopes = pow2_slopes(n_heads)
            else:
                closest = 2 ** math.floor(math.log2(n_heads))
                slopes = pow2_slopes(closest)
                slopes += pow2_slopes(2 * closest)[0::2][:n_heads - closest]
            return np.asarray(slopes, dtype=np.float32).reshape(n_heads, 1, 1)
        b, s, d = x.shape
        h = HEADS
        hd = d // h
        scale = hd ** (-0.5)
        qkv = x @ W_qkv.T
        q, k, v = jnp.split(qkv, 3, axis=-1)
        q = q.reshape(b, s, h, hd).transpose(0, 2, 1, 3)
        k = k.reshape(b, s, h, hd).transpose(0, 2, 1, 3)
        v = v.reshape(b, s, h, hd).transpose(0, 2, 1, 3)
        scores = jnp.einsum('bhqd,bhkd->bhqk', q, k) * scale
        pos = jnp.arange(s)
        rel = (pos[None, :] - pos[:, None]).astype(scores.dtype)
        slopes = jnp.asarray(_alibi_slopes(h))
        scores = scores - slopes * rel
        causal_mask = pos[None, :] > pos[:, None]
        scores = jnp.where(causal_mask, jnp.finfo(scores.dtype).min, scores)
        weights = jax.nn.softmax(scores, axis=-1)
        out = jnp.einsum('bhqk,bhkd->bhqd', weights, v)
        out = out.transpose(0, 2, 1, 3).reshape(b, s, d)
        return out @ W_o.T

    def _L0_ffn_ref(x, Wg, bg, W1, b1, W2, b2):
        import jax, jax.numpy as jnp
        import numpy as np
        D_MODEL = 256
        D_HIDDEN = 1024
        N_EXPERTS = 8
        B, S = (2, 512)
        logits = jnp.einsum('bsd,de->bse', x, Wg) + bg
        expert_idx = jnp.argmax(logits, axis=-1)
        h = jax.nn.gelu(jnp.einsum('bsd,edh->bseh', x, W1) + b1, approximate=False)
        y = jnp.einsum('bseh,ehd->bsed', h, W2) + b2
        out = jnp.take_along_axis(y, expert_idx[:, :, None, None], axis=2)[:, :, 0, :]
        return out
    x = L0_attn_x
    mod = (_silu(L0_c) @ L0_wmod).reshape(L0_c.shape[0], 6, 1, -1)
    sa, ca, ga, sb, cb, gb = (mod[:, 0], mod[:, 1], mod[:, 2], mod[:, 3], mod[:, 4], mod[:, 5])
    ga = (2 * (ga >= 0) - 1) * jnp.maximum(jnp.abs(ga), 0.25)
    gb = (2 * (gb >= 0) - 1) * jnp.maximum(jnp.abs(gb), 0.25)
    h = _layernorm(x, axis=-1) * (1 + ca) + sa
    x = x + ga * _L0_attn_ref(h, L0_attn_W_qkv, L0_attn_W_o)
    h = _layernorm(x, axis=-1) * (1 + cb) + sb
    x = x + gb * _L0_ffn_ref(h, L0_ffn_Wg, L0_ffn_bg, L0_ffn_W1, L0_ffn_b1, L0_ffn_W2, L0_ffn_b2)
    return x

_drawn_inputs = setup_inputs


def setup_inputs(seed=0):
    import zlib

    import numpy as np

    out = dict(_drawn_inputs(seed))
    spreads = {'L0_ffn_bg': (0.0, 0.1), 'L0_ffn_b1': (0.0, 0.465), 'L0_ffn_b2': (0.0, 0.321)}
    factors = {'L0_attn_W_qkv': 3.097, 'L0_attn_W_o': 3.676}
    for name, (base, spread) in spreads.items():
        noise = np.random.default_rng([zlib.crc32(name.encode()), seed]).standard_normal(out[name].shape)
        drawn = base * np.exp(spread * noise) if base else spread * noise
        out[name] = jnp.asarray(drawn.astype(out[name].dtype))
    for name, factor in factors.items():
        out[name] = (out[name] * factor).astype(out[name].dtype)
    return out
```

```python
import concourse.bass as bass
from concourse import mybir
from contextlib import ExitStack
import numpy as np

fp32 = mybir.dt.float32
bf16 = mybir.dt.bfloat16
i32 = mybir.dt.int32
ALU = mybir.AluOpType
ACT = mybir.ActivationFunctionType
AX = mybir.AxisListType

P = 128
B, S, D, H = 2, 2048, 256, 16
HD = D // H
KC = D // P
NTOK = B * S
CH = 512
TPC = CH // P
NCH = NTOK // CH
CPB = S // CH
NT = NTOK // P
G = 4
NG = H // G
HW = 32
NIT = B * NG
E, F = 8, 1024
FC = F // P
SLOTS = NT + E - 1
EPS = 1e-5
SCALE = HD ** -0.5
Q_PART = [0, 0, 1, 0, 1, 2]
K_PART = [0, 1, 0, 2, 1, 0]
R_POS = 6 * HD
R_MAX = R_POS + 3
R_ALL = R_MAX + 3
PIECE = 1024
LAG = 74

C_ID, C_MQ, C_MK, C_TRI, C_SEL, C_SMALL = 0, P, 2 * P, 3 * P, 4 * P, 5 * P
C_RANK, C_THR, C_TILE, C_END = C_SMALL, C_SMALL + E, C_SMALL + E + NT, C_SMALL + E + NT + SLOTS + 1


class Tensors:
    pass


def max_pieces():
    out = []
    for c in range(CPB):
        for j in range(G):
            for t in range(TPC):
                n = (c * TPC + t + 1) * P
                k = -(-n // PIECE)
                cut = [P * ((n // P) * i // k) for i in range(k + 1)]
                for i in range(k):
                    out.append((c, j, t, i, cut[i], cut[i + 1], i == k - 1))
    return out


PIECES = max_pieces()
NP = len(PIECES)
STEPS = [(c, kb) for c in range(CPB) for kb in range(TPC * (c + 1))]
NS = len(STEPS)
CHUNK_END = [max(k for k, p in enumerate(PIECES) if p[0] == c) for c in range(CPB)]


def step_cols(c, kb):
    return max(0, kb - c * TPC) * P


def plan(ahead):
    ends = np.cumsum([(p[5] - p[4]) / CH for p in PIECES])
    first = int(np.searchsorted(ends, LAG))
    todo = [(ends[k], 0, k) for k in range(first, NP)]
    if ahead:
        todo += [(ends[-1] + ends[k], 1, k) for k in range(first)]
    late = []

    def piece():
        _, di, k = todo.pop(0)
        yield ("max", di, k)
        if k in CHUNK_END:
            late.append((s + 2, ("rows", di, CHUNK_END.index(k))))

    at = 0.0
    for s, (c, kb) in enumerate(STEPS):
        yield ("step", s)
        for x in [x for x in late if x[0] <= s]:
            late.remove(x)
            yield x[1]
        at += G * (CH - step_cols(c, kb)) / CH
        while todo and todo[0][0] <= at + LAG:
            yield from piece()
        if kb == TPC * (c + 1) - 1 and s + 1 < NS:
            late += [(s + 1, ("take", c)), (s + 3, ("norm", c))]
    while todo:
        yield from piece()
    for x in late:
        yield x[1]
    yield ("last",)
    yield ("take", CPB - 1)
    yield ("norm", CPB - 1)


def plan_before():
    first = int(np.searchsorted(np.cumsum([(p[5] - p[4]) / CH for p in PIECES]), LAG))
    for k in range(first):
        yield ("max", 0, k)
        if k - 3 in CHUNK_END:
            yield ("rows", 0, CHUNK_END.index(k - 3))


def open_stage(nc, ctx):
    def sb(name, shape, dt=fp32):
        return ctx.enter_context(nc.sbuf_tensor(name, shape, dt))

    def pb(name, shape, dt=fp32):
        return ctx.enter_context(nc.psum_tensor(name, shape, dt))

    def sem(name):
        return ctx.enter_context(nc.semaphore(name))

    return sb, pb, sem


def stage_setup(nc, g):
    with ExitStack() as ctx:
        sb, pb, sem = open_stage(nc, ctx)
        wmod = sb("wmod", [P, KC, 6 * D])
        cT = sb("cT", [P, KC, B])
        ex = sb("ex", [P, KC, B])
        e1 = sb("e1", [P, KC, B])
        rc = sb("rc", [P, KC, B])
        sc = sb("sc", [P, KC, B])
        scb = sb("scb", [P, B, KC, P])
        ones = sb("ones0", [P, P])
        sgn = sb("sgn", [P, B, 2, D])
        val = sb("val", [P, B, 2, D])
        mag = sb("mag", [P, B, 2, D])
        al = sb("al", [H, S])
        alr = sb("alr", [H, S])
        alp = sb("alp", [H, 3, S], bf16)
        bb = sb("bb", [P, (E * F + E * D) // P])
        bbr = sb("bbr", [P, (E * F + E * D) // P])
        bbp = sb("bbp", [P, 3, (E * F + E * D) // P], bf16)
        zero = sb("zero", [P, TPC, D])
        ps_col = pb("ps_col", [P, 8, B])
        ps_row = pb("ps_row", [P, 2, CH])
        loaded, wmod_in, al_in, bb_in = sem("loaded"), sem("wmod_in"), sem("al_in"), sem("bb_in")
        exp_done, silu_done, cols_done, rows_done, rows_read = (
            sem("exp_done"), sem("silu_done"), sem("cols_done"), sem("rows_done"), sem("rows_read"))
        dve, pool, ones_set, stored, weights = (
            sem("dve_chain"), sem("pool_chain"), sem("ones_set"), sem("stored"), sem("weights"))
        nb1 = E * F // P
        with nc.Block() as block:
            @block.sync
            def _(sp):
                sp.dma_start(cT[:], g.cT).then_inc(loaded, 16)
                sp.dma_start(g.const[:], g.const_dram).then_inc(loaded, 16)
                sp.dma_start(wmod[:], g.wmod.rearrange("(k p) n -> p k n", p=P)).then_inc(wmod_in, 16)
                sp.dma_start(al[:], g.alibi).then_inc(al_in, 16)
                sp.dma_start(bb[:, 0:nb1], g.b1.rearrange("e (a n) -> (e a) n", n=nb1)).then_inc(bb_in, 16)
                sp.dma_start(bb[:, nb1:], g.b2.rearrange("e (a n) -> (e a) n", n=E * D // P)).then_inc(bb_in, 16)
                sp.dma_start(g.wqkv[:], g.wqkvT.rearrange("(k p) n -> p k n", p=P)).then_inc(weights, 16)
                sp.wait_ge(pool, 5)
                for b in range(B):
                    sp.dma_start(g.pos_rows[b * NG:(b + 1) * NG].rearrange("g j s t -> (g j) s t"),
                                 alp[:]).then_inc(stored, 16)
                sp.wait_ge(pool, 10)
                sp.dma_start(g.b1_rows.rearrange("s (p n) -> p s n", p=P), bbp[:, :, 0:nb1]).then_inc(stored, 16)
                sp.dma_start(g.b2_rows.rearrange("s (p n) -> p s n", p=P), bbp[:, :, nb1:]).then_inc(stored, 16)
                sp.wait_ge(pool, 11)
                for i in range(0, SLOTS + 2, TPC):
                    n = min(TPC, SLOTS + 2 - i)
                    sp.dma_start(g.sorted_h[i * P:(i + n) * P, :].rearrange("(n p) d -> p n d", p=P),
                                 zero[:, 0:n, :]).then_inc(stored, 16)
                sp.wait_ge(weights, 16)
                sp.wait_ge(stored, 16 * (B + 2 + -(-(SLOTS + 2) // TPC)))

            @block.gpsimd
            def _(gp):
                def link(ins):
                    link.n += 1
                    ins.then_inc(pool, 1)
                    gp.wait_ge(pool, link.n)
                link.n = 0
                for src, rest, parts, ready in ((al, alr, alp, al_in), (bb, bbr, bbp, bb_in)):
                    gp.wait_ge(ready, 16 if src is al else 32)
                    link(nc.gpsimd.tensor_copy(parts[:, 0, :], src[:]))
                    link(nc.gpsimd.tensor_tensor(rest[:], src[:], parts[:, 0, :], ALU.subtract))
                    link(nc.gpsimd.tensor_copy(parts[:, 1, :], rest[:]))
                    link(nc.gpsimd.tensor_tensor(rest[:], rest[:], parts[:, 1, :], ALU.subtract))
                    link(nc.gpsimd.tensor_copy(parts[:, 2, :], rest[:]))
                link(nc.gpsimd.memset(zero[:], 0.0))

            @block.scalar
            def _(act):
                act.wait_ge(loaded, 32)
                nc.scalar.activation(ex[:], cT[:], ACT.Exp, scale=-1.0).then_inc(exp_done, 1)

            @block.vector
            def _(v):
                def link(ins):
                    link.n += 1
                    ins.then_inc(dve, 1)
                    v.wait_ge(dve, link.n)
                link.n = 0
                v.wait_ge(loaded, 32)
                nc.vector.memset(ones[:], 1.0)
                nc.vector.tensor_copy(g.ident_b[:], g.const[:, C_ID:C_ID + P])
                nc.vector.tensor_copy(g.mask_q[:], g.const[:, C_MQ:C_MQ + P])
                link(nc.vector.tensor_copy(g.mask_k[:], g.const[:, C_MK:C_MK + P]))
                v.wait_ge(exp_done, 1)
                link(nc.vector.tensor_scalar(e1[:], ex[:], 1.0, None, ALU.add))
                link(nc.vector.reciprocal(rc[:], e1[:]))
                link(nc.vector.tensor_tensor(sc[:], rc[:], cT[:], ALU.mult))
                for b in range(B):
                    for k in range(KC):
                        last = nc.vector.tensor_scalar(scb[:, b, k, :], ones[:], sc[:, k, b:b + 1], None, ALU.mult)
                last.then_inc(silu_done, 1)
                v.wait_ge(cols_done, 1)
                nc.vector.tensor_copy(g.shift[:], ps_col[:, 0:KC, :])
                nc.vector.tensor_scalar(g.gain[:], ps_col[:, KC:2 * KC, :], 1.0, None, ALU.add)
                for b in range(B):
                    v.wait_ge(rows_done, b + 1)
                    nc.vector.tensor_copy(g.mod[:, b, 1, :], ps_row[:, 0, D:2 * D])
                    nc.vector.tensor_scalar(g.mod[:, b, 2, :], ps_row[:, 1, 0:D], 1.0, None, ALU.add)
                    for i, gate in ((0, ps_row[:, 0, 0:D]), (1, ps_row[:, 1, D:2 * D])):
                        nc.vector.tensor_scalar(sgn[:, b, i, :], gate, 0.0, 2.0, ALU.is_ge, ALU.mult)
                        link(nc.vector.tensor_copy(val[:, b, i, :], gate))
                        last = nc.vector.scalar_tensor_tensor(mag[:, b, i, :], gate, -1.0, val[:, b, i, :],
                                                              ALU.mult, ALU.max)
                    last.then_inc(rows_read, 1)
                    v.wait_ge(rows_read, b + 1)
                    link(nc.vector.tensor_scalar(mag[:, b, :, :], mag[:, b, :, :], 0.25, None, ALU.max))
                    for i, row in ((0, 0), (1, 3)):
                        link(nc.vector.scalar_tensor_tensor(g.mod[:, b, row, :], sgn[:, b, i, :], 1.0,
                                                            mag[:, b, i, :], ALU.subtract, ALU.mult))

            @block.tensor
            def _(pe):
                pe.wait_ge(silu_done, 1)
                pe.wait_ge(wmod_in, 16)
                for n in range(2 * KC):
                    for k in range(KC):
                        last = nc.tensor.matmul(ps_col[:, n, :], wmod[:, k, n * P:(n + 1) * P], sc[:, k, :],
                                                start=(k == 0), stop=(k == KC - 1))
                last.then_inc(cols_done, 1)
                for b in range(B):
                    if b:
                        pe.wait_ge(rows_read, b)
                    for n in range(2):
                        for k in range(KC):
                            last = nc.tensor.matmul(ps_row[:, n, :], scb[:, b, k, :],
                                                    wmod[:, k, 2 * D + n * CH:2 * D + (n + 1) * CH],
                                                    start=(k == 0), stop=(k == KC - 1))
                    last.then_inc(rows_done, 1)


def stage_qkv(nc, g):
    with ExitStack() as ctx:
        sb, pb, sem = open_stage(nc, ctx)
        xt = sb("xt", [P, 2, TPC, D])
        st = sb("st", [P, TPC, 6])
        mv = sb("mv", [P, TPC, 2])
        ve, sd, rs = sb("ve", [P, TPC]), sb("sd", [P, TPC]), sb("rs", [P, TPC])
        xn = sb("xn", [P, 2, TPC, D])
        hT = sb("hT", [P, 2, KC, CH])
        rest = sb("rest", [P, 2, CH])
        parts = sb("parts", [P, 2, 3, CH], bf16)
        vp = sb("vp", [P, 2, 2, H, HW])
        ps_t = pb("ps_t", [P, KC, CH])
        ps_q = pb("ps_q", [P, 2, CH])
        ps_v = pb("ps_v", [P, 2, 2, D])
        x_in = [sem(f"x_in{i}") for i in range(2)]
        dve, normed, turned, moded = sem("dve_chain1"), sem("normed"), sem("turned"), sem("moded")
        qk_done, part1, rest_done, pool, v_done, v_set = (
            sem("qk_done"), sem("part1"), sem("rest_done"), sem("pool1"), sem("v_done"), sem("v_set"))
        parts_out = [sem(f"parts_out{i}") for i in range(2)]
        v_out = [sem(f"v_out{i}") for i in range(2)]
        vp_set, var_done, sd_done = sem("vp_set"), sem("var_done"), sem("sd_done")
        x_v = g.x.rearrange("b (n t p) d -> (b n) p t d", p=P, t=TPC)
        v_v = g.v_rows.rearrange("(b g) (n p) c -> b n p g c", b=B, p=P)
        NF = 4

        with nc.Block() as block:
            @block.sync
            def _(sp):
                for n in range(2):
                    sp.dma_start(xt[:, n, :, :], x_v[n]).then_inc(x_in[n], 16)
                for n in range(NCH):
                    b, c = n // CPB, n % CPB
                    for f in range(NF):
                        u = n * NF + f
                        sp.wait_ge(pool, 3 * (u + 1))
                        for half in range(2):
                            sp.dma_start(
                                g.qk_rows[b * NG + (f % 2) * 2 + half, f // 2, :, :, c * CH:(c + 1) * CH]
                                .rearrange("s r t -> r s t"),
                                parts[half * 64:(half + 1) * 64, u % 2, :, :]).then_inc(parts_out[u % 2], 16)
                    for w in range(2):
                        u = n * 2 + w
                        sp.wait_ge(v_set, u + 1)
                        for i in range(2):
                            tile = c * TPC + 2 * w + i
                            sp.dma_start(v_v[b, tile], vp[:, u % 2, i, :, :].rearrange("p (g j) c -> p g (j c)", g=NG)
                                         ).then_inc(v_out[u % 2], 16)
                    if n + 2 < NCH:
                        sp.wait_ge(normed, n + 1)
                        sp.dma_start(xt[:, n % 2, :, :], x_v[n + 2]).then_inc(x_in[n % 2], 16)
                for i in range(2):
                    sp.wait_ge(parts_out[i], 32 * NCH * NF // 2)
                    sp.wait_ge(v_out[i], 32 * NCH)

            @block.vector
            def _(v):
                def link(ins):
                    link.n += 1
                    ins.then_inc(dve, 1)
                    v.wait_ge(dve, link.n)
                link.n = 0

                def norm(n):
                    v.wait_ge(x_in[n % 2], 16 * (n // 2 + 1))
                    for t in range(TPC):
                        last = nc.vector.bn_stats(st[:, t, :], xt[:, n % 2, t, :])
                    link(last)
                    for t in range(TPC):
                        last = nc.vector.bn_aggr(mv[:, t, :], st[:, t, :])
                    link(last)
                    nc.vector.tensor_scalar(ve[:], mv[:, :, 1], EPS, None, ALU.add).then_inc(var_done, 1)
                    v.wait_ge(sd_done, n + 1)
                    link(nc.vector.reciprocal(rs[:], sd[:]))
                    if n >= 2:
                        v.wait_ge(turned, n - 1)
                    for t in range(TPC):
                        last = nc.vector.tensor_scalar(xn[:, n % 2, t, :], xt[:, n % 2, t, :], mv[:, t, 0:1],
                                                       rs[:, t:t + 1], ALU.subtract, ALU.mult)
                    last.then_inc(normed, 1)
                    v.wait_ge(normed, n + 1)

                for i in range(2):
                    nc.vector.memset(vp[:, i, :, :, HD:HW], 0.0).then_inc(vp_set, 1)
                v.wait_ge(vp_set, 2)
                for i in range(2):
                    nc.vector.memset(vp[:, i, :, :, HD:HD + 1], 1.0).then_inc(vp_set, 1)
                norm(0)
                for n in range(NCH):
                    for f in range(NF):
                        u = n * NF + f
                        v.wait_ge(part1, u + 1)
                        if u >= 2:
                            v.wait_ge(pool, 3 * (u - 1))
                        nc.vector.scalar_tensor_tensor(rest[:, u % 2, :], ps_q[:, u % 2, :],
                                                       SCALE if f < 2 else 1.0, parts[:, u % 2, 0, :],
                                                       ALU.mult, ALU.subtract).then_inc(rest_done, 1)
                        if f == 1 and n + 1 < NCH:
                            norm(n + 1)
                    for w in range(2):
                        u = n * 2 + w
                        v.wait_ge(v_done, u + 1)
                        if u >= 2:
                            v.wait_ge(v_out[u % 2], 32 * (u // 2))
                        for i in range(2):
                            last = nc.vector.tensor_copy(vp[:, u % 2, i, :, 0:HD],
                                                         ps_v[:, u % 2, i, :].rearrange("p (h c) -> p h c", c=HD))
                        last.then_inc(v_set, 1)

            @block.scalar
            def _(act):
                def modulate(n):
                    act.wait_ge(turned, n + 1)
                    if n >= 2:
                        act.wait_ge(v_done, 2 * (n - 1))
                    for k in range(KC):
                        last = nc.scalar.activation(hT[:, n % 2, k, :], ps_t[:, k, :], ACT.Identity,
                                                    bias=g.shift[:, k, n // CPB:n // CPB + 1],
                                                    scale=g.gain[:, k, n // CPB:n // CPB + 1])
                    last.then_inc(moded, 1)

                def deviation(n):
                    act.wait_ge(var_done, n + 1)
                    nc.scalar.activation(sd[:], ve[:], ACT.Sqrt).then_inc(sd_done, 1)

                deviation(0)
                modulate(0)
                for n in range(NCH):
                    for f in range(NF):
                        u = n * NF + f
                        if f == 2 and n + 1 < NCH:
                            deviation(n + 1)
                        act.wait_ge(qk_done, u + 1)
                        if u >= 2:
                            act.wait_ge(parts_out[u % 2], 32 * (u // 2))
                        nc.scalar.activation(parts[:, u % 2, 0, :], ps_q[:, u % 2, :], ACT.Copy,
                                             scale=SCALE if f < 2 else 1.0).then_inc(part1, 1)
                    if n + 1 < NCH:
                        modulate(n + 1)

            @block.gpsimd
            def _(gp):
                def link(ins):
                    link.n += 1
                    ins.then_inc(pool, 1)
                    gp.wait_ge(pool, link.n)
                link.n = 0
                for u in range(NCH * NF):
                    gp.wait_ge(rest_done, u + 1)
                    link(nc.gpsimd.tensor_copy(parts[:, u % 2, 1, :], rest[:, u % 2, :]))
                    link(nc.gpsimd.tensor_tensor(rest[:, u % 2, :], rest[:, u % 2, :], parts[:, u % 2, 1, :],
                                                 ALU.subtract))
                    link(nc.gpsimd.tensor_copy(parts[:, u % 2, 2, :], rest[:, u % 2, :]))

            @block.tensor
            def _(pe):
                def turn(n):
                    pe.wait_ge(normed, n + 1)
                    if n:
                        pe.wait_ge(moded, n)
                    for k in range(KC):
                        for t in range(TPC):
                            last = nc.tensor.transpose(ps_t[:, k, t * P:(t + 1) * P],
                                                       xn[:, n % 2, t, k * P:(k + 1) * P], g.const[:, C_ID:C_ID + P])
                    last.then_inc(turned, 1)

                turn(0)
                for n in range(NCH):
                    pe.wait_ge(moded, n + 1)
                    for f in range(NF):
                        u = n * NF + f
                        if u >= 2:
                            pe.wait_ge(rest_done, u - 1)
                        for k in range(KC):
                            last = nc.tensor.matmul(ps_q[:, u % 2, :], g.wqkv[:, k, f * P:(f + 1) * P],
                                                    hT[:, n % 2, k, :], start=(k == 0), stop=(k == KC - 1))
                        last.then_inc(qk_done, 1)
                    if n + 1 < NCH:
                        turn(n + 1)
                    for w in range(2):
                        u = n * 2 + w
                        if u >= 2:
                            pe.wait_ge(v_set, u - 1)
                        for i in range(2):
                            t = 2 * w + i
                            for k in range(KC):
                                last = nc.tensor.matmul(ps_v[:, u % 2, i, :], hT[:, n % 2, k, t * P:(t + 1) * P],
                                                        g.wqkv[:, k, 2 * D:3 * D], start=(k == 0), stop=(k == KC - 1))
                        last.then_inc(v_done, 1)


def stage_attention(nc, g):
    with ExitStack() as ctx:
        sb, pb, sem = open_stage(nc, ctx)
        kh = sb("kh", [P, 2, G, S], bf16)
        qh = sb("qh", [P, 2, G, S], bf16)
        vh = sb("vh", [P, 2, S // P, P])
        pr = sb("pr", [P, 2, G, CH])
        part = sb("part", [P, 2, 2, TPC, G])
        mx = sb("mx", [P, TPC, G])
        ms = sb("ms", [P, TPC, G, 3], bf16)
        none = sb("none", [P, TPC, G])
        mrow = sb("mrow", [G * 3, CH], bf16)
        osb = sb("osb", [P, CH])
        rsb = sb("rsb", [P, CH])
        on = sb("on", [P, CH])
        ps_s = pb("ps_s", [P, 2, PIECE])
        ps_w = pb("ps_w", [P, 2, CH])
        ps_o = pb("ps_o", [P, CH])
        ps_m = pb("ps_m", [P, CH])
        rows_set, none_set, mx_done = sem("rows_set"), sem("none_set"), sem("mx_done")
        loaded = [sem(f"loaded{i}") for i in range(2)]
        s_ready, s_read = sem("s_ready"), sem("s_read")
        w_ready, p_ready, pv_done = sem("w_ready"), sem("p_ready"), sem("pv_done")
        pool, m_turned, m_copied, m_in = sem("pool2"), sem("m_turned"), sem("m_copied"), sem("m_in")
        o_copied, spread, r_ready, on_ready, o_out = (
            sem("o_copied"), sem("spread"), sem("r_ready"), sem("on_ready"), sem("o_out"))
        NLOAD = 15
        MOPS = 5
        ROWS0 = sum(x[0] == "rows" for x in plan_before())
        psm_b = ps_m[0:G * 3, 0:CH // 2].bitcast(bf16)

        def load_count(n, u, di):
            return (n + (u + di) // 2) * 16 * NLOAD + 16 * NLOAD

        with nc.Block() as block:
            @block.sync
            def _(sp):
                def load(it, u):
                    src = g.qk_rows[bass.ds(it, 1)].rearrange("a w s (j d) t -> (a w) s d j t", d=HD)
                    for r in range(6):
                        rows = slice(r * HD, (r + 1) * HD)
                        sp.dma_start(kh[rows, u, :, :], src[1, K_PART[r]]).then_inc(loaded[u], 16)
                        sp.dma_start(qh[rows, u, :, :], src[0, Q_PART[r]]).then_inc(loaded[u], 16)
                    sp.dma_start(kh[R_POS:R_MAX, u, :, :],
                                 g.pos_rows[bass.ds(it, 1)].rearrange("a j s t -> s (a j) t")
                                 ).then_inc(loaded[u], 16)
                    for z in (slice(0, P // 2), slice(P // 2, P)):
                        sp.dma_start(vh[z, u, :, :],
                                     g.v_rows[bass.ds(it, 1)].rearrange("a (n p) c -> p (a n) c", p=P)[z]
                                     ).then_inc(loaded[u], 16)

                def rows(it, u, di, c):
                    sp.wait_ge(m_copied, (it + di) * CPB + c + 1)
                    for j in range(G):
                        sp.dma_start(qh[R_MAX:R_ALL, (u + di) % 2, j, c * CH:(c + 1) * CH],
                                     mrow[3 * j:3 * j + 3, :]).then_inc(m_in, 16)

                def body(n, u, todo, reload):
                    it = n * 2 + u
                    for kind, *a in todo:
                        if kind == "rows":
                            rows(it, u, *a)
                        elif kind == "norm":
                            sp.wait_ge(on_ready, it * CPB + a[0] + 2)
                            sp.dma_start(g.att_rows[bass.ds(it, 1), :, a[0] * CH:(a[0] + 1) * CH]
                                         .rearrange("a p t -> (a p) t"), on[:]).then_inc(o_out, 16)
                    if reload:
                        sp.wait_ge(pv_done, it * NS + NS + 2)
                        load(it + 2, u)

                sp.sem_inc(o_out, 1)
                sp.wait_ge(rows_set, 4)
                load(0, 0)
                load(1, 1)
                for kind, *a in plan_before():
                    if kind == "rows":
                        rows(0, 0, *a)
                with sp.Fori(0, NIT // 2 - 1) as n:
                    for u in range(2):
                        body(n, u, plan(True), True)
                body(NIT // 2 - 1, 0, plan(True), False)
                body(NIT // 2 - 1, 1, plan(False), False)
                sp.wait_ge(o_out, 16 * NIT * CPB + 1)

            @block.tensor
            def _(pe):
                def maxima(n, u, di, k):
                    c, j, t, i, k0, k1, last = PIECES[k]
                    par = (u + di) % 2
                    count = (n * 2 + u + di) * NP + k
                    if k == 0:
                        pe.wait_ge(loaded[par], load_count(n, u, di))
                    if not isinstance(count, int) or count >= 2:
                        pe.wait_ge(s_read, count - 1)
                    q0 = (c * TPC + t) * P
                    for a in range(k0, k1, CH):
                        z = min(a + CH, k1)
                        diag = last and z == k1
                        mm = nc.tensor.matmul(ps_s[:, k % 2, a - k0:z - k0], qh[0:R_MAX, par, j, q0:q0 + P],
                                              kh[0:R_MAX, par, j, a:z], start=True, stop=not diag)
                    if last:
                        mm = nc.tensor.matmul(ps_s[:, k % 2, k1 - P - k0:k1 - k0], g.ident_b[:], g.mask_q[:],
                                              start=False, stop=True)
                    mm.then_inc(s_ready, 1)

                def scores(it, u, s, j):
                    c, kb = STEPS[s]
                    col = step_cols(c, kb)
                    pe.wait_ge(p_ready, (it * NS + s) * G + j + 1)
                    diag = kb >= c * TPC
                    mm = nc.tensor.matmul(ps_w[:, j % 2, col:CH], kh[0:R_ALL, u, j, kb * P:(kb + 1) * P],
                                          qh[0:R_ALL, u, j, c * CH + col:(c + 1) * CH], start=True, stop=not diag)
                    if diag:
                        mm = nc.tensor.matmul(ps_w[:, j % 2, col:col + P], g.ident_b[:], g.mask_k[:],
                                              start=False, stop=True)
                    mm.then_inc(w_ready, 1)

                def rest_of_step(it, u, s):
                    scores(it, u, s, 2)
                    scores(it, u, s, 3)

                def values(it, u, s):
                    c, kb = STEPS[s]
                    col = step_cols(c, kb)
                    if kb == 0:
                        pe.wait_ge(o_copied, it * CPB + c + 1)
                    pe.wait_ge(p_ready, (it * NS + s) * G + G + 2)
                    for j in range(G):
                        mm = nc.tensor.matmul(ps_o[HW * j:HW * (j + 1), col:CH], vh[:, u, kb, HW * j:HW * (j + 1)],
                                              pr[:, s % 2, j, col:CH], start=(kb == 0),
                                              stop=(kb == TPC * (c + 1) - 1))
                    mm.then_inc(pv_done, 1)

                def turn_rows(q, norms):
                    pe.wait_ge(pool, (q + 1) * MOPS)
                    pe.wait_ge(m_copied, q)
                    pe.wait_ge(r_ready, norms)
                    for t in range(TPC):
                        mm = nc.tensor.transpose(psm_b[:, t * P:(t + 1) * P],
                                                 ms[:, t, :, :].rearrange("p j s -> p (j s)"), g.ident_b[:])
                    mm.then_inc(m_turned, 1)

                def spread_sums(q, rows):
                    pe.wait_ge(o_copied, q + 2)
                    pe.wait_ge(m_copied, rows)
                    nc.tensor.matmul(ps_m[:], g.const[:, C_SEL:C_SEL + P], osb[:], start=True, stop=True
                                     ).then_inc(spread, 1)

                def body(n, u, todo):
                    it = n * 2 + u
                    rows, norms, waiting = 0, 0, None
                    for kind, *a in todo:
                        if kind == "step":
                            s, = a
                            c, kb = STEPS[s]
                            if waiting is not None:
                                rest_of_step(it, u, waiting)
                            if kb == 0:
                                pe.wait_ge(m_in, (it * CPB + c + 1) * 16 * G)
                            scores(it, u, s, 0)
                            scores(it, u, s, 1)
                            if s:
                                values(it, u, s - 1)
                            waiting = s
                        elif kind == "max":
                            maxima(n, u, *a)
                            if waiting is not None:
                                rest_of_step(it, u, waiting)
                                waiting = None
                        elif kind == "rows":
                            turn_rows((it + a[0]) * CPB + a[1], it * CPB + norms + 1)
                            rows += 1
                        elif kind == "last":
                            if waiting is not None:
                                rest_of_step(it, u, waiting)
                            values(it, u, NS - 1)
                        elif kind == "norm":
                            spread_sums(it * CPB + a[0], it * CPB + ROWS0 + rows)
                            norms += 1

                for kind, *a in plan_before():
                    if kind == "max":
                        maxima(0, 0, *a)
                    else:
                        turn_rows(a[1], 1)
                with pe.Fori(0, NIT // 2 - 1) as n:
                    for u in range(2):
                        body(n, u, plan(True))
                body(NIT // 2 - 1, 0, plan(True))
                body(NIT // 2 - 1, 1, plan(False))

            @block.scalar
            def _(act):
                def copy_rows(q):
                    act.wait_ge(m_turned, q + 1)
                    act.wait_ge(m_in, q * 16 * G)
                    nc.scalar.copy(mrow[:], psm_b).then_inc(m_copied, 1)

                def body(n, u, todo):
                    it = n * 2 + u
                    for kind, *a in todo:
                        if kind == "step":
                            s, = a
                            col = step_cols(*STEPS[s])
                            act.wait_ge(pv_done, it * NS + s + 1)
                            for j in range(G):
                                act.wait_ge(w_ready, (it * NS + s) * G + j + 1)
                                nc.scalar.activation(pr[:, s % 2, j, col:CH], ps_w[:, j % 2, col:CH],
                                                     ACT.Exp).then_inc(p_ready, 1)
                        elif kind == "rows":
                            copy_rows((it + a[0]) * CPB + a[1])
                        elif kind == "take":
                            c, = a
                            act.wait_ge(pv_done, it * NS + STEPS.index((c, TPC * (c + 1) - 1)) + 3)
                            act.wait_ge(on_ready, it * CPB + c + 1)
                            nc.scalar.copy(osb[:], ps_o[:]).then_inc(o_copied, 1)

                act.sem_inc(p_ready, 2)
                act.sem_inc(o_copied, 1)
                for kind, *a in plan_before():
                    if kind == "rows":
                        copy_rows(a[1])
                with act.Fori(0, NIT // 2 - 1) as n:
                    for u in range(2):
                        body(n, u, plan(True))
                body(NIT // 2 - 1, 0, plan(True))
                body(NIT // 2 - 1, 1, plan(False))

            @block.vector
            def _(v):
                def reduce_piece(n, u, di, k):
                    c, j, t, i, k0, k1, last = PIECES[k]
                    it = n * 2 + u + di
                    v.wait_ge(s_ready, it * NP + k + 1)
                    nc.vector.tensor_reduce(part[:, c % 2, i, t, j:j + 1], ps_s[:, k % 2, 0:k1 - k0],
                                            AX.X, ALU.max).then_inc(s_read, 1)
                    if k in CHUNK_END:
                        q = it * CPB + c
                        v.wait_ge(s_read, it * NP + k + 1)
                        v.wait_ge(pool, q * MOPS)
                        nc.vector.tensor_reduce(mx[:], part[:, c % 2, 0:i + 1, :, :].rearrange("p i t j -> p t j i"),
                                                AX.X, ALU.max, negate=True).then_inc(mx_done, 1)

                def body(n, u, todo):
                    it = n * 2 + u
                    for kind, *a in todo:
                        if kind == "max":
                            reduce_piece(n, u, *a)
                        elif kind == "norm":
                            q = it * CPB + a[0]
                            v.wait_ge(spread, q + 1)
                            v.wait_ge(on_ready, q + 1)
                            nc.vector.reciprocal(rsb[:], ps_m[:]).then_inc(r_ready, 1)

                v.sem_inc(r_ready, 1)
                for kind, *a in plan_before():
                    if kind == "max":
                        reduce_piece(0, 0, *a)
                with v.Fori(0, NIT // 2 - 1) as n:
                    for u in range(2):
                        body(n, u, plan(True))
                body(NIT // 2 - 1, 0, plan(True))
                body(NIT // 2 - 1, 1, plan(False))

            @block.gpsimd
            def _(gp):
                def split_maxima(it, c):
                    q = it * CPB + c
                    done = [0]

                    def link(ins):
                        done[0] += 1
                        ins.then_inc(pool, 1)
                        gp.wait_ge(pool, q * MOPS + done[0])

                    gp.wait_ge(mx_done, q + 1)
                    gp.wait_ge(m_turned, q)
                    for i in range(3):
                        link(nc.gpsimd.tensor_tensor(ms[:, :, :, i], mx[:], none[:], ALU.add))
                        if i < 2:
                            link(nc.gpsimd.tensor_tensor(mx[:], mx[:], ms[:, :, :, i], ALU.subtract))

                def body(n, u, todo):
                    it = n * 2 + u
                    for kind, *a in todo:
                        if kind == "rows":
                            split_maxima(it + a[0], a[1])
                        elif kind == "norm":
                            q = it * CPB + a[0]
                            gp.wait_ge(r_ready, q + 2)
                            gp.wait_ge(o_out, q * 16 + 1)
                            nc.gpsimd.tensor_tensor(on[:], osb[:], rsb[:], ALU.mult).then_inc(on_ready, 1)

                gp.sem_inc(pv_done, 2)
                gp.sem_inc(on_ready, 1)
                nc.gpsimd.memset(none[:], 0.0).then_inc(none_set, 1)
                gp.wait_ge(none_set, 1)
                for u in range(2):
                    nc.gpsimd.memset(kh[R_POS:R_ALL, u, :, :], 1.0).then_inc(rows_set, 1)
                    nc.gpsimd.memset(qh[R_POS:R_ALL, u, :, :], 1.0).then_inc(rows_set, 1)
                for kind, *a in plan_before():
                    if kind == "rows":
                        split_maxima(0, a[1])
                with gp.Fori(0, NIT // 2 - 1) as n:
                    for u in range(2):
                        body(n, u, plan(True))
                body(NIT // 2 - 1, 0, plan(True))
                body(NIT // 2 - 1, 1, plan(False))


def stage_mix(nc, g):
    with ExitStack() as ctx:
        sb, pb, sem = open_stage(nc, ctx)
        wo = sb("wo", [P, NG, D])
        wg = sb("wg", [P, KC, E])
        bg = sb("bg", [P, E])
        at = sb("at", [P, 2, NG, CH])
        xt = sb("xt3", [P, 2, TPC, D])
        y1 = sb("y1", [P, TPC, D])
        x1 = sb("x1", [P, 2, TPC, D])
        st = sb("st3", [P, TPC, 6])
        mv = sb("mv3", [P, TPC, 2])
        ve, sd, rs = sb("ve3", [P, TPC]), sb("sd3", [P, TPC]), sb("rs3", [P, TPC])
        xn = sb("xn3", [P, TPC, D])
        tm = sb("tm3", [P, TPC, D])
        hT = sb("hT3", [P, 2, KC, P])
        ps_a = pb("ps_a", [P, 2, CH])
        ps_t = pb("ps_t3", [P, 2, CH])
        ps_l = pb("ps_l", [P, 2, CH])
        w_in = sem("w_in3")
        in3 = [sem(f"in3_{i}") for i in range(2)]
        a_done, y_ready, x1_ready, dve, xn_ready, pool, h_ready = (
            sem("a_done"), sem("y_ready"), sem("x1_ready"), sem("dve3"), sem("xn_ready"), sem("pool3"),
            sem("h_ready"))
        var_done, sd_done = sem("var_done3"), sem("sd_done3")
        turned, h_copied, l_done, l_read = sem("turned3"), sem("h_copied"), sem("l_done"), sem("l_read")
        x1_out = [sem(f"x1_out{i}") for i in range(2)]
        x_v = g.x.rearrange("b (n t p) d -> (b n) p t d", p=P, t=TPC)
        x1_v = g.x1_rows.rearrange("(n t p) d -> n p t d", p=P, t=TPC)

        with nc.Block() as block:
            @block.sync
            def _(sp):
                def load(n):
                    b, c = n // CPB, n % CPB
                    sp.dma_start(at[:, n % 2, :, :],
                                 g.att_rows[b * NG:(b + 1) * NG, :, c * CH:(c + 1) * CH].rearrange("g p t -> p g t")
                                 ).then_inc(in3[n % 2], 16)
                    sp.dma_start(xt[:, n % 2, :, :], x_v[n]).then_inc(in3[n % 2], 16)

                sp.dma_start(wo[:], g.woT.rearrange("g p n -> p g n")).then_inc(w_in, 16)
                sp.dma_start(wg[:], g.wg.rearrange("(k p) e -> p k e", p=P)).then_inc(w_in, 16)
                sp.dma_start(bg[:], g.bg.unsqueeze(0).to_broadcast([P, E])).then_inc(w_in, 16)
                load(0)
                load(1)
                for n in range(NCH):
                    sp.wait_ge(x1_ready, TPC * (n + 1))
                    sp.dma_start(x1_v[n], x1[:, n % 2, :, :]).then_inc(x1_out[n % 2], 16)
                    if n + 2 < NCH:
                        load(n + 2)
                for i in range(2):
                    sp.wait_ge(x1_out[i], 16 * NCH // 2)

            @block.tensor
            def _(pe):
                def mix(n):
                    pe.wait_ge(in3[n % 2], 32 * (n // 2 + 1))
                    for t in range(TPC):
                        u = n * TPC + t
                        if u >= 2:
                            pe.wait_ge(y_ready, u - 1)
                        for k in range(NG):
                            mm = nc.tensor.matmul(ps_a[:, u % 2, 0:D], at[:, n % 2, k, t * P:(t + 1) * P], wo[:, k, :],
                                                  start=(k == 0), stop=(k == NG - 1))
                        mm.then_inc(a_done, 1)

                pe.wait_ge(w_in, 48)
                mix(0)
                for n in range(NCH):
                    if n + 1 < NCH:
                        mix(n + 1)
                    for t in range(TPC + 1):
                        u = n * TPC + t
                        if t < TPC:
                            pe.wait_ge(h_ready, u + 1)
                            if u >= 2:
                                pe.wait_ge(h_copied, u - 1)
                            for k in range(KC):
                                mm = nc.tensor.transpose(ps_t[:, u % 2, k * P:(k + 1) * P],
                                                         g.h2[:, u, k * P:(k + 1) * P], g.const[:, C_ID:C_ID + P])
                            mm.then_inc(turned, 1)
                        if t:
                            u -= 1
                            pe.wait_ge(h_copied, u + 1)
                            if t == 1 and n >= 2:
                                pe.wait_ge(l_read, n - 1)
                            for k in range(KC):
                                mm = nc.tensor.matmul(ps_l[:, n % 2, (t - 1) * E:t * E], hT[:, u % 2, k, :], wg[:, k, :],
                                                      start=(k == 0), stop=(k == KC - 1))
                            mm.then_inc(l_done, 1)

            @block.scalar
            def _(act):
                for u in range(NT):
                    if u % TPC == 0:
                        act.wait_ge(var_done, u // TPC + 1)
                        nc.scalar.activation(sd[:], ve[:], ACT.Sqrt).then_inc(sd_done, 1)
                    act.wait_ge(turned, u + 1)
                    if u >= 2:
                        act.wait_ge(l_done, u - 1)
                    nc.scalar.copy(hT[:, u % 2, :, :], ps_t[:, u % 2, 0:D].rearrange("p (k t) -> p k t", k=KC)
                                   ).then_inc(h_copied, 1)

            @block.vector
            def _(v):
                def link(ins):
                    link.n += 1
                    ins.then_inc(dve, 1)
                    v.wait_ge(dve, link.n)
                link.n = 0

                def gated(n):
                    for t in range(TPC):
                        v.wait_ge(a_done, n * TPC + t + 1)
                        if n:
                            v.wait_ge(x1_ready, (n - 1) * TPC + t + 1)
                        nc.vector.tensor_tensor(y1[:, t, :], ps_a[:, (n * TPC + t) % 2, 0:D],
                                                g.mod[:, n // CPB, 0, :], ALU.mult).then_inc(y_ready, 1)

                v.wait_ge(w_in, 48)
                gated(0)
                for n in range(NCH):
                    v.wait_ge(x1_ready, TPC * (n + 1))
                    for t in range(TPC):
                        last = nc.vector.bn_stats(st[:, t, :], x1[:, n % 2, t, :])
                    link(last)
                    for t in range(TPC):
                        last = nc.vector.bn_aggr(mv[:, t, :], st[:, t, :])
                    link(last)
                    nc.vector.tensor_scalar(ve[:], mv[:, :, 1], EPS, None, ALU.add).then_inc(var_done, 1)
                    v.wait_ge(sd_done, n + 1)
                    link(nc.vector.reciprocal(rs[:], sd[:]))
                    if n:
                        v.wait_ge(h_ready, TPC * n)
                    for t in range(TPC):
                        last = nc.vector.tensor_scalar(xn[:, t, :], x1[:, n % 2, t, :], mv[:, t, 0:1],
                                                       rs[:, t:t + 1], ALU.subtract, ALU.mult)
                    last.then_inc(xn_ready, 1)
                    v.wait_ge(xn_ready, n + 1)
                    if n + 1 < NCH:
                        gated(n + 1)
                    v.wait_ge(l_done, TPC * (n + 1))
                    nc.vector.tensor_tensor(g.logits[:, n * TPC:(n + 1) * TPC, :],
                                            ps_l[:, n % 2, 0:TPC * E].rearrange("p (t e) -> p t e", e=E),
                                            bg[:].unsqueeze(1).to_broadcast([P, TPC, E]), ALU.add).then_inc(l_read, 1)

            @block.gpsimd
            def _(gp):
                def residual(n):
                    gp.wait_ge(in3[n % 2], 32 * (n // 2 + 1))
                    if n >= 2:
                        gp.wait_ge(x1_out[n % 2], 16 * (n // 2))
                        gp.wait_ge(xn_ready, n - 1)
                    for t in range(TPC):
                        gp.wait_ge(y_ready, n * TPC + t + 1)
                        nc.gpsimd.tensor_tensor(x1[:, n % 2, t, :], y1[:, t, :], xt[:, n % 2, t, :], ALU.add
                                                ).then_inc(x1_ready, 1)

                residual(0)
                for n in range(NCH):
                    if n + 1 < NCH:
                        residual(n + 1)
                    gp.wait_ge(xn_ready, n + 1)
                    for t in range(TPC):
                        u = n * TPC + t
                        if n:
                            gp.wait_ge(h_ready, u - TPC + 1)
                        nc.gpsimd.tensor_tensor(tm[:, t, :], xn[:, t, :], g.mod[:, n // CPB, 2, :], ALU.mult
                                                ).then_inc(pool, 1)
                        gp.wait_ge(pool, u + 1)
                        nc.gpsimd.tensor_tensor(g.h2[:, u, :], tm[:, t, :], g.mod[:, n // CPB, 1, :], ALU.add
                                                ).then_inc(h_ready, 1)


def stage_route(nc, g):
    with ExitStack() as ctx:
        sb, pb, sem = open_stage(nc, ctx)
        top = sb("top", [P, NT])
        key = sb("key", [P, NT, E])
        hot = sb("hot", [P, NT, E])
        ones = sb("ones4", [P, P])
        run = sb("run", [P, 2, NT, E])
        tot = sb("tot", [P, NT, E])
        over = sb("over", [P, E, NT])
        tiles = sb("tiles", [P, E])
        cum = sb("cum", [P, 2, E])
        base = sb("base", [P, E])
        slot = sb("slot", [P, NT, E])
        slot_f = sb("slot_f", [P, NT])
        of_tile = sb("of_tile", [P, SLOTS + 1, E])
        exp_f = sb("exp_f", [P, SLOTS + 1])
        ps_p = pb("ps_p", [P, NT, E])
        ps_n = pb("ps_n", [P, NT, E])
        dve, hot_done, sums, slots_done, scattered = (
            sem("dve4"), sem("hot_done"), sem("sums4"), sem("slots_done"), sem("scattered"))
        rank = g.const[:, C_RANK:C_RANK + E]
        with nc.Block() as block:
            @block.vector
            def _(v):
                def link(ins):
                    link.n += 1
                    ins.then_inc(dve, 1)
                    v.wait_ge(dve, link.n)
                link.n = 0
                rank_b = rank.unsqueeze(1).to_broadcast([P, NT, E])
                nc.vector.memset(ones[:], 1.0)
                link(nc.vector.tensor_reduce(top[:], g.logits[:], AX.X, ALU.max))
                link(nc.vector.tensor_tensor(hot[:], g.logits[:], top[:].unsqueeze(2).to_broadcast([P, NT, E]),
                                             ALU.is_equal))
                link(nc.vector.tensor_tensor(key[:], hot[:], rank_b, ALU.mult))
                link(nc.vector.tensor_reduce(top[:], key[:], AX.X, ALU.max))
                nc.vector.tensor_tensor(hot[:], rank_b, top[:].unsqueeze(2).to_broadcast([P, NT, E]),
                                        ALU.is_equal).then_inc(hot_done, 1)
                v.wait_ge(sums, 1)
                nc.vector.tensor_copy(run[:, 0, :, :], ps_n[:])
                link(nc.vector.tensor_copy(tot[:], ps_n[:]))
                i, d = 0, 1
                while d < NT:
                    nc.vector.tensor_copy(run[:, 1 - i, 0:d, :], run[:, i, 0:d, :])
                    link(nc.vector.tensor_tensor(run[:, 1 - i, d:NT, :], run[:, i, d:NT, :], run[:, i, 0:NT - d, :],
                                                 ALU.add))
                    i, d = 1 - i, 2 * d
                link(nc.vector.tensor_tensor(over[:], run[:, i, NT - 1, :].unsqueeze(2).to_broadcast([P, E, NT]),
                                             g.const[:, C_THR:C_THR + NT].unsqueeze(1).to_broadcast([P, E, NT]),
                                             ALU.is_gt))
                link(nc.vector.tensor_reduce(tiles[:], over[:], AX.X, ALU.add))
                link(nc.vector.tensor_copy(cum[:, 0, :], tiles[:]))
                j, d = 0, 1
                while d < E:
                    nc.vector.tensor_copy(cum[:, 1 - j, 0:d], cum[:, j, 0:d])
                    link(nc.vector.tensor_tensor(cum[:, 1 - j, d:E], cum[:, j, d:E], cum[:, j, 0:E - d], ALU.add))
                    j, d = 1 - j, 2 * d
                link(nc.vector.tensor_tensor(base[:], cum[:, j, :], tiles[:], ALU.subtract))
                link(nc.vector.tensor_scalar(base[:], base[:], float(P), None, ALU.mult))
                link(nc.vector.tensor_tensor(slot[:], run[:, i, :, :], tot[:], ALU.subtract))
                link(nc.vector.tensor_tensor(slot[:], ps_p[:], slot[:], ALU.add))
                link(nc.vector.tensor_tensor(slot[:], slot[:], base[:].unsqueeze(1).to_broadcast([P, NT, E]), ALU.add))
                link(nc.vector.tensor_tensor(slot[:], slot[:], hot[:], ALU.mult))
                link(nc.vector.tensor_reduce(slot_f[:], slot[:], AX.X, ALU.add))
                nc.vector.tensor_copy(g.slots[:], slot_f[:]).then_inc(slots_done, 1)
                link(nc.vector.tensor_tensor(of_tile[:], cum[:, j, :].unsqueeze(1).to_broadcast([P, SLOTS + 1, E]),
                                             g.const[:, C_TILE:C_END].unsqueeze(2).to_broadcast([P, SLOTS + 1, E]),
                                             ALU.is_le))
                link(nc.vector.tensor_reduce(exp_f[:], of_tile[:], AX.X, ALU.add))
                link(nc.vector.tensor_scalar(g.expert[:], exp_f[:], float(E - 1), None, ALU.min))

            @block.tensor
            def _(pe):
                pe.wait_ge(hot_done, 1)
                nc.tensor.matmul(ps_p[:].rearrange("p t e -> p (t e)"), g.const[:, C_TRI:C_TRI + P],
                                 hot[:].rearrange("p t e -> p (t e)"), start=True, stop=True)
                nc.tensor.matmul(ps_n[:].rearrange("p t e -> p (t e)"), ones[:],
                                 hot[:].rearrange("p t e -> p (t e)"), start=True, stop=True).then_inc(sums, 1)

            @block.gpsimd
            def _(gp):
                gp.wait_ge(slots_done, 1)
                for t in range(NT):
                    nc.gpsimd.indirect_dma_start(
                        out=g.sorted_h, out_offset=bass.IndirectOffsetOnAxis(ap=g.slots[:, t:t + 1], axis=0),
                        in_=g.h2[:, t, :], in_offset=None).then_inc(scattered, 16)
                gp.wait_ge(scattered, 16 * NT)


def stage_experts(nc, g):
    with ExitStack() as ctx:
        sb, pb, sem = open_stage(nc, ctx)
        w2 = sb("w2", [P, FC, E, D])
        b1s = sb("b1s", [3, E, F], bf16)
        b2s = sb("b2s", [3, E, D], bf16)
        one3 = sb("one3", [3, P], bf16)
        ht = sb("ht", [P, 2, D])
        hT = sb("hT5", [P, 2, KC, P])
        ge = sb("ge", [P, 2, F])
        gT = sb("gT", [P, FC, P])
        ys = sb("ys", [P, 2, D])
        ps_x = pb("ps_x", [P, CH])
        ps_1 = pb("ps_1", [P, 2, CH])
        ps_g = pb("ps_g", [P, 2, CH])
        ps_y = pb("ps_y", [P, CH])
        w_in, set5 = sem("w_in5"), sem("set5")
        h_in = [sem(f"h_in{i}") for i in range(2)]
        x_turned, x_copied, f_done, g_done, g_turned, g_copied, y_done, y_copied = (
            sem("x_turned"), sem("x_copied"), sem("f_done"), sem("g_done"), sem("g_turned"), sem("g_copied"),
            sem("y_done"), sem("y_copied"))
        y_out = [sem(f"y_out{i}") for i in range(2)]

        def pairs(eng, body):
            with eng.Fori(0, SLOTS // 2) as n:
                for u in range(2):
                    body(n, u)
            if SLOTS % 2:
                body(SLOTS // 2, 0)

        with nc.Block() as block:
            @block.sync
            def _(sp):
                sp.dma_start(b1s[:], g.b1_rows.rearrange("s (e n) -> s e n", e=E)).then_inc(w_in, 16)
                sp.dma_start(b2s[:], g.b2_rows.rearrange("s (e n) -> s e n", e=E)).then_inc(w_in, 16)
                for k in range(FC):
                    sp.dma_start(w2[:, k, :, :], g.w2.rearrange("e (k p) n -> k p e n", p=P)[k]).then_inc(w_in, 16)

                def body(n, u):
                    i = n * 2 + u
                    sp.wait_ge(x_turned, i + 1)
                    sp.dma_start(ht[:, u, :],
                                 g.sorted_h[bass.ds((i + 2) * P, P), :]).then_inc(h_in[u], 16)
                    sp.wait_ge(y_copied, i + 2)
                    sp.dma_start(g.sorted_y[bass.ds(i * P, P), :], ys[:, u, :]).then_inc(y_out[u], 16)

                for i in range(2):
                    sp.sem_inc(y_out[i], 1)
                    sp.dma_start(ht[:, i, :], g.sorted_h[i * P:(i + 1) * P, :]).then_inc(h_in[i], 16)
                pairs(sp, body)
                sp.wait_ge(y_out[0], 16 * (SLOTS // 2 + SLOTS % 2) + 1)
                sp.wait_ge(y_out[1], 16 * (SLOTS // 2) + 1)
                sp.wait_ge(h_in[0], 16 * (1 + SLOTS // 2 + SLOTS % 2))
                sp.wait_ge(h_in[1], 16 * (1 + SLOTS // 2))

            @block.gpsimd
            def _(gp):
                nc.gpsimd.memset(one3[:], 1.0).then_inc(set5, 1)

            @block.tensor
            def _(pe):
                def turn_in(n, u):
                    i = n * 2 + u
                    pe.wait_ge(h_in[u], 16 * n + 16)
                    pe.wait_ge(x_copied, i + 1)
                    for k in range(KC):
                        mm = nc.tensor.transpose(ps_x[:, k * P:(k + 1) * P], ht[:, u, k * P:(k + 1) * P],
                                                 g.const[:, C_ID:C_ID + P])
                    mm.then_inc(x_turned, 1)

                def up(n, u, half, e):
                    i = n * 2 + u
                    pe.wait_ge(x_copied, i + 2)
                    pe.wait_ge(g_done, i * 2 + 1)
                    cols = slice(half * CH, (half + 1) * CH)
                    nc.tensor.matmul(ps_1[:, half, :], one3[:], b1s[:, bass.ds(e, 1), cols]
                                     .rearrange("s a n -> s (a n)"), start=True, stop=False)
                    for k in range(KC):
                        mm = nc.tensor.matmul(ps_1[:, half, :], hT[:, u, k, :],
                                              g.w1[:, k, bass.ds(e, 1), cols].rearrange("p a n -> p (a n)"),
                                              start=False, stop=(k == KC - 1))
                    mm.then_inc(f_done, 1)

                def turn_hidden(n, u):
                    i = n * 2 + u
                    for half in range(2):
                        pe.wait_ge(g_done, i * 2 + half + 2)
                        pe.wait_ge(g_copied, i * 2 + 1)
                        for k in range(FC // 2):
                            f = half * FC // 2 + k
                            mm = nc.tensor.transpose(ps_g[:, half, k * P:(k + 1) * P], ge[:, u, f * P:(f + 1) * P],
                                                     g.const[:, C_ID:C_ID + P])
                        mm.then_inc(g_turned, 1)

                def down(n, u, e):
                    i = n * 2 + u
                    pe.wait_ge(y_copied, i + 1)
                    nc.tensor.matmul(ps_y[:, 0:D], one3[:], b2s[:, bass.ds(e, 1), :].rearrange("s a n -> s (a n)"),
                                     start=True, stop=False)
                    for f in range(FC):
                        if f % (FC // 2) == 0:
                            pe.wait_ge(g_copied, i * 2 + f // (FC // 2) + 2)
                        mm = nc.tensor.matmul(ps_y[:, 0:D], gT[:, f, :],
                                              w2[:, f, bass.ds(e, 1), :].rearrange("p a n -> p (a n)"),
                                              start=False, stop=(f == FC - 1))
                    mm.then_inc(y_done, 1)

                def body(n, u):
                    i = n * 2 + u
                    e = pe.value_load(g.expert[0:1, bass.ds(i, 1)], min_val=0, max_val=E - 1)
                    turn_in(n, u)
                    up(n, u, 0, e)
                    up(n, u, 1, e)
                    turn_hidden(n, u)
                    down(n, u, e)

                pe.sem_inc(y_done, 1)
                pe.wait_ge(set5, 1)
                pe.wait_ge(w_in, 16 * (2 + FC))
                pairs(pe, body)

            @block.scalar
            def _(act):
                def body(n, u):
                    i = n * 2 + u
                    for half in range(2):
                        act.wait_ge(f_done, i * 2 + half + 1)
                        nc.scalar.activation(ge[:, u, half * CH:(half + 1) * CH], ps_1[:, half, :], ACT.Gelu
                                             ).then_inc(g_done, 1)
                    act.wait_ge(y_done, i + 2)
                    act.wait_ge(y_out[u], 16 * n + 1)
                    nc.scalar.copy(ys[:, u, :], ps_y[:, 0:D]).then_inc(y_copied, 1)
                act.sem_inc(g_done, 1)
                act.sem_inc(y_copied, 1)
                pairs(act, body)

            @block.vector
            def _(v):
                def body(n, u):
                    i = n * 2 + u
                    v.wait_ge(x_turned, i + 1)
                    nc.vector.tensor_copy(hT[:, u, :, :], ps_x[:, 0:D].rearrange("p (k t) -> p k t", k=KC)
                                          ).then_inc(x_copied, 1)
                    for half in range(2):
                        v.wait_ge(g_turned, i * 2 + half + 1)
                        v.wait_ge(y_done, i + 1)
                        nc.vector.tensor_copy(gT[:, half * FC // 2:(half + 1) * FC // 2, :],
                                              ps_g[:, half, :].rearrange("p (k t) -> p k t", t=P)
                                              ).then_inc(g_copied, 1)
                v.sem_inc(x_copied, 1)
                v.sem_inc(g_copied, 1)
                pairs(v, body)


def stage_finish(nc, g):
    with ExitStack() as ctx:
        sb, pb, sem = open_stage(nc, ctx)
        RING = 4
        x1 = sb("x6", [P, RING, D])
        y = sb("y6", [P, RING, D])
        yg = sb("yg", [P, RING, D])
        o = sb("o6", [P, RING, D])
        x_in = [sem(f"x_in6{i}") for i in range(RING)]
        y_in = [sem(f"y_in6{i}") for i in range(RING)]
        gated, summed = sem("gated6"), sem("summed6")
        o_out = [sem(f"o_out6{i}") for i in range(RING)]
        with nc.Block() as block:
            @block.sync
            def _(sp):
                for t in range(RING):
                    sp.dma_start(x1[:, t, :], g.x1_rows[t * P:(t + 1) * P, :]).then_inc(x_in[t], 16)
                for t in range(NT):
                    r = t % RING
                    sp.wait_ge(summed, t + 1)
                    sp.dma_start(g.out.rearrange("b s d -> (b s) d")[t * P:(t + 1) * P, :], o[:, r, :]
                                 ).then_inc(o_out[r], 16)
                    if t + RING < NT:
                        sp.dma_start(x1[:, r, :], g.x1_rows[(t + RING) * P:(t + RING + 1) * P, :]).then_inc(x_in[r], 16)
                for r in range(RING):
                    sp.wait_ge(o_out[r], 16 * NT // RING)

            @block.gpsimd
            def _(gp):
                for t in range(NT):
                    r = t % RING
                    if t >= RING:
                        gp.wait_ge(gated, t - RING + 1)
                    nc.gpsimd.indirect_dma_start(
                        out=y[:, r, :], out_offset=None, in_=g.sorted_y,
                        in_offset=bass.IndirectOffsetOnAxis(ap=g.slots[:, t:t + 1], axis=0)).then_inc(y_in[r], 16)

            @block.vector
            def _(v):
                for t in range(NT):
                    r = t % RING
                    v.wait_ge(y_in[r], 16 * (t // RING + 1))
                    nc.vector.tensor_tensor(yg[:, r, :], y[:, r, :], g.mod[:, t // (NT // B), 3, :], ALU.mult
                                            ).then_inc(gated, 1)
                    v.wait_ge(gated, t + 1)
                    v.wait_ge(x_in[r], 16 * (t // RING + 1))
                    if t >= RING:
                        v.wait_ge(o_out[r], 16 * (t // RING))
                    nc.vector.tensor_tensor(o[:, r, :], yg[:, r, :], x1[:, r, :], ALU.add).then_inc(summed, 1)


def build(nc, g, stages=(0, 1, 2, 3, 4, 5, 6)):
    def dram(name, shape, dt):
        return nc.dram_tensor(name, shape, dt, kind="Internal").ap()

    g.qk_rows = dram("qk_rows", (NIT, 2, 3, G * HD, S), bf16)
    g.v_rows = dram("v_rows", (NIT, S, P), fp32)
    g.pos_rows = dram("pos_rows", (NIT, G, 3, S), bf16)
    g.att_rows = dram("att_rows", (NIT, P, S), fp32)
    g.b1_rows = dram("b1_rows", (3, E * F), bf16)
    g.b2_rows = dram("b2_rows", (3, E * D), bf16)
    g.x1_rows = dram("x1_rows", (NTOK, D), fp32)
    g.sorted_h = dram("sorted_h", ((SLOTS + 2) * P, D), fp32)
    g.sorted_y = dram("sorted_y", (SLOTS * P, D), fp32)
    with ExitStack() as ctx:
        sb, pb, sem = open_stage(nc, ctx)
        g.const = sb("const", [P, C_END])
        g.ident_b = sb("ident_b", [P, P], bf16)
        g.mask_q = sb("mask_q", [P, P], bf16)
        g.mask_k = sb("mask_k", [P, P], bf16)
        g.shift = sb("shift", [P, KC, B])
        g.gain = sb("gain", [P, KC, B])
        g.mod = sb("mod", [P, B, 4, D])
        g.logits = sb("logits", [P, NT, E])
        g.slots = sb("slots", [P, NT], i32)
        g.expert = sb("expert", [P, SLOTS + 1], i32)
        with ExitStack() as early:
            g.wqkv = early.enter_context(nc.sbuf_tensor("wqkv", [P, KC, 3 * D], fp32))
            if 0 in stages: stage_setup(nc, g)
            if 1 in stages: stage_qkv(nc, g)
        g.w1 = sb("w1", [P, KC, E, F])
        w1_in = sem("w1_in")
        with nc.Block() as block:
            @block.sync
            def _(sp):
                for k in range(KC):
                    sp.dma_start(g.w1[:, k, :, :], g.w1_dram.rearrange("e (k p) n -> k p e n", p=P)[k]
                                 ).then_inc(w1_in, 16)
                sp.wait_ge(w1_in, 16 * KC)
        if 2 in stages: stage_attention(nc, g)
        with ExitStack() as mid:
            g.h2 = mid.enter_context(nc.sbuf_tensor("h2", [P, NT, D], fp32))
            if 3 in stages: stage_mix(nc, g)
            if 4 in stages: stage_route(nc, g)
        if 5 in stages: stage_experts(nc, g)
        if 6 in stages: stage_finish(nc, g)


def constants():
    c = np.zeros((P, C_END), np.float32)
    i, j = np.arange(P)[:, None], np.arange(P)[None, :]
    c[:, C_ID:C_ID + P] = i == j
    c[:, C_MQ:C_MQ + P] = np.where(j > i, -1e30, 0.0)
    c[:, C_MK:C_MK + P] = np.where(j < i, -1e30, 0.0)
    c[:, C_TRI:C_TRI + P] = i < j
    c[:, C_SEL:C_SEL + P] = i == HW * (j // HW) + HD
    c[:, C_RANK:C_RANK + E] = E - np.arange(E)
    c[:, C_THR:C_THR + NT] = P * np.arange(NT)
    c[:, C_TILE:C_END] = np.arange(SLOTS + 1)
    start = 2.0 ** (-2.0 ** -(np.log2(H) - 3))
    slopes = np.array([start * start ** i for i in range(H)], np.float32)
    alibi = -slopes[:, None] * np.arange(S, dtype=np.float32)[None, :]
    return c, alibi.astype(np.float32)


def laid_out(inputs):
    a = {k: np.ascontiguousarray(np.asarray(v)) for k, v in inputs.items()}
    wo = np.zeros((NG, G, HW, D), np.float32)
    wo[:, :, :HD, :] = a["L0_attn_W_o"].T.reshape(NG, G, HD, D)
    const, alibi = constants()
    return {
        "x": a["L0_attn_x"],
        "wqkvT": np.ascontiguousarray(a["L0_attn_W_qkv"].T),
        "woT": wo.reshape(NG, P, D),
        "wg": a["L0_ffn_Wg"], "bg": a["L0_ffn_bg"],
        "w1_dram": a["L0_ffn_W1"], "b1": a["L0_ffn_b1"], "w2": a["L0_ffn_W2"], "b2": a["L0_ffn_b2"],
        "cT": np.ascontiguousarray(a["L0_c"].T.reshape(KC, P, B).transpose(1, 0, 2)),
        "wmod": a["L0_wmod"],
        "const_dram": const, "alibi": alibi,
    }


def kernel(**inputs):
    import concourse.bacc as _bacc
    from concourse.bass_utils import run_bass_kernel_spmd as _run

    nc = _bacc.Bacc("TRN2", target_bir_lowering=False, num_devices=1)
    g, arrays = Tensors(), {}
    for name, a in laid_out(inputs).items():
        arrays["in_" + name] = a
        g.__dict__[name] = nc.dram_tensor("in_" + name, a.shape, mybir.dt.from_np(a.dtype), kind="ExternalInput").ap()
    g.out = nc.dram_tensor("out_0", (B, S, D), fp32, kind="ExternalOutput").ap()
    build(nc, g)
    r = _run(nc, [arrays], core_ids=[0])
    return r.results[0]["out_0"]
```

```python
import concourse.bass as bass
from concourse import mybir
from contextlib import ExitStack
import numpy as np

fp32 = mybir.dt.float32
bf16 = mybir.dt.bfloat16
i32 = mybir.dt.int32
ALU = mybir.AluOpType
ACT = mybir.ActivationFunctionType
AX = mybir.AxisListType

P = 128
B, S, D, H = 2, 2048, 256, 16
HD = D // H
KC = D // P
NTOK = B * S
CH = 512
TPC = CH // P
NCH = NTOK // CH
CPB = S // CH
NT = NTOK // P
G = 4
NG = H // G
HW = 32
NIT = B * NG
E, F = 8, 1024
FC = F // P
SLOTS = NT + E - 1
EPS = 1e-5
SCALE = HD ** -0.5
Q_PART = [0, 0, 1, 0, 1, 2]
K_PART = [0, 1, 0, 2, 1, 0]
R_POS = 6 * HD
R_MAX = R_POS + 3
R_ALL = R_MAX + 3
PIECE = 1024
LAG = 0.55
SLACK = 0.02
ROWS_AFTER, NORM_AFTER = 6, 6
CUT = 4

C_ID, C_MQ, C_MK, C_TRI, C_SMALL = 0, P, 2 * P, 3 * P, 4 * P
C_RANK, C_THR, C_TILE, C_END = C_SMALL, C_SMALL + E, C_SMALL + E + NT, C_SMALL + E + NT + SLOTS + 1


class Tensors:
    pass


def max_pieces():
    out = []
    for c in range(CPB):
        for t in range(TPC):
            n = (c * TPC + t + 1) * P
            whole, rest = divmod(n, PIECE)
            for i in range(whole):
                out += [(c, t, j, 1, i, i * PIECE, (i + 1) * PIECE, not rest and i == whole - 1) for j in range(G)]
            if rest:
                h = min(G, max(1, PIECE // seat(rest)))
                out += [(c, t, j, h, whole, whole * PIECE, n, True) for j in range(0, G, h)]
    return out


def seat(n):
    return n if n <= CH // 2 or n > CH else CH


def products(k):
    c, t, j0, nh, i, k0, k1, last = PIECES[k]
    return [(j, (j - j0) * seat(k1 - k0) - k0, a, min(a + CH, k1), last and min(a + CH, k1) == k1)
            for j in range(j0, j0 + nh) for a in range(k0, k1, CH)]


PIECES = max_pieces()
NP = len(PIECES)
STEPS = [(c, kb) for c in range(CPB) for kb in range(TPC * (c + 1))]
NS = len(STEPS)
CHUNK_END = [max(k for k, p in enumerate(PIECES) if p[0] == c) for c in range(CPB)]


def step_cols(c, kb):
    return max(0, kb - c * TPC) * P


def step_units(s):
    n = CH - step_cols(*STEPS[s])
    h = CH // n if n <= CH // 2 else 1
    return [range(j, j + h) for j in range(0, G, h)]


UNITS = [sum(len(step_units(s)) for s in range(n)) for n in range(NS + 1)]


def before_lag():
    cols = np.cumsum([p[3] * (p[6] - p[5]) for p in PIECES])
    return int(np.searchsorted(cols, LAG * cols[-1]))


def round_order():
    hop = 190
    first = before_lag()
    ones = [(k // NP, k % NP, i) for k in range(first, first + NP) for i in range(len(products(k % NP)))]
    cost1 = [(z - a + P * d) / 2.4 for _, k, i in ones for _, _, a, z, d in [products(k)[i]]]
    width = [CH - step_cols(*x) for x in STEPS]
    units = [(s, i) for s in range(NS) for i in range(len(step_units(s)))]
    unit_cost = [len(step_units(s)[i]) * (width[s] + P * (width[s] < CH or STEPS[s][1] % TPC == 0 and
                 STEPS[s][1] == STEPS[s][0] * TPC)) / 2.4 for s, i in units]
    exp_cost = [51 + len(step_units(s)[i]) * width[s] / 1.2 for s, i in units]
    value_cost = [width[v - 1] * 4 / 2.4 + 60 for v in range(NS)]
    all1, all2 = sum(cost1), sum(unit_cost) + sum(value_cost)
    pe = act = dve = 0.0
    exps, reads, sums = [0.0, 0.0], [0.0, 0.0], [0.0, 0.0]
    step_end = [0.0] * (NS + 1)
    for _ in range(2):
        out, i1, i2, v, done1, done2 = [], 0, 0, 0, 0.0, 0.0
        step_end[0] = step_end[NS]
        while i1 < len(ones) or i2 < len(units) or v < NS:
            ahead = done1 / all1 - done2 / all2
            choices = []
            if i2 < len(units) and units[i2][0] <= v:
                choices.append((max(pe, exps[-2]), 0, "unit"))
            if v < NS and (i2 == len(units) or units[i2] > (v, 0)):
                choices.append((max(pe, step_end[v]), 2, "values"))
            if i1 < len(ones) and (ahead < SLACK or not choices):
                choices.append((max(pe, reads[-2]) if ones[i1][2] == 0 else pe, 1 if ahead < 0 else 3, "max"))
                if ahead < -SLACK:
                    choices = choices[-1:]
            start, _, what = min(choices)
            if what == "unit":
                s, i = units[i2]
                pe = start + unit_cost[i2]
                act = max(act, pe + hop, sums[-2] + hop) + exp_cost[i2]
                exps.append(act + hop)
                step_end[s + 1] = act + hop
                done2 += unit_cost[i2]
                i2 += 1
                out.append(("unit", 0, s, i))
            elif what == "values":
                pe = start + value_cost[v]
                sums.append(pe)
                done2 += value_cost[v]
                out.append(("values", 0 if v else -1, (v - 1) % NS))
                v += 1
            else:
                r, k, i = ones[i1]
                pe = start + cost1[i1]
                done1 += cost1[i1]
                i1 += 1
                if i == len(products(k)) - 1:
                    dve = max(dve, pe + hop) + 65 + PIECES[k][3] * (PIECES[k][6] - PIECES[k][5]) / 0.96
                    reads.append(dve + hop)
                    out.append(("max", r, k))
                else:
                    out.append(("part", r, k, i))
    return out


def whole_plan():
    core = [("part" if i < len(products(k)) - 1 else "max", 0, k, i)[:4 if i < len(products(k)) - 1 else 3]
            for k in range(before_lag()) for i in range(len(products(k)))]
    order = round_order()
    for r in range(NIT):
        core += [(x[0], x[1] + r, *x[2:]) for x in order if 0 <= x[1] + r < NIT]
    core.append(("values", NIT - 1, NS - 1))
    out, late, units, maxima = [], [], 0, 0
    for x in core:
        out.append(x)
        kind, r, a = x[:3]
        units += kind == "unit"
        maxima += kind == "max"
        if kind == "max" and a in CHUNK_END:
            late.append((units + ROWS_AFTER, maxima + 2, ("rows", r, CHUNK_END.index(a))))
        if kind == "values":
            c, kb = STEPS[a]
            if kb == TPC * (c + 1) - 1:
                late.append((units + 1, 0, ("take", r, c)))
                late.append((units + NORM_AFTER, 0, ("norm", r, c)))
            if a == NS - 1 and r + 2 < NIT:
                out.append(("load", r + 2))
        for y in [y for y in late if y[0] <= units or y[1] and units == 0 and y[1] <= maxima]:
            late.remove(y)
            out.append(y[2])
    return out + [y[2] for y in late]


def plan():
    items = whole_plan()
    cuts = [items.index(("unit", r, CUT, 0)) for r in range(NIT)] + [len(items)]
    parts = [[(x[0], x[1] - r, *x[2:]) for x in items[cuts[r]:cuts[r + 1]]] for r in range(NIT)]
    assert all(p == parts[0] for p in parts[:NIT - 2])
    return items[:cuts[0]], parts[0], parts[NIT - 2], parts[NIT - 1]


def open_stage(nc, ctx):
    def sb(name, shape, dt=fp32):
        return ctx.enter_context(nc.sbuf_tensor(name, shape, dt))

    def pb(name, shape, dt=fp32):
        return ctx.enter_context(nc.psum_tensor(name, shape, dt))

    def sem(name):
        return ctx.enter_context(nc.semaphore(name))

    return sb, pb, sem


def stage_setup(nc, g):
    with ExitStack() as ctx:
        sb, pb, sem = open_stage(nc, ctx)
        wmod = sb("wmod", [P, KC, 6 * D])
        cT = sb("cT", [P, KC, B])
        ex = sb("ex", [P, KC, B])
        e1 = sb("e1", [P, KC, B])
        rc = sb("rc", [P, KC, B])
        sc = sb("sc", [P, KC, B])
        scb = sb("scb", [P, B, KC, P])
        ones = sb("ones0", [P, P])
        sgn = sb("sgn", [P, B, 2, D])
        val = sb("val", [P, B, 2, D])
        mag = sb("mag", [P, B, 2, D])
        al = sb("al", [H, S])
        alr = sb("alr", [H, S])
        alp = sb("alp", [H, 3, S], bf16)
        bb = sb("bb", [P, (E * F + E * D) // P])
        bbr = sb("bbr", [P, (E * F + E * D) // P])
        bbp = sb("bbp", [P, 3, (E * F + E * D) // P], bf16)
        zero = sb("zero", [P, TPC, D])
        ps_col = pb("ps_col", [P, 8, B])
        ps_row = pb("ps_row", [P, 2, CH])
        loaded, wmod_in, al_in, bb_in = sem("loaded"), sem("wmod_in"), sem("al_in"), sem("bb_in")
        exp_done, silu_done, cols_done, rows_done, rows_read = (
            sem("exp_done"), sem("silu_done"), sem("cols_done"), sem("rows_done"), sem("rows_read"))
        dve, pool, ones_set, stored, weights = (
            sem("dve_chain"), sem("pool_chain"), sem("ones_set"), sem("stored"), sem("weights"))
        nb1 = E * F // P
        with nc.Block() as block:
            @block.sync
            def _(sp):
                sp.dma_start(cT[:], g.cT).then_inc(loaded, 16)
                sp.dma_start(g.const[:], g.const_dram).then_inc(loaded, 16)
                sp.dma_start(wmod[:], g.wmod.rearrange("(k p) n -> p k n", p=P)).then_inc(wmod_in, 16)
                sp.dma_start(al[:], g.alibi).then_inc(al_in, 16)
                sp.dma_start(bb[:, 0:nb1], g.b1.rearrange("e (a n) -> (e a) n", n=nb1)).then_inc(bb_in, 16)
                sp.dma_start(bb[:, nb1:], g.b2.rearrange("e (a n) -> (e a) n", n=E * D // P)).then_inc(bb_in, 16)
                sp.dma_start(g.wqkv[:], g.wqkvT.rearrange("(k p) n -> p k n", p=P)).then_inc(weights, 16)
                sp.wait_ge(pool, 5)
                for b in range(B):
                    sp.dma_start(g.pos_rows[b * NG:(b + 1) * NG].rearrange("g j s t -> (g j) s t"),
                                 alp[:]).then_inc(stored, 16)
                sp.wait_ge(pool, 10)
                sp.dma_start(g.b1_rows.rearrange("s (p n) -> p s n", p=P), bbp[:, :, 0:nb1]).then_inc(stored, 16)
                sp.dma_start(g.b2_rows.rearrange("s (p n) -> p s n", p=P), bbp[:, :, nb1:]).then_inc(stored, 16)
                sp.wait_ge(pool, 11)
                for i in range(0, SLOTS + 2, TPC):
                    n = min(TPC, SLOTS + 2 - i)
                    sp.dma_start(g.sorted_h[i * P:(i + n) * P, :].rearrange("(n p) d -> p n d", p=P),
                                 zero[:, 0:n, :]).then_inc(stored, 16)
                sp.wait_ge(weights, 16)
                sp.wait_ge(stored, 16 * (B + 2 + -(-(SLOTS + 2) // TPC)))

            @block.gpsimd
            def _(gp):
                def link(ins):
                    link.n += 1
                    ins.then_inc(pool, 1)
                    gp.wait_ge(pool, link.n)
                link.n = 0
                for src, rest, parts, ready in ((al, alr, alp, al_in), (bb, bbr, bbp, bb_in)):
                    gp.wait_ge(ready, 16 if src is al else 32)
                    link(nc.gpsimd.tensor_copy(parts[:, 0, :], src[:]))
                    link(nc.gpsimd.tensor_tensor(rest[:], src[:], parts[:, 0, :], ALU.subtract))
                    link(nc.gpsimd.tensor_copy(parts[:, 1, :], rest[:]))
                    link(nc.gpsimd.tensor_tensor(rest[:], rest[:], parts[:, 1, :], ALU.subtract))
                    link(nc.gpsimd.tensor_copy(parts[:, 2, :], rest[:]))
                link(nc.gpsimd.memset(zero[:], 0.0))

            @block.scalar
            def _(act):
                act.wait_ge(loaded, 32)
                nc.scalar.activation(ex[:], cT[:], ACT.Exp, scale=-1.0).then_inc(exp_done, 1)

            @block.vector
            def _(v):
                def link(ins):
                    link.n += 1
                    ins.then_inc(dve, 1)
                    v.wait_ge(dve, link.n)
                link.n = 0
                v.wait_ge(loaded, 32)
                nc.vector.memset(ones[:], 1.0)
                nc.vector.tensor_copy(g.ident_b[:], g.const[:, C_ID:C_ID + P])
                nc.vector.tensor_copy(g.mask_q[:], g.const[:, C_MQ:C_MQ + P])
                link(nc.vector.tensor_copy(g.mask_k[:], g.const[:, C_MK:C_MK + P]))
                v.wait_ge(exp_done, 1)
                link(nc.vector.tensor_scalar(e1[:], ex[:], 1.0, None, ALU.add))
                link(nc.vector.reciprocal(rc[:], e1[:]))
                link(nc.vector.tensor_tensor(sc[:], rc[:], cT[:], ALU.mult))
                for b in range(B):
                    for k in range(KC):
                        last = nc.vector.tensor_scalar(scb[:, b, k, :], ones[:], sc[:, k, b:b + 1], None, ALU.mult)
                last.then_inc(silu_done, 1)
                v.wait_ge(cols_done, 1)
                nc.vector.tensor_copy(g.shift[:], ps_col[:, 0:KC, :])
                nc.vector.tensor_scalar(g.gain[:], ps_col[:, KC:2 * KC, :], 1.0, None, ALU.add)
                for b in range(B):
                    v.wait_ge(rows_done, b + 1)
                    nc.vector.tensor_copy(g.mod[:, b, 1, :], ps_row[:, 0, D:2 * D])
                    nc.vector.tensor_scalar(g.mod[:, b, 2, :], ps_row[:, 1, 0:D], 1.0, None, ALU.add)
                    for i, gate in ((0, ps_row[:, 0, 0:D]), (1, ps_row[:, 1, D:2 * D])):
                        nc.vector.tensor_scalar(sgn[:, b, i, :], gate, 0.0, 2.0, ALU.is_ge, ALU.mult)
                        link(nc.vector.tensor_copy(val[:, b, i, :], gate))
                        last = nc.vector.scalar_tensor_tensor(mag[:, b, i, :], gate, -1.0, val[:, b, i, :],
                                                              ALU.mult, ALU.max)
                    last.then_inc(rows_read, 1)
                    v.wait_ge(rows_read, b + 1)
                    link(nc.vector.tensor_scalar(mag[:, b, :, :], mag[:, b, :, :], 0.25, None, ALU.max))
                    for i, row in ((0, 0), (1, 3)):
                        link(nc.vector.scalar_tensor_tensor(g.mod[:, b, row, :], sgn[:, b, i, :], 1.0,
                                                            mag[:, b, i, :], ALU.subtract, ALU.mult))

            @block.tensor
            def _(pe):
                pe.wait_ge(silu_done, 1)
                pe.wait_ge(wmod_in, 16)
                for n in range(2 * KC):
                    for k in range(KC):
                        last = nc.tensor.matmul(ps_col[:, n, :], wmod[:, k, n * P:(n + 1) * P], sc[:, k, :],
                                                start=(k == 0), stop=(k == KC - 1))
                last.then_inc(cols_done, 1)
                for b in range(B):
                    if b:
                        pe.wait_ge(rows_read, b)
                    for n in range(2):
                        for k in range(KC):
                            last = nc.tensor.matmul(ps_row[:, n, :], scb[:, b, k, :],
                                                    wmod[:, k, 2 * D + n * CH:2 * D + (n + 1) * CH],
                                                    start=(k == 0), stop=(k == KC - 1))
                    last.then_inc(rows_done, 1)


def stage_qkv(nc, g):
    with ExitStack() as ctx:
        sb, pb, sem = open_stage(nc, ctx)
        xt = sb("xt", [P, 2, TPC, D])
        st = sb("st", [P, TPC, 6])
        mv = sb("mv", [P, TPC, 2])
        ve, sd, rs = sb("ve", [P, TPC]), sb("sd", [P, TPC]), sb("rs", [P, TPC])
        xn = sb("xn", [P, 2, TPC, D])
        hT = sb("hT", [P, 2, KC, CH])
        rest = sb("rest", [P, 2, CH])
        parts = sb("parts", [P, 2, 3, CH], bf16)
        vp = sb("vp", [P, 2, 2, H, HW])
        ps_t = pb("ps_t", [P, KC, CH])
        ps_q = pb("ps_q", [P, 2, CH])
        ps_v = pb("ps_v", [P, 2, 2, D])
        x_in = [sem(f"x_in{i}") for i in range(2)]
        dve, normed, turned, moded = sem("dve_chain1"), sem("normed"), sem("turned"), sem("moded")
        qk_done, part1, rest_done, pool, v_done, v_set = (
            sem("qk_done"), sem("part1"), sem("rest_done"), sem("pool1"), sem("v_done"), sem("v_set"))
        parts_out = [sem(f"parts_out{i}") for i in range(2)]
        v_out = [sem(f"v_out{i}") for i in range(2)]
        part2 = sem("part2")
        vp_set, var_done, sd_done = sem("vp_set"), sem("var_done"), sem("sd_done")
        x_v = g.x.rearrange("b (n t p) d -> (b n) p t d", p=P, t=TPC)
        v_v = g.v_rows.rearrange("(b g) (n p) c -> b n p g c", b=B, p=P)
        NF = 4

        with nc.Block() as block:
            @block.sync
            def _(sp):
                for n in range(2):
                    sp.dma_start(xt[:, n, :, :], x_v[n]).then_inc(x_in[n], 16)
                for n in range(NCH):
                    b, c = n // CPB, n % CPB
                    for f in range(NF):
                        u = n * NF + f
                        sp.wait_ge(pool, u + 1)
                        for half in range(2):
                            sp.dma_start(
                                g.qk_rows[b * NG + (f % 2) * 2 + half, f // 2, :, :, c * CH:(c + 1) * CH]
                                .rearrange("s r t -> r s t"),
                                parts[half * 64:(half + 1) * 64, u % 2, :, :]).then_inc(parts_out[u % 2], 16)
                    for w in range(2):
                        u = n * 2 + w
                        sp.wait_ge(v_set, u + 1)
                        for i in range(2):
                            tile = c * TPC + 2 * w + i
                            sp.dma_start(v_v[b, tile], vp[:, u % 2, i, :, :].rearrange("p (g j) c -> p g (j c)", g=NG)
                                         ).then_inc(v_out[u % 2], 16)
                    if n + 2 < NCH:
                        sp.wait_ge(normed, n + 1)
                        sp.dma_start(xt[:, n % 2, :, :], x_v[n + 2]).then_inc(x_in[n % 2], 16)
                for i in range(2):
                    sp.wait_ge(parts_out[i], 32 * NCH * NF // 2)
                    sp.wait_ge(v_out[i], 32 * NCH)

            @block.vector
            def _(v):
                def link(ins):
                    link.n += 1
                    ins.then_inc(dve, 1)
                    v.wait_ge(dve, link.n)
                link.n = 0

                def norm(n):
                    v.wait_ge(x_in[n % 2], 16 * (n // 2 + 1))
                    for t in range(TPC):
                        last = nc.vector.bn_stats(st[:, t, :], xt[:, n % 2, t, :])
                    link(last)
                    for t in range(TPC):
                        last = nc.vector.bn_aggr(mv[:, t, :], st[:, t, :])
                    link(last)
                    nc.vector.tensor_scalar(ve[:], mv[:, :, 1], EPS, None, ALU.add).then_inc(var_done, 1)
                    v.wait_ge(sd_done, n + 1)
                    link(nc.vector.reciprocal(rs[:], sd[:]))
                    if n >= 2:
                        v.wait_ge(turned, n - 1)
                    for t in range(TPC):
                        last = nc.vector.tensor_scalar(xn[:, n % 2, t, :], xt[:, n % 2, t, :], mv[:, t, 0:1],
                                                       rs[:, t:t + 1], ALU.subtract, ALU.mult)
                    last.then_inc(normed, 1)
                    v.wait_ge(normed, n + 1)

                for i in range(2):
                    nc.vector.memset(vp[:, i, :, :, HD:HW], 0.0).then_inc(vp_set, 1)
                v.wait_ge(vp_set, 2)
                for i in range(2):
                    nc.vector.memset(vp[:, i, :, :, HD:HD + 1], 1.0).then_inc(vp_set, 1)
                norm(0)
                for n in range(NCH):
                    for f in range(NF):
                        u = n * NF + f
                        v.wait_ge(part1, u + 1)
                        if u >= 2:
                            v.wait_ge(pool, u - 1)
                        nc.vector.scalar_tensor_tensor(rest[:, u % 2, :], ps_q[:, u % 2, :],
                                                       SCALE if f < 2 else 1.0, parts[:, u % 2, 0, :],
                                                       ALU.mult, ALU.subtract).then_inc(rest_done, 1)
                        if f == 1 and n + 1 < NCH:
                            norm(n + 1)
                    for w in range(2):
                        u = n * 2 + w
                        v.wait_ge(v_done, u + 1)
                        if u >= 2:
                            v.wait_ge(v_out[u % 2], 32 * (u // 2))
                        for i in range(2):
                            last = nc.vector.tensor_copy(vp[:, u % 2, i, :, 0:HD],
                                                         ps_v[:, u % 2, i, :].rearrange("p (h c) -> p h c", c=HD))
                        last.then_inc(v_set, 1)

            @block.scalar
            def _(act):
                def modulate(n):
                    act.wait_ge(turned, n + 1)
                    if n >= 2:
                        act.wait_ge(v_done, 2 * (n - 1))
                    for k in range(KC):
                        last = nc.scalar.activation(hT[:, n % 2, k, :], ps_t[:, k, :], ACT.Identity,
                                                    bias=g.shift[:, k, n // CPB:n // CPB + 1],
                                                    scale=g.gain[:, k, n // CPB:n // CPB + 1])
                    last.then_inc(moded, 1)

                def second_part(u):
                    act.wait_ge(rest_done, u + 1)
                    nc.scalar.copy(parts[:, u % 2, 1, :], rest[:, u % 2, :]).then_inc(part2, 1)

                def deviation(n):
                    act.wait_ge(var_done, n + 1)
                    nc.scalar.activation(sd[:], ve[:], ACT.Sqrt).then_inc(sd_done, 1)

                deviation(0)
                modulate(0)
                for n in range(NCH):
                    for f in range(NF):
                        u = n * NF + f
                        if f == 2 and n + 1 < NCH:
                            deviation(n + 1)
                        act.wait_ge(qk_done, u + 1)
                        if u >= 2:
                            act.wait_ge(parts_out[u % 2], 32 * (u // 2))
                        nc.scalar.activation(parts[:, u % 2, 0, :], ps_q[:, u % 2, :], ACT.Copy,
                                             scale=SCALE if f < 2 else 1.0).then_inc(part1, 1)
                        if u:
                            second_part(u - 1)
                    if n + 1 < NCH:
                        modulate(n + 1)
                second_part(NCH * NF - 1)

            @block.gpsimd
            def _(gp):
                for u in range(NCH * NF):
                    gp.wait_ge(part2, u + 1)
                    nc.gpsimd.tensor_tensor(parts[:, u % 2, 2, :], rest[:, u % 2, :], parts[:, u % 2, 1, :],
                                            ALU.subtract).then_inc(pool, 1)

            @block.tensor
            def _(pe):
                def turn(n):
                    pe.wait_ge(normed, n + 1)
                    if n:
                        pe.wait_ge(moded, n)
                    for k in range(KC):
                        for t in range(TPC):
                            last = nc.tensor.transpose(ps_t[:, k, t * P:(t + 1) * P],
                                                       xn[:, n % 2, t, k * P:(k + 1) * P], g.const[:, C_ID:C_ID + P])
                    last.then_inc(turned, 1)

                turn(0)
                for n in range(NCH):
                    pe.wait_ge(moded, n + 1)
                    for f in range(NF):
                        u = n * NF + f
                        if u >= 2:
                            pe.wait_ge(rest_done, u - 1)
                        for k in range(KC):
                            last = nc.tensor.matmul(ps_q[:, u % 2, :], g.wqkv[:, k, f * P:(f + 1) * P],
                                                    hT[:, n % 2, k, :], start=(k == 0), stop=(k == KC - 1))
                        last.then_inc(qk_done, 1)
                    if n + 1 < NCH:
                        turn(n + 1)
                    for w in range(2):
                        u = n * 2 + w
                        if u >= 2:
                            pe.wait_ge(v_set, u - 1)
                        for i in range(2):
                            t = 2 * w + i
                            for k in range(KC):
                                last = nc.tensor.matmul(ps_v[:, u % 2, i, :], hT[:, n % 2, k, t * P:(t + 1) * P],
                                                        g.wqkv[:, k, 2 * D:3 * D], start=(k == 0), stop=(k == KC - 1))
                        last.then_inc(v_done, 1)


def stage_attention(nc, g):
    with ExitStack() as ctx:
        sb, pb, sem = open_stage(nc, ctx)
        kh = sb("kh", [P, 2, G, S], bf16)
        qh = sb("qh", [P, 2, G, S], bf16)
        vh = sb("vh", [P, 2, S // P, P])
        pr = sb("pr", [P, 2, G, CH])
        part = sb("part", [P, 2, 2, TPC, G])
        mx = sb("mx", [P, TPC, G])
        ms = sb("ms", [P, TPC, G, 3], bf16)
        none = sb("none", [P, TPC, G])
        mrow = sb("mrow", [G * 3, CH], bf16)
        osb = sb("osb", [P, CH])
        rsum = sb("rsum", [P, TPC, G])
        on = sb("on", [P, 2, TPC, G * HD])
        ps_s = pb("ps_s", [P, 2, PIECE])
        ps_w = pb("ps_w", [P, 2, CH])
        ps_o = pb("ps_o", [P, CH])
        ps_m = pb("ps_m", [P, TPC, P])
        rows_set, none_set, mx_done = sem("rows_set"), sem("none_set"), sem("mx_done")
        loaded = [sem(f"loaded{i}") for i in range(2)]
        s_ready, s_read = sem("s_ready"), sem("s_read")
        w_ready, p_ready, pv_done = sem("w_ready"), sem("p_ready"), sem("pv_done")
        pool, m_turned, m_copied, m_in = sem("pool2"), sem("m_turned"), sem("m_copied"), sem("m_in")
        o_copied, o_turned, r_done, on_ready = sem("o_copied"), sem("o_turned"), sem("r_done"), sem("on_ready")
        o_out = [sem(f"o_out{i}") for i in range(2)]
        NLOAD = 15
        MOPS = 5
        before, turn, tail0, tail1 = plan()
        psm_b = ps_m[0:G * 3, 0:TPC // 2, :].rearrange("p t q -> p (t q)").bitcast(bf16)
        sums = ps_m[:].rearrange("p t (j c) -> p t j c", j=G)

        def over(eng, do):
            do(before, 0, 0, True)
            with eng.Fori(0, NIT // 2 - 1) as n:
                for u in range(2):
                    do(turn, n, u, False)
            do(tail0, NIT // 2 - 1, 0, False)
            do(tail1, NIT // 2 - 1, 1, False)

        ROWS0, NORMS0 = (sum(x[0] == kind for x in before) for kind in ("rows", "norm"))

        with nc.Block() as block:
            @block.sync
            def _(sp):
                def load(r, u):
                    src = g.qk_rows[bass.ds(r, 1)].rearrange("a w s (j d) t -> (a w) s d j t", d=HD)
                    for k in range(6):
                        rows = slice(k * HD, (k + 1) * HD)
                        sp.dma_start(kh[rows, u, :, :], src[1, K_PART[k]]).then_inc(loaded[u], 16)
                        sp.dma_start(qh[rows, u, :, :], src[0, Q_PART[k]]).then_inc(loaded[u], 16)
                    sp.dma_start(kh[R_POS:R_MAX, u, :, :],
                                 g.pos_rows[bass.ds(r, 1)].rearrange("a j s t -> s (a j) t")
                                 ).then_inc(loaded[u], 16)
                    for z in (slice(0, P // 2), slice(P // 2, P)):
                        sp.dma_start(vh[z, u, :, :],
                                     g.v_rows[bass.ds(r, 1)].rearrange("a (n p) c -> p (a n) c", p=P)[z]
                                     ).then_inc(loaded[u], 16)

                def do(items, n, u, first):
                    for kind, dr, *a in items:
                        r, ru = n * 2 + u + dr, (u + dr) % 2
                        if kind == "rows":
                            c, = a
                            sp.wait_ge(m_copied, r * CPB + c + 1)
                            for j in range(G):
                                sp.dma_start(qh[R_MAX:R_ALL, ru, j, c * CH:(c + 1) * CH],
                                             mrow[3 * j:3 * j + 3, :]).then_inc(m_in, 16)
                        elif kind == "load":
                            sp.wait_ge(pv_done, (r - 1) * NS + 2)
                            load(r, ru)
                        elif kind == "norm":
                            c, = a
                            sp.wait_ge(on_ready, r * CPB + c + 2)
                            sp.dma_start(g.att_rows[bass.ds(r, 1), :, c * TPC:(c + 1) * TPC, :]
                                         .rearrange("a p t d -> p (a t) d"), on[:, c % 2, :, :]
                                         ).then_inc(o_out[c % 2], 16)

                for i in range(2):
                    sp.sem_inc(o_out[i], 1)
                sp.wait_ge(rows_set, 4)
                load(0, 0)
                load(1, 1)
                for k in range(KC):
                    sp.dma_start(g.w1[:, k, :, :], g.w1_dram.rearrange("e (k p) n -> k p e n", p=P)[k]
                                 ).then_inc(g.w1_in, 16)
                over(sp, do)
                for i in range(2):
                    sp.wait_ge(o_out[i], 16 * NIT * CPB // 2 + 1)

            @block.tensor
            def _(pe):
                def maxima(n, u, r, ru, dr, k, i):
                    c, t = PIECES[k][:2]
                    j, at, a, z, diag = products(k)[i]
                    count = r * NP + k
                    if k == 0 and i == 0:
                        pe.wait_ge(loaded[ru], (n + (u + dr) // 2 + 1) * 16 * NLOAD)
                    if i == 0 and (not isinstance(count, int) or count >= 2):
                        pe.wait_ge(s_read, count - 1)
                    q0 = (c * TPC + t) * P
                    mm = nc.tensor.matmul(ps_s[:, k % 2, at + a:at + z], qh[0:R_MAX, ru, j, q0:q0 + P],
                                          kh[0:R_MAX, ru, j, a:z], start=True, stop=not diag)
                    if diag:
                        mm = nc.tensor.matmul(ps_s[:, k % 2, at + z - P:at + z], g.ident_b[:], g.mask_q[:],
                                              start=False, stop=True)
                    if i == len(products(k)) - 1:
                        mm.then_inc(s_ready, 1)

                def scores(r, ru, s, i):
                    c, kb = STEPS[s]
                    col = step_cols(c, kb)
                    w = CH - col
                    bank = (UNITS[s] + i) % 2
                    heads = step_units(s)[i]
                    pe.wait_ge(p_ready, r * UNITS[NS] + UNITS[s] + i + 1)
                    diag = kb >= c * TPC
                    for j in heads:
                        at = (j - heads[0]) * w
                        mm = nc.tensor.matmul(ps_w[:, bank, at:at + w], kh[0:R_ALL, ru, j, kb * P:(kb + 1) * P],
                                              qh[0:R_ALL, ru, j, c * CH + col:(c + 1) * CH],
                                              start=True, stop=not diag)
                        if diag:
                            mm = nc.tensor.matmul(ps_w[:, bank, at:at + P], g.ident_b[:], g.mask_k[:],
                                                  start=False, stop=True)
                    mm.then_inc(w_ready, 1)

                def values(r, ru, s):
                    c, kb = STEPS[s]
                    col = step_cols(c, kb)
                    q = r * CPB + c
                    if kb == 0 and (not isinstance(q, int) or q >= 1):
                        pe.wait_ge(o_copied, q)
                    pe.wait_ge(p_ready, r * UNITS[NS] + UNITS[s + 1] + 2)
                    for j in range(G):
                        mm = nc.tensor.matmul(ps_o[HW * j:HW * (j + 1), col:CH], vh[:, ru, kb, HW * j:HW * (j + 1)],
                                              pr[:, s % 2, j, col:CH], start=(kb == 0),
                                              stop=(kb == TPC * (c + 1) - 1))
                    mm.then_inc(pv_done, 1)

                def do(items, n, u, first):
                    rows = 0 if first else (n * 2 + u) * CPB + ROWS0
                    norms = 0 if first else (n * 2 + u) * CPB + NORMS0
                    for kind, dr, *a in items:
                        r, ru = n * 2 + u + dr, (u + dr) % 2
                        if kind == "unit":
                            s, i = a
                            c, kb = STEPS[s]
                            if kb == 0 and i == 0:
                                pe.wait_ge(m_in, (r * CPB + c + 1) * 16 * G)
                            scores(r, ru, s, i)
                        elif kind == "values":
                            values(r, ru, a[0])
                        elif kind == "part":
                            maxima(n, u, r, ru, dr, *a)
                        elif kind == "max":
                            maxima(n, u, r, ru, dr, *a, len(products(a[0])) - 1)
                        elif kind == "rows":
                            pe.wait_ge(pool, (r * CPB + a[0] + 1) * MOPS)
                            if not isinstance(rows, int) or rows >= 1:
                                pe.wait_ge(m_copied, rows)
                            pe.wait_ge(on_ready, norms + 1)
                            for t in range(TPC):
                                mm = nc.tensor.transpose(psm_b[:, t * P:(t + 1) * P],
                                                         ms[:, t, :, :].rearrange("p j s -> p (j s)"), g.ident_b[:])
                            mm.then_inc(m_turned, 1)
                            rows = rows + 1
                        elif kind == "norm":
                            pe.wait_ge(o_copied, r * CPB + a[0] + 1)
                            pe.wait_ge(m_copied, rows)
                            pe.wait_ge(on_ready, norms + 1)
                            for t in range(TPC):
                                mm = nc.tensor.transpose(ps_m[:, t, :], osb[:, t * P:(t + 1) * P],
                                                         g.const[:, C_ID:C_ID + P])
                            mm.then_inc(o_turned, 1)
                            norms = norms + 1

                pe.sem_inc(o_turned, 1)
                over(pe, do)

            @block.scalar
            def _(act):
                def weights(r, s, i):
                    col = step_cols(*STEPS[s])
                    w = CH - col
                    heads = step_units(s)[i]
                    j, h = heads[0], len(heads)
                    if i == 0:
                        act.wait_ge(pv_done, r * NS + s + 1)
                    act.wait_ge(w_ready, r * UNITS[NS] + UNITS[s] + i + 1)
                    nc.scalar.activation(pr[:, s % 2, j:j + h, col:CH],
                                         ps_w[:, (UNITS[s] + i) % 2, 0:h * w].rearrange("p (h q) -> p h q", h=h),
                                         ACT.Exp).then_inc(p_ready, 1)

                def do(items, n, u, first):
                    for kind, dr, *a in items:
                        r = n * 2 + u + dr
                        if kind == "unit":
                            weights(r, *a)
                        elif kind == "rows":
                            q = r * CPB + a[0]
                            act.wait_ge(m_turned, q + 1)
                            if not isinstance(q, int) or q >= 1:
                                act.wait_ge(m_in, q * 16 * G)
                            nc.scalar.copy(mrow[:], psm_b).then_inc(m_copied, 1)
                        elif kind == "take":
                            c, = a
                            q = r * CPB + c
                            act.wait_ge(pv_done, r * NS + STEPS.index((c, TPC * (c + 1) - 1)) + 3)
                            act.wait_ge(o_turned, q + 1)
                            nc.scalar.copy(osb[:], ps_o[:]).then_inc(o_copied, 1)

                act.sem_inc(p_ready, 2)
                over(act, do)

            @block.vector
            def _(v):
                def do(items, n, u, first):
                    for kind, dr, *a in items:
                        r = n * 2 + u + dr
                        if kind == "max":
                            k, = a
                            c, t, j, nh, i, k0, k1, last = PIECES[k]
                            w = seat(k1 - k0)
                            v.wait_ge(s_ready, r * NP + k + 1)
                            nc.vector.tensor_reduce(
                                part[:, c % 2, i, t, j:j + nh],
                                ps_s[:, k % 2, 0:nh * w].rearrange("p (h k) -> p h k", h=nh)[:, :, 0:k1 - k0],
                                AX.X, ALU.max).then_inc(s_read, 1)
                            if k in CHUNK_END:
                                q = r * CPB + c
                                v.wait_ge(s_read, r * NP + k + 1)
                                if not isinstance(q, int) or q >= 1:
                                    v.wait_ge(pool, q * MOPS)
                                nc.vector.tensor_reduce(
                                    mx[:], part[:, c % 2, 0:i + 1, :, :].rearrange("p i t j -> p t j i"),
                                    AX.X, ALU.max, negate=True).then_inc(mx_done, 1)
                        elif kind == "norm":
                            c, = a
                            q = r * CPB + c
                            v.wait_ge(o_turned, q + 2)
                            nc.vector.reciprocal(rsum[:], sums[:, :, :, HD]).then_inc(r_done, 1)
                            v.wait_ge(r_done, q + 1)
                            v.wait_ge(o_out[c % 2], (r * (CPB // 2) + c // 2) * 16 + 1)
                            nc.vector.tensor_tensor(on[:, c % 2, :, :].rearrange("p t (j d) -> p t j d", j=G),
                                                    sums[:, :, :, 0:HD],
                                                    rsum[:].unsqueeze(3).to_broadcast([P, TPC, G, HD]),
                                                    ALU.mult).then_inc(on_ready, 1)
                v.sem_inc(on_ready, 1)
                over(v, do)

            @block.gpsimd
            def _(gp):
                def do(items, n, u, first):
                    for kind, dr, *a in items:
                        if kind != "rows":
                            continue
                        q = (n * 2 + u + dr) * CPB + a[0]
                        done = 0
                        gp.wait_ge(mx_done, q + 1)
                        if not isinstance(q, int) or q >= 1:
                            gp.wait_ge(m_turned, q)
                        for i in range(3):
                            nc.gpsimd.tensor_tensor(ms[:, :, :, i], mx[:], none[:], ALU.add).then_inc(pool, 1)
                            done += 1
                            if i < 2:
                                gp.wait_ge(pool, q * MOPS + done)
                                nc.gpsimd.tensor_tensor(mx[:], mx[:], ms[:, :, :, i], ALU.subtract
                                                        ).then_inc(pool, 1)
                                done += 1
                                gp.wait_ge(pool, q * MOPS + done)

                gp.sem_inc(pv_done, 2)
                nc.gpsimd.memset(none[:], 0.0).then_inc(none_set, 1)
                gp.wait_ge(none_set, 1)
                for u in range(2):
                    nc.gpsimd.memset(kh[R_POS:R_ALL, u, :, :], 1.0).then_inc(rows_set, 1)
                    nc.gpsimd.memset(qh[R_POS:R_ALL, u, :, :], 1.0).then_inc(rows_set, 1)
                over(gp, do)


def stage_mix(nc, g):
    with ExitStack() as ctx:
        sb, pb, sem = open_stage(nc, ctx)
        RING = 4
        AHEAD = 2
        wo_in = sb("wo_in", [P, KC, D])
        wo = sb("wo", [P, B, KC, D])
        wg = sb("wg", [P, KC, E])
        bg = sb("bg", [P, E])
        eps = sb("eps3", [P, 1])
        at = sb("at", [P, AHEAD, TPC, D])
        aT = sb("aT", [P, 2, KC, P])
        xt = sb("xt3", [P, AHEAD, TPC, D])
        x1 = sb("x1", [P, AHEAD, TPC, D])
        st = sb("st3", [P, RING, 6])
        mv = sb("mv3", [P, RING, 2])
        sd, rs = sb("sd3", [P, RING]), sb("rs3", [P, RING])
        hT = sb("hT3", [P, 2, KC, P])
        ps_i = pb("ps_i", [P, 2, CH])
        ps_a = pb("ps_a", [P, 2, CH])
        ps_t = pb("ps_t3", [P, 2, CH])
        ps_l = pb("ps_l", [P, 2, CH])
        w_in = sem("w_in3")
        in3 = [sem(f"in3_{i}") for i in range(AHEAD)]
        wo_ready, i_turned, i_copied, a_done, x1_ready = (
            sem("wo_ready"), sem("i_turned"), sem("i_copied"), sem("a_done"), sem("x1_ready"))
        st_ready, mv_ready, sd_ready, rs_ready, scaled, h_ready = (
            sem("st_ready"), sem("mv_ready"), sem("sd_ready"), sem("rs_ready"), sem("scaled"), sem("h_ready"))
        turned, h_copied, l_done, l_read = sem("turned3"), sem("h_copied"), sem("l_done"), sem("l_read")
        x1_out = [sem(f"x1_out{i}") for i in range(AHEAD)]
        x_v = g.x.rearrange("b (n t p) d -> (b n) p t d", p=P, t=TPC)
        x1_v = g.x1_rows.rearrange("(n t p) d -> n p t d", p=P, t=TPC)
        MIX, SUM, NORM, TURN, GATE = 1, 1, 2, 5, 6

        def at_tile(u):
            return u // TPC, u // TPC % AHEAD, u % TPC

        with nc.Block() as block:
            @block.sync
            def _(sp):
                def load(n):
                    b, c = n // CPB, n % CPB
                    for i in range(NG):
                        sp.dma_start(at[:, n % AHEAD, :, i * G * HD:(i + 1) * G * HD],
                                     g.att_rows[b * NG + i, :, c * TPC:(c + 1) * TPC, :]
                                     ).then_inc(in3[n % AHEAD], 16)
                    sp.dma_start(xt[:, n % AHEAD, :, :], x_v[n]).then_inc(in3[n % AHEAD], 16)

                sp.dma_start(wo_in[:], g.woT.rearrange("(k p) n -> p k n", p=P)).then_inc(w_in, 16)
                sp.dma_start(wg[:], g.wg.rearrange("(k p) e -> p k e", p=P)).then_inc(w_in, 16)
                sp.dma_start(bg[:], g.bg.unsqueeze(0).to_broadcast([P, E])).then_inc(w_in, 16)
                for n in range(AHEAD):
                    load(n)
                for k in range(FC):
                    sp.dma_start(g.w2_s[:, k, :, :], g.w2.rearrange("e (k p) n -> k p e n", p=P)[k]
                                 ).then_inc(g.w2_in, 16)
                for n in range(NCH):
                    sp.wait_ge(x1_ready, TPC * (n + 1))
                    sp.dma_start(x1_v[n], x1[:, n % AHEAD, :, :]).then_inc(x1_out[n % AHEAD], 16)
                    if n + AHEAD < NCH:
                        load(n + AHEAD)
                for i in range(AHEAD):
                    sp.wait_ge(x1_out[i], 16 * NCH // AHEAD)

            @block.tensor
            def _(pe):
                def turn_in(u):
                    n, buf, t = at_tile(u)
                    if t == 0:
                        pe.wait_ge(in3[buf], 16 * (NG + 1) * (n // AHEAD + 1))
                    if u >= 2:
                        pe.wait_ge(i_copied, u - 1)
                    for k in range(KC):
                        mm = nc.tensor.transpose(ps_i[:, u % 2, k * P:(k + 1) * P],
                                                 at[:, buf, t, k * P:(k + 1) * P], g.const[:, C_ID:C_ID + P])
                    mm.then_inc(i_turned, 1)

                def mix(u):
                    pe.wait_ge(i_copied, u + 1)
                    if u >= 2:
                        pe.wait_ge(x1_ready, u - 1)
                    for k in range(KC):
                        mm = nc.tensor.matmul(ps_a[:, u % 2, 0:D], aT[:, u % 2, k, :], wo[:, u // (NT // B), k, :],
                                              start=(k == 0), stop=(k == KC - 1))
                    mm.then_inc(a_done, 1)

                def turn(u):
                    pe.wait_ge(h_ready, u + 1)
                    if u >= 2:
                        pe.wait_ge(h_copied, u - 1)
                    for k in range(KC):
                        mm = nc.tensor.transpose(ps_t[:, u % 2, k * P:(k + 1) * P],
                                                 g.h2[:, u, k * P:(k + 1) * P], g.const[:, C_ID:C_ID + P])
                    mm.then_inc(turned, 1)

                def gate(u):
                    n, _, t = at_tile(u)
                    pe.wait_ge(h_copied, u + 1)
                    if t == 0 and n >= 2:
                        pe.wait_ge(l_read, n - 1)
                    for k in range(KC):
                        mm = nc.tensor.matmul(ps_l[:, n % 2, t * E:(t + 1) * E], hT[:, u % 2, k, :], wg[:, k, :],
                                              start=(k == 0), stop=(k == KC - 1))
                    mm.then_inc(l_done, 1)

                pe.wait_ge(w_in, 48)
                pe.wait_ge(wo_ready, 1)
                for u in range(NT + GATE):
                    if u < NT:
                        turn_in(u)
                    if 0 <= u - MIX < NT:
                        mix(u - MIX)
                    if 0 <= u - TURN < NT:
                        turn(u - TURN)
                    if 0 <= u - GATE < NT:
                        gate(u - GATE)

            @block.scalar
            def _(act):
                for u in range(NT + TURN):
                    if u < NT:
                        act.wait_ge(i_turned, u + 1)
                        if u >= 2:
                            act.wait_ge(a_done, u - 1)
                        nc.scalar.copy(aT[:, u % 2, :, :], ps_i[:, u % 2, 0:D].rearrange("p (k t) -> p k t", k=KC)
                                       ).then_inc(i_copied, 1)
                    w = u - NORM
                    if 0 <= w < NT:
                        act.wait_ge(mv_ready, w + 1)
                        if w >= RING:
                            act.wait_ge(rs_ready, w - RING + 1)
                        nc.scalar.activation(sd[:, w % RING:w % RING + 1], mv[:, w % RING, 1:2], ACT.Sqrt,
                                             bias=eps[:, 0:1]).then_inc(sd_ready, 1)
                    w = u - TURN
                    if 0 <= w < NT:
                        act.wait_ge(turned, w + 1)
                        if w >= 2:
                            act.wait_ge(l_done, w - 1)
                        nc.scalar.copy(hT[:, w % 2, :, :], ps_t[:, w % 2, 0:D].rearrange("p (k t) -> p k t", k=KC)
                                       ).then_inc(h_copied, 1)

            @block.vector
            def _(v):
                v.wait_ge(w_in, 48)
                nc.vector.memset(eps[:], EPS)
                for b in range(B):
                    for k in range(KC):
                        last = nc.vector.tensor_tensor(wo[:, b, k, :], wo_in[:, k, :], g.mod[:, b, 0, :], ALU.mult)
                last.then_inc(wo_ready, 1)
                for u in range(NT + GATE + 2):
                    if u < NT:
                        n, buf, t = at_tile(u)
                        if t == 0 and n >= AHEAD:
                            v.wait_ge(x1_out[buf], 16 * (n // AHEAD))
                            v.wait_ge(scaled, TPC * (n - AHEAD + 1))
                        v.wait_ge(a_done, u + 1)
                        nc.vector.tensor_tensor(x1[:, buf, t, :], ps_a[:, u % 2, 0:D], xt[:, buf, t, :], ALU.add
                                                ).then_inc(x1_ready, 1)
                    w = u - 1
                    if 0 <= w < NT:
                        v.wait_ge(st_ready, w + 1)
                        if w >= RING:
                            v.wait_ge(scaled, w - RING + 1)
                            v.wait_ge(sd_ready, w - RING + 1)
                        nc.vector.bn_aggr(mv[:, w % RING, :], st[:, w % RING, :]).then_inc(mv_ready, 1)
                    w = u - 2
                    if 0 <= w < NT:
                        v.wait_ge(sd_ready, w + 1)
                        if w >= RING:
                            v.wait_ge(h_ready, w - RING + 1)
                        nc.vector.reciprocal(rs[:, w % RING:w % RING + 1], sd[:, w % RING:w % RING + 1]
                                             ).then_inc(rs_ready, 1)
                    if u < NT:
                        v.wait_ge(x1_ready, u + 1)
                        if u >= RING:
                            v.wait_ge(mv_ready, u - RING + 1)
                        nc.vector.bn_stats(st[:, u % RING, :], x1[:, buf, t, :]).then_inc(st_ready, 1)
                    w = u - 1
                    if 0 <= w < NT:
                        _, buf, t = at_tile(w)
                        v.wait_ge(mv_ready, w + 1)
                        if w >= RING:
                            v.wait_ge(h_ready, w - RING + 1)
                        nc.vector.scalar_tensor_tensor(g.h2[:, w, :], x1[:, buf, t, :],
                                                       mv[:, w % RING, 0:1], g.mod[:, w // (NT // B), 2, :],
                                                       ALU.subtract, ALU.mult).then_inc(scaled, 1)
                    w = u - 2
                    if 0 <= w < NT:
                        v.wait_ge(rs_ready, w + 1)
                        v.wait_ge(scaled, w + 1)
                        nc.vector.scalar_tensor_tensor(g.h2[:, w, :], g.h2[:, w, :], rs[:, w % RING:w % RING + 1],
                                                       g.mod[:, w // (NT // B), 1, :], ALU.mult, ALU.add
                                                       ).then_inc(h_ready, 1)
                    n = (u - GATE - 1) // TPC - 1
                    if (u - GATE - 1) % TPC == 0 and n >= 0:
                        v.wait_ge(l_done, TPC * (n + 1))
                        nc.vector.tensor_tensor(g.logits[:, n * TPC:(n + 1) * TPC, :],
                                                ps_l[:, n % 2, 0:TPC * E].rearrange("p (t e) -> p t e", e=E),
                                                bg[:].unsqueeze(1).to_broadcast([P, TPC, E]), ALU.add
                                                ).then_inc(l_read, 1)


def stage_route(nc, g):
    with ExitStack() as ctx:
        sb, pb, sem = open_stage(nc, ctx)
        top = sb("top", [P, NT])
        key = sb("key", [P, NT, E])
        hot = sb("hot", [P, NT, E])
        ones = sb("ones4", [P, P])
        run = sb("run", [P, 2, NT, E])
        tot = sb("tot", [P, NT, E])
        over = sb("over", [P, E, NT])
        tiles = sb("tiles", [P, E])
        cum = sb("cum", [P, 2, E])
        base = sb("base", [P, E])
        slot = sb("slot", [P, NT, E])
        slot_f = sb("slot_f", [P, NT])
        of_tile = sb("of_tile", [P, SLOTS + 1, E])
        exp_f = sb("exp_f", [P, SLOTS + 1])
        ps_p = pb("ps_p", [P, NT, E])
        ps_n = pb("ps_n", [P, NT, E])
        dve, hot_done, sums, slots_done, scattered = (
            sem("dve4"), sem("hot_done"), sem("sums4"), sem("slots_done"), sem("scattered"))
        rank = g.const[:, C_RANK:C_RANK + E]
        with nc.Block() as block:
            @block.vector
            def _(v):
                def link(ins):
                    link.n += 1
                    ins.then_inc(dve, 1)
                    v.wait_ge(dve, link.n)
                link.n = 0
                rank_b = rank.unsqueeze(1).to_broadcast([P, NT, E])
                nc.vector.memset(ones[:], 1.0)
                link(nc.vector.tensor_reduce(top[:], g.logits[:], AX.X, ALU.max))
                link(nc.vector.tensor_tensor(hot[:], g.logits[:], top[:].unsqueeze(2).to_broadcast([P, NT, E]),
                                             ALU.is_equal))
                link(nc.vector.tensor_tensor(key[:], hot[:], rank_b, ALU.mult))
                link(nc.vector.tensor_reduce(top[:], key[:], AX.X, ALU.max))
                nc.vector.tensor_tensor(hot[:], rank_b, top[:].unsqueeze(2).to_broadcast([P, NT, E]),
                                        ALU.is_equal).then_inc(hot_done, 1)
                v.wait_ge(sums, 1)
                nc.vector.tensor_copy(run[:, 0, :, :], ps_n[:])
                link(nc.vector.tensor_copy(tot[:], ps_n[:]))
                i, d = 0, 1
                while d < NT:
                    nc.vector.tensor_copy(run[:, 1 - i, 0:d, :], run[:, i, 0:d, :])
                    link(nc.vector.tensor_tensor(run[:, 1 - i, d:NT, :], run[:, i, d:NT, :], run[:, i, 0:NT - d, :],
                                                 ALU.add))
                    i, d = 1 - i, 2 * d
                link(nc.vector.tensor_tensor(over[:], run[:, i, NT - 1, :].unsqueeze(2).to_broadcast([P, E, NT]),
                                             g.const[:, C_THR:C_THR + NT].unsqueeze(1).to_broadcast([P, E, NT]),
                                             ALU.is_gt))
                link(nc.vector.tensor_reduce(tiles[:], over[:], AX.X, ALU.add))
                link(nc.vector.tensor_copy(cum[:, 0, :], tiles[:]))
                j, d = 0, 1
                while d < E:
                    nc.vector.tensor_copy(cum[:, 1 - j, 0:d], cum[:, j, 0:d])
                    link(nc.vector.tensor_tensor(cum[:, 1 - j, d:E], cum[:, j, d:E], cum[:, j, 0:E - d], ALU.add))
                    j, d = 1 - j, 2 * d
                link(nc.vector.tensor_tensor(base[:], cum[:, j, :], tiles[:], ALU.subtract))
                link(nc.vector.tensor_scalar(base[:], base[:], float(P), None, ALU.mult))
                link(nc.vector.tensor_tensor(slot[:], run[:, i, :, :], tot[:], ALU.subtract))
                link(nc.vector.tensor_tensor(slot[:], ps_p[:], slot[:], ALU.add))
                link(nc.vector.tensor_tensor(slot[:], slot[:], base[:].unsqueeze(1).to_broadcast([P, NT, E]), ALU.add))
                link(nc.vector.tensor_tensor(slot[:], slot[:], hot[:], ALU.mult))
                link(nc.vector.tensor_reduce(slot_f[:], slot[:], AX.X, ALU.add))
                nc.vector.tensor_copy(g.slots[:], slot_f[:]).then_inc(slots_done, 1)
                link(nc.vector.tensor_tensor(of_tile[:], cum[:, j, :].unsqueeze(1).to_broadcast([P, SLOTS + 1, E]),
                                             g.const[:, C_TILE:C_END].unsqueeze(2).to_broadcast([P, SLOTS + 1, E]),
                                             ALU.is_le))
                link(nc.vector.tensor_reduce(exp_f[:], of_tile[:], AX.X, ALU.add))
                link(nc.vector.tensor_scalar(g.expert[:], exp_f[:], float(E - 1), None, ALU.min))

            @block.tensor
            def _(pe):
                pe.wait_ge(hot_done, 1)
                nc.tensor.matmul(ps_p[:].rearrange("p t e -> p (t e)"), g.const[:, C_TRI:C_TRI + P],
                                 hot[:].rearrange("p t e -> p (t e)"), start=True, stop=True)
                nc.tensor.matmul(ps_n[:].rearrange("p t e -> p (t e)"), ones[:],
                                 hot[:].rearrange("p t e -> p (t e)"), start=True, stop=True).then_inc(sums, 1)

            @block.gpsimd
            def _(gp):
                gp.wait_ge(slots_done, 1)
                for t in range(NT):
                    nc.gpsimd.indirect_dma_start(
                        out=g.sorted_h, out_offset=bass.IndirectOffsetOnAxis(ap=g.slots[:, t:t + 1], axis=0),
                        in_=g.h2[:, t, :], in_offset=None).then_inc(scattered, 16)
                gp.wait_ge(scattered, 16 * NT)


def stage_experts(nc, g):
    with ExitStack() as ctx:
        sb, pb, sem = open_stage(nc, ctx)
        b1s = sb("b1s", [3, E, F], bf16)
        b2s = sb("b2s", [3, E, D], bf16)
        one3 = sb("one3", [3, P], bf16)
        ht = sb("ht", [P, 2, D])
        hT = sb("hT5", [P, 2, KC, P])
        ge = sb("ge", [P, 2, F])
        gT = sb("gT", [P, FC, P])
        ys = sb("ys", [P, 2, D])
        ps_x = pb("ps_x", [P, CH])
        ps_1 = pb("ps_1", [P, 2, CH])
        ps_g = pb("ps_g", [P, 2, CH])
        ps_y = pb("ps_y", [P, CH])
        w_in, set5 = sem("w_in5"), sem("set5")
        h_in = [sem(f"h_in{i}") for i in range(2)]
        x_turned, x_copied, f_done, g_done, g_turned, g_copied, y_done, y_copied = (
            sem("x_turned"), sem("x_copied"), sem("f_done"), sem("g_done"), sem("g_turned"), sem("g_copied"),
            sem("y_done"), sem("y_copied"))
        y_out = [sem(f"y_out{i}") for i in range(2)]

        def pairs(eng, body):
            with eng.Fori(0, SLOTS // 2) as n:
                for u in range(2):
                    body(n, u)
            if SLOTS % 2:
                body(SLOTS // 2, 0)

        with nc.Block() as block:
            @block.sync
            def _(sp):
                sp.dma_start(b1s[:], g.b1_rows.rearrange("s (e n) -> s e n", e=E)).then_inc(w_in, 16)
                sp.dma_start(b2s[:], g.b2_rows.rearrange("s (e n) -> s e n", e=E)).then_inc(w_in, 16)

                def body(n, u):
                    i = n * 2 + u
                    sp.wait_ge(x_turned, i + 1)
                    sp.dma_start(ht[:, u, :],
                                 g.sorted_h[bass.ds((i + 2) * P, P), :]).then_inc(h_in[u], 16)
                    sp.wait_ge(y_copied, i + 2)
                    sp.dma_start(g.sorted_y[bass.ds(i * P, P), :], ys[:, u, :]).then_inc(y_out[u], 16)

                for i in range(2):
                    sp.sem_inc(y_out[i], 1)
                    sp.dma_start(ht[:, i, :], g.sorted_h[i * P:(i + 1) * P, :]).then_inc(h_in[i], 16)
                pairs(sp, body)
                sp.wait_ge(y_out[0], 16 * (SLOTS // 2 + SLOTS % 2) + 1)
                sp.wait_ge(y_out[1], 16 * (SLOTS // 2) + 1)
                sp.wait_ge(h_in[0], 16 * (1 + SLOTS // 2 + SLOTS % 2))
                sp.wait_ge(h_in[1], 16 * (1 + SLOTS // 2))

            @block.gpsimd
            def _(gp):
                nc.gpsimd.memset(one3[:], 1.0).then_inc(set5, 1)

            @block.tensor
            def _(pe):
                def turn_in(n, u):
                    i = n * 2 + u
                    pe.wait_ge(h_in[u], 16 * n + 16)
                    pe.wait_ge(x_copied, i + 1)
                    for k in range(KC):
                        mm = nc.tensor.transpose(ps_x[:, k * P:(k + 1) * P], ht[:, u, k * P:(k + 1) * P],
                                                 g.const[:, C_ID:C_ID + P])
                    mm.then_inc(x_turned, 1)

                def up(n, u, half, e):
                    i = n * 2 + u
                    pe.wait_ge(x_copied, i + 2)
                    pe.wait_ge(g_done, i * 2 + 1)
                    cols = slice(half * CH, (half + 1) * CH)
                    nc.tensor.matmul(ps_1[:, half, :], one3[:], b1s[:, bass.ds(e, 1), cols]
                                     .rearrange("s a n -> s (a n)"), start=True, stop=False)
                    for k in range(KC):
                        mm = nc.tensor.matmul(ps_1[:, half, :], hT[:, u, k, :],
                                              g.w1[:, k, bass.ds(e, 1), cols].rearrange("p a n -> p (a n)"),
                                              start=False, stop=(k == KC - 1))
                    mm.then_inc(f_done, 1)

                def turn_hidden(n, u):
                    i = n * 2 + u
                    for half in range(2):
                        pe.wait_ge(g_done, i * 2 + half + 2)
                        pe.wait_ge(g_copied, i * 2 + 1)
                        for k in range(FC // 2):
                            f = half * FC // 2 + k
                            mm = nc.tensor.transpose(ps_g[:, half, k * P:(k + 1) * P], ge[:, u, f * P:(f + 1) * P],
                                                     g.const[:, C_ID:C_ID + P])
                        mm.then_inc(g_turned, 1)

                def down(n, u, e):
                    i = n * 2 + u
                    pe.wait_ge(y_copied, i + 1)
                    nc.tensor.matmul(ps_y[:, 0:D], one3[:], b2s[:, bass.ds(e, 1), :].rearrange("s a n -> s (a n)"),
                                     start=True, stop=False)
                    for f in range(FC):
                        if f % (FC // 2) == 0:
                            pe.wait_ge(g_copied, i * 2 + f // (FC // 2) + 2)
                        mm = nc.tensor.matmul(ps_y[:, 0:D], gT[:, f, :],
                                              g.w2_s[:, f, bass.ds(e, 1), :].rearrange("p a n -> p (a n)"),
                                              start=False, stop=(f == FC - 1))
                    mm.then_inc(y_done, 1)

                def body(n, u):
                    i = n * 2 + u
                    e = pe.value_load(g.expert[0:1, bass.ds(i, 1)], min_val=0, max_val=E - 1)
                    turn_in(n, u)
                    up(n, u, 0, e)
                    up(n, u, 1, e)
                    turn_hidden(n, u)
                    down(n, u, e)

                pe.sem_inc(y_done, 1)
                pe.wait_ge(set5, 1)
                pe.wait_ge(g.w1_in, 16 * KC)
                pe.wait_ge(w_in, 32)
                pe.wait_ge(g.w2_in, 16 * FC)
                pairs(pe, body)

            @block.scalar
            def _(act):
                def body(n, u):
                    i = n * 2 + u
                    for half in range(2):
                        act.wait_ge(f_done, i * 2 + half + 1)
                        nc.scalar.activation(ge[:, u, half * CH:(half + 1) * CH], ps_1[:, half, :], ACT.Gelu
                                             ).then_inc(g_done, 1)
                    act.wait_ge(y_done, i + 2)
                    act.wait_ge(y_out[u], 16 * n + 1)
                    nc.scalar.copy(ys[:, u, :], ps_y[:, 0:D]).then_inc(y_copied, 1)
                act.sem_inc(g_done, 1)
                act.sem_inc(y_copied, 1)
                pairs(act, body)

            @block.vector
            def _(v):
                def body(n, u):
                    i = n * 2 + u
                    v.wait_ge(x_turned, i + 1)
                    nc.vector.tensor_copy(hT[:, u, :, :], ps_x[:, 0:D].rearrange("p (k t) -> p k t", k=KC)
                                          ).then_inc(x_copied, 1)
                    for half in range(2):
                        v.wait_ge(g_turned, i * 2 + half + 1)
                        v.wait_ge(y_done, i + 1)
                        nc.vector.tensor_copy(gT[:, half * FC // 2:(half + 1) * FC // 2, :],
                                              ps_g[:, half, :].rearrange("p (k t) -> p k t", t=P)
                                              ).then_inc(g_copied, 1)
                v.sem_inc(x_copied, 1)
                v.sem_inc(g_copied, 1)
                pairs(v, body)


def stage_finish(nc, g):
    with ExitStack() as ctx:
        sb, pb, sem = open_stage(nc, ctx)
        RING = 4
        x1 = sb("x6", [P, RING, D])
        y = sb("y6", [P, RING, D])
        yg = sb("yg", [P, RING, D])
        o = sb("o6", [P, RING, D])
        x_in = [sem(f"x_in6{i}") for i in range(RING)]
        y_in = [sem(f"y_in6{i}") for i in range(RING)]
        gated, summed = sem("gated6"), sem("summed6")
        o_out = [sem(f"o_out6{i}") for i in range(RING)]
        with nc.Block() as block:
            @block.sync
            def _(sp):
                for t in range(RING):
                    sp.dma_start(x1[:, t, :], g.x1_rows[t * P:(t + 1) * P, :]).then_inc(x_in[t], 16)
                for t in range(NT):
                    r = t % RING
                    sp.wait_ge(summed, t + 1)
                    sp.dma_start(g.out.rearrange("b s d -> (b s) d")[t * P:(t + 1) * P, :], o[:, r, :]
                                 ).then_inc(o_out[r], 16)
                    if t + RING < NT:
                        sp.dma_start(x1[:, r, :], g.x1_rows[(t + RING) * P:(t + RING + 1) * P, :]).then_inc(x_in[r], 16)
                for r in range(RING):
                    sp.wait_ge(o_out[r], 16 * NT // RING)

            @block.gpsimd
            def _(gp):
                for t in range(NT):
                    r = t % RING
                    if t >= RING:
                        gp.wait_ge(gated, t - RING + 1)
                    nc.gpsimd.indirect_dma_start(
                        out=y[:, r, :], out_offset=None, in_=g.sorted_y,
                        in_offset=bass.IndirectOffsetOnAxis(ap=g.slots[:, t:t + 1], axis=0)).then_inc(y_in[r], 16)

            @block.vector
            def _(v):
                for t in range(NT):
                    r = t % RING
                    v.wait_ge(y_in[r], 16 * (t // RING + 1))
                    nc.vector.tensor_tensor(yg[:, r, :], y[:, r, :], g.mod[:, t // (NT // B), 3, :], ALU.mult
                                            ).then_inc(gated, 1)
                    v.wait_ge(gated, t + 1)
                    v.wait_ge(x_in[r], 16 * (t // RING + 1))
                    if t >= RING:
                        v.wait_ge(o_out[r], 16 * (t // RING))
                    nc.vector.tensor_tensor(o[:, r, :], yg[:, r, :], x1[:, r, :], ALU.add).then_inc(summed, 1)


def build(nc, g, stages=(0, 1, 2, 3, 4, 5, 6)):
    def dram(name, shape, dt):
        return nc.dram_tensor(name, shape, dt, kind="Internal").ap()

    g.qk_rows = dram("qk_rows", (NIT, 2, 3, G * HD, S), bf16)
    g.v_rows = dram("v_rows", (NIT, S, P), fp32)
    g.pos_rows = dram("pos_rows", (NIT, G, 3, S), bf16)
    g.att_rows = dram("att_rows", (NIT, P, S // P, G * HD), fp32)
    g.b1_rows = dram("b1_rows", (3, E * F), bf16)
    g.b2_rows = dram("b2_rows", (3, E * D), bf16)
    g.x1_rows = dram("x1_rows", (NTOK, D), fp32)
    g.sorted_h = dram("sorted_h", ((SLOTS + 2) * P, D), fp32)
    g.sorted_y = dram("sorted_y", (SLOTS * P, D), fp32)
    with ExitStack() as ctx:
        sb, pb, sem = open_stage(nc, ctx)
        g.const = sb("const", [P, C_END])
        g.ident_b = sb("ident_b", [P, P], bf16)
        g.mask_q = sb("mask_q", [P, P], bf16)
        g.mask_k = sb("mask_k", [P, P], bf16)
        g.shift = sb("shift", [P, KC, B])
        g.gain = sb("gain", [P, KC, B])
        g.mod = sb("mod", [P, B, 4, D])
        g.logits = sb("logits", [P, NT, E])
        g.slots = sb("slots", [P, NT], i32)
        g.expert = sb("expert", [P, SLOTS + 1], i32)
        with ExitStack() as early:
            g.wqkv = early.enter_context(nc.sbuf_tensor("wqkv", [P, KC, 3 * D], fp32))
            if 0 in stages: stage_setup(nc, g)
            if 1 in stages: stage_qkv(nc, g)
        g.w1 = sb("w1", [P, KC, E, F])
        g.w1_in = sem("w1_in")
        if 2 in stages: stage_attention(nc, g)
        g.w2_s = sb("w2_s", [P, FC, E, D])
        g.w2_in = sem("w2_in")
        with ExitStack() as mid:
            g.h2 = mid.enter_context(nc.sbuf_tensor("h2", [P, NT, D], fp32))
            if 3 in stages: stage_mix(nc, g)
            if 4 in stages: stage_route(nc, g)
        if 5 in stages: stage_experts(nc, g)
        if 6 in stages: stage_finish(nc, g)


def constants():
    c = np.zeros((P, C_END), np.float32)
    i, j = np.arange(P)[:, None], np.arange(P)[None, :]
    c[:, C_ID:C_ID + P] = i == j
    c[:, C_MQ:C_MQ + P] = np.where(j > i, -1e30, 0.0)
    c[:, C_MK:C_MK + P] = np.where(j < i, -1e30, 0.0)
    c[:, C_TRI:C_TRI + P] = i < j
    c[:, C_RANK:C_RANK + E] = E - np.arange(E)
    c[:, C_THR:C_THR + NT] = P * np.arange(NT)
    c[:, C_TILE:C_END] = np.arange(SLOTS + 1)
    start = 2.0 ** (-2.0 ** -(np.log2(H) - 3))
    slopes = np.array([start * start ** i for i in range(H)], np.float32)
    alibi = -slopes[:, None] * np.arange(S, dtype=np.float32)[None, :]
    return c, alibi.astype(np.float32)


def laid_out(inputs):
    a = {k: np.ascontiguousarray(np.asarray(v)) for k, v in inputs.items()}
    const, alibi = constants()
    return {
        "x": a["L0_attn_x"],
        "wqkvT": np.ascontiguousarray(a["L0_attn_W_qkv"].T),
        "woT": np.ascontiguousarray(a["L0_attn_W_o"].T),
        "wg": a["L0_ffn_Wg"], "bg": a["L0_ffn_bg"],
        "w1_dram": a["L0_ffn_W1"], "b1": a["L0_ffn_b1"], "w2": a["L0_ffn_W2"], "b2": a["L0_ffn_b2"],
        "cT": np.ascontiguousarray(a["L0_c"].T.reshape(KC, P, B).transpose(1, 0, 2)),
        "wmod": a["L0_wmod"],
        "const_dram": const, "alibi": alibi,
    }


def kernel(**inputs):
    import concourse.bacc as _bacc
    from concourse.bass_utils import run_bass_kernel_spmd as _run

    nc = _bacc.Bacc("TRN2", target_bir_lowering=False, num_devices=1)
    g, arrays = Tensors(), {}
    for name, a in laid_out(inputs).items():
        arrays["in_" + name] = a
        g.__dict__[name] = nc.dram_tensor("in_" + name, a.shape, mybir.dt.from_np(a.dtype), kind="ExternalInput").ap()
    g.out = nc.dram_tensor("out_0", (B, S, D), fp32, kind="ExternalOutput").ap()
    build(nc, g)
    r = _run(nc, [arrays], core_ids=[0])
    return r.results[0]["out_0"]
```

```python
import concourse.bass as bass
from concourse import mybir
from contextlib import ExitStack
import numpy as np

fp32 = mybir.dt.float32
bf16 = mybir.dt.bfloat16
i32 = mybir.dt.int32
ALU = mybir.AluOpType
ACT = mybir.ActivationFunctionType
AX = mybir.AxisListType

P = 128
B, S, D, H = 2, 2048, 256, 16
HD = D // H
KC = D // P
NTOK = B * S
CH = 512
TPC = CH // P
NCH = NTOK // CH
CPB = S // CH
NT = NTOK // P
G = 4
NG = H // G
HW = 32
NIT = B * NG
E, F = 8, 1024
FC = F // P
SLOTS = NT + E - 1
ROW = D + 1
REGION = NTOK + P
FILL = E * REGION
EPS = 1e-5
SCALE = HD ** -0.5
NF = 4
NU = NCH * NF
NPARTS = 5
LOADS = 15
Q_PART = [0, 0, 1, 0, 1, 2]
K_PART = [0, 1, 0, 2, 1, 0]
R_POS = 6 * HD
R_MAX = R_POS + 3
R_ALL = R_MAX + 3
PIECE = 1024
LAG = 0.55
SLACK = 0.04
ROWS_AFTER, NORM_AFTER = 5, 6
CUT = 4

C_ID, C_MQ, C_MK, C_TRI, C_SMALL = 0, P, 2 * P, 3 * P, 4 * P
C_RANK, C_THR, C_TOKEN = C_SMALL, C_SMALL + E, C_SMALL + E + NT
C_REGION = C_TOKEN + NT
C_TILE = C_REGION + E
C_END = C_TILE + SLOTS + 2


class Tensors:
    pass


def max_pieces():
    out = []
    for c in range(CPB):
        for t in range(TPC):
            n = (c * TPC + t + 1) * P
            whole, rest = divmod(n, PIECE)
            for i in range(whole):
                out += [(c, t, j, 1, i, i * PIECE, (i + 1) * PIECE, not rest and i == whole - 1) for j in range(G)]
            if rest:
                h = min(G, max(1, PIECE // seat(rest)))
                out += [(c, t, j, h, whole, whole * PIECE, n, True) for j in range(0, G, h)]
    return out


def seat(n):
    return n if n <= CH // 2 or n > CH else CH


def products(k):
    c, t, j0, nh, i, k0, k1, last = PIECES[k]
    return [(j, (j - j0) * seat(k1 - k0) - k0, a, min(a + CH, k1), last and min(a + CH, k1) == k1)
            for j in range(j0, j0 + nh) for a in range(k0, k1, CH)]


PIECES = max_pieces()
NP = len(PIECES)
STEPS = [(c, kb) for c in range(CPB) for kb in range(TPC * (c + 1))]
NS = len(STEPS)
CHUNK_END = [max(k for k, p in enumerate(PIECES) if p[0] == c) for c in range(CPB)]


def step_cols(c, kb):
    return max(0, kb - c * TPC) * P


def step_units(s):
    n = CH - step_cols(*STEPS[s])
    h = CH // n if n <= CH // 2 else 1
    return [range(j, j + h) for j in range(0, G, h)]


UNITS = [sum(len(step_units(s)) for s in range(n)) for n in range(NS + 1)]


def before_lag():
    cols = np.cumsum([p[3] * (p[6] - p[5]) for p in PIECES])
    return int(np.searchsorted(cols, LAG * cols[-1]))


def round_order():
    hop = 190
    first = before_lag()
    ones = [(k // NP, k % NP, i) for k in range(first, first + NP) for i in range(len(products(k % NP)))]
    cost1 = [(z - a + P * d) / 2.4 for _, k, i in ones for _, _, a, z, d in [products(k)[i]]]
    width = [CH - step_cols(*x) for x in STEPS]
    units = [(s, i) for s in range(NS) for i in range(len(step_units(s)))]
    unit_cost = [len(step_units(s)[i]) * (width[s] + P * (width[s] < CH or STEPS[s][1] % TPC == 0 and
                 STEPS[s][1] == STEPS[s][0] * TPC)) / 2.4 for s, i in units]
    exp_cost = [51 + len(step_units(s)[i]) * width[s] / 1.2 for s, i in units]
    value_cost = [width[v - 1] * 4 / 2.4 + 60 for v in range(NS)]
    all1, all2 = sum(cost1), sum(unit_cost) + sum(value_cost)
    pe = act = dve = 0.0
    exps, reads, sums = [0.0, 0.0], [0.0, 0.0], [0.0, 0.0]
    step_end = [0.0] * (NS + 1)
    for _ in range(2):
        out, i1, i2, v, done1, done2 = [], 0, 0, 0, 0.0, 0.0
        step_end[0] = step_end[NS]
        while i1 < len(ones) or i2 < len(units) or v < NS:
            ahead = done1 / all1 - done2 / all2
            choices = []
            if i2 < len(units) and units[i2][0] <= v:
                choices.append((max(pe, exps[-2]), 0, "unit"))
            if v < NS and (i2 == len(units) or units[i2] > (v, 0)):
                choices.append((max(pe, step_end[v]), 2, "values"))
            if i1 < len(ones) and (ahead < SLACK or not choices):
                choices.append((max(pe, reads[-2]) if ones[i1][2] == 0 else pe, 1 if ahead < 0 else 3, "max"))
                if ahead < -SLACK:
                    choices = choices[-1:]
            start, _, what = min(choices)
            if what == "unit":
                s, i = units[i2]
                pe = start + unit_cost[i2]
                act = max(act, pe + hop, sums[-2] + hop) + exp_cost[i2]
                exps.append(act + hop)
                step_end[s + 1] = act + hop
                done2 += unit_cost[i2]
                i2 += 1
                out.append(("unit", 0, s, i))
            elif what == "values":
                pe = start + value_cost[v]
                sums.append(pe)
                done2 += value_cost[v]
                out.append(("values", 0 if v else -1, (v - 1) % NS))
                v += 1
            else:
                r, k, i = ones[i1]
                pe = start + cost1[i1]
                done1 += cost1[i1]
                i1 += 1
                if i == len(products(k)) - 1:
                    dve = max(dve, pe + hop) + 65 + PIECES[k][3] * (PIECES[k][6] - PIECES[k][5]) / 0.96
                    reads.append(dve + hop)
                    out.append(("max", r, k))
                else:
                    out.append(("part", r, k, i))
    return out


def whole_plan():
    core = [("part" if i < len(products(k)) - 1 else "max", 0, k, i)[:4 if i < len(products(k)) - 1 else 3]
            for k in range(before_lag()) for i in range(len(products(k)))]
    order = round_order()
    for r in range(NIT):
        core += [(x[0], x[1] + r, *x[2:]) for x in order if 0 <= x[1] + r < NIT]
    core.append(("values", NIT - 1, NS - 1))
    out, late, units, maxima = [], [], 0, 0
    for x in core:
        out.append(x)
        kind, r, a = x[:3]
        units += kind == "unit"
        maxima += kind == "max"
        if kind == "max" and a in CHUNK_END:
            late.append((units + ROWS_AFTER, maxima + 2, ("rows", r, CHUNK_END.index(a))))
        if kind == "values":
            c, kb = STEPS[a]
            if kb == TPC * (c + 1) - 1:
                late.append((units + 1, 0, ("take", r, c)))
                late.append((units + NORM_AFTER, 0, ("norm", r, c)))
            if a == NS - 1 and r + 2 < NIT:
                out.append(("load", r + 2))
        for y in [y for y in late if y[0] <= units or y[1] and units == 0 and y[1] <= maxima]:
            late.remove(y)
            out.append(y[2])
    return out + [y[2] for y in late]


def plan():
    items = whole_plan()
    cuts = [items.index(("unit", r, CUT, 0)) for r in range(NIT)] + [len(items)]
    parts = [[(x[0], x[1] - r, *x[2:]) for x in items[cuts[r]:cuts[r + 1]]] for r in range(NIT)]
    assert all(p == parts[0] for p in parts[:NIT - 2])
    return items[:cuts[0]], parts[0], parts[NIT - 2], parts[NIT - 1]


def open_stage(nc, ctx):
    def sb(name, shape, dt=fp32):
        return ctx.enter_context(nc.sbuf_tensor(name, shape, dt))

    def pb(name, shape, dt=fp32):
        return ctx.enter_context(nc.psum_tensor(name, shape, dt))

    def sem(name):
        return ctx.enter_context(nc.semaphore(name))

    return sb, pb, sem


def load_round(sp, g, r, u, first=0, end=LOADS):
    src = g.qk_rows[bass.ds(r, 1)].rearrange("a w s (j d) t -> (a w) s d j t", d=HD)
    pos = g.pos_rows[bass.ds(r, 1)].rearrange("a s (j t) -> s (a j) t", j=G)
    val = g.v_rows[bass.ds(r, 1)].rearrange("a (n p) c -> p (a n) c", p=P)
    transfers = [(g.kh[u][k * HD:(k + 1) * HD, :, :], src[1, K_PART[k]]) for k in range(6)]
    transfers += [(g.qh[u][k * HD:(k + 1) * HD, :, :], src[0, Q_PART[k]]) for k in range(6)]
    transfers += [(g.kh[u][R_POS:R_MAX, :, :], pos)]
    transfers += [(g.vh[u][z, :, :], val[z]) for z in (slice(0, P // 2), slice(P // 2, P))]
    assert len(transfers) == LOADS
    for out, in_ in transfers[first:end]:
        sp.dma_start(out, in_).then_inc(g.loaded[u], 16)


def load_ones(sp, g, u):
    one_v = g.one_rows.rearrange("s (j t) -> s j t", j=G)
    sp.dma_start(g.kh[u][R_MAX:R_ALL, :, :], one_v).then_inc(g.ones_in[u], 16)
    sp.dma_start(g.qh[u][R_POS:R_MAX, :, :], one_v).then_inc(g.ones_in[u], 16)


def stage_qkv(nc, g):
    with ExitStack() as ctx:
        sb, pb, sem = open_stage(nc, ctx)
        NQ, NREST = 4, 3
        parts, vp, parts_out, v_out = g.parts, g.vp, g.parts_out, g.v_out
        wqkv = sb("wqkv", [P, KC, 3 * D])
        wmod = sb("wmod", [P, KC, 6 * D])
        cT = sb("cT", [P, KC, B])
        ex, e1, rc, sc = (sb(n, [P, KC, B]) for n in ("ex", "e1", "rc", "sc"))
        shift = sb("shift", [P, KC, B])
        gain = sb("gain", [P, KC, B])
        mod, sgn, mag = sb("modr", [B, 4, D]), sb("sgn", [B, 2, D]), sb("mag", [B, 2, D])
        NA = H * S // P
        al, alr, alp = sb("al", [P, NA]), sb("alr", [P, NA]), sb("alp", [P, 3, NA], bf16)
        nb1, nb = E * F // P, (E * F + E * D) // P
        bb, bbr, bbp = sb("bb", [P, nb]), sb("bbr", [P, nb]), sb("bbp", [P, 3, nb], bf16)
        one = sb("one", [3 * G * S // NA, NA], bf16)
        xt = sb("xt", [P, 2, TPC, D])
        st = sb("st", [P, TPC, 6])
        mv = sb("mv", [P, TPC, 2])
        ve, sd, rs = sb("ve", [P, TPC]), sb("sd", [P, TPC]), sb("rs", [P, TPC])
        xn = sb("xn", [P, TPC, D])
        hT = sb("hT", [P, 2, KC, CH])
        rest = sb("rest", [P, NREST, CH])
        ps_t = pb("ps_t", [P, KC, CH])
        ps_q = pb("ps_q", [P, NQ, CH])
        ps_v = pb("ps_v", [P, 2, 2, D])
        ps_col = ps_q[:, 0, 0:8 * B].rearrange("p (n b) -> p n b", b=B)
        ps_row = ps_v[0:B].rearrange("b n i d -> b (n i) d")
        c_in, const_in, wcol_in, wrow_in, al_in, bb_in, wqkv_in = (
            sem("c_in"), sem("const_in"), sem("wcol_in"), sem("wrow_in"), sem("al_in"), sem("bb_in"), sem("wqkv_in"))
        exp_done, silu_done, cols_done, cols_read, rows_done, rows_read, mod_set = (
            sem("exp_done"), sem("silu_done"), sem("cols_done"), sem("cols_read"), sem("rows_done"),
            sem("rows_read"), sem("mod_set"))
        split, tables_out = sem("split"), sem("tables_out")
        x_in = [sem(f"x_in{i}") for i in range(2)]
        dve, normed, turned, moded = sem("dve_chain1"), sem("normed"), sem("turned"), sem("moded")
        qk_done, part1, part2, rest_done, part3 = (
            sem("qk_done"), sem("part1"), sem("part2"), sem("rest_done"), sem("part3"))
        v_done, v_set, vp_set, var_done, sd_done = (
            sem("v_done"), sem("v_set"), sem("vp_set"), sem("var_done"), sem("sd_done"))
        x_v = g.x.rearrange("b (n t p) d -> (b n) p t d", p=P, t=TPC)
        v_v = g.v_rows.rearrange("(b g) (n p) c -> b n p g c", b=B, p=P)
        TABLES = NIT + 4

        with nc.Block() as block:
            @block.sync
            def _(sp):
                wmod_v = g.wmod.rearrange("(k p) n -> p k n", p=P)
                sp.dma_start(cT[:], g.cT).then_inc(c_in, 16)
                sp.dma_start(xt[:, 0, :, :], x_v[0]).then_inc(x_in[0], 16)
                sp.dma_start(wmod[:, :, 0:2 * D], wmod_v[:, :, 0:2 * D]).then_inc(wcol_in, 16)
                sp.dma_start(g.const[:], g.const_dram).then_inc(const_in, 16)
                sp.dma_start(wqkv[:], g.wqkvT.rearrange("(k p) n -> p k n", p=P)).then_inc(wqkv_in, 16)
                sp.dma_start(al[:], g.alibi.rearrange("h (a n) -> (h a) n", n=NA)).then_inc(al_in, 16)
                sp.dma_start(wmod[:, :, 2 * D:], wmod_v[:, :, 2 * D:]).then_inc(wrow_in, 16)
                sp.dma_start(xt[:, 1, :, :], x_v[1]).then_inc(x_in[1], 16)
                sp.dma_start(bb[:, 0:nb1], g.b1.rearrange("e (a n) -> (e a) n", n=nb1)).then_inc(bb_in, 16)
                sp.dma_start(bb[:, nb1:], g.b2.rearrange("e (a n) -> (e a) n", n=E * D // P)).then_inc(bb_in, 16)

                def tables():
                    sp.wait_ge(split, 11)
                    sp.dma_start(g.one_rows.rearrange("s (a n) -> (s a) n", n=NA), one[:]
                                 ).then_inc(tables_out, 16)
                    for r in range(NIT):
                        h = r % NG * (P // NG)
                        sp.dma_start(g.pos_rows[r].rearrange("s (a n) -> a s n", n=NA), alp[h:h + P // NG]
                                     ).then_inc(tables_out, 16)
                    sp.dma_start(g.b1_rows.rearrange("s (p n) -> p s n", p=P), bbp[:, :, 0:nb1]
                                 ).then_inc(tables_out, 16)
                    sp.dma_start(g.b2_rows.rearrange("s (p n) -> p s n", p=P), bbp[:, :, nb1:]
                                 ).then_inc(tables_out, 16)
                    sp.wait_ge(mod_set, 1)
                    sp.dma_start(g.mod_rows, mod[:]).then_inc(tables_out, 16)

                for n in range(NCH):
                    b, c = n // CPB, n % CPB
                    if n + 2 < NCH:
                        sp.wait_ge(normed, n + 1)
                        sp.dma_start(xt[:, n % 2, :, :], x_v[n + 2]).then_inc(x_in[n % 2], 16)
                    for f in range(NF):
                        u = n * NF + f
                        sp.wait_ge(part3, u + 1)
                        for half in range(2):
                            sp.dma_start(
                                g.qk_rows[b * NG + (f % 2) * 2 + half, f // 2, :, :, c * CH:(c + 1) * CH]
                                .rearrange("s r t -> r s t"),
                                parts[half * 64:(half + 1) * 64, u % NPARTS, :, :]).then_inc(parts_out[u % NPARTS], 16)
                    for w in range(2):
                        u = n * 2 + w
                        sp.wait_ge(v_set, u + 1)
                        for i in range(2):
                            tile = c * TPC + 2 * w + i
                            sp.dma_start(v_v[b, tile], vp[:, u % 2, i, :, :].rearrange("p (g j) c -> p g (j c)", g=NG)
                                         ).then_inc(v_out[u % 2], 16)
                    if n == 0:
                        tables()
                    if n == CPB - 1:
                        for i in range(NPARTS):
                            sp.wait_ge(parts_out[i], 32 * len(range(i, CPB * NF, NPARTS)))
                        for i in range(2):
                            sp.wait_ge(v_out[i], 32 * CPB)
                        sp.wait_ge(tables_out, 16 * TABLES)
                        load_ones(sp, g, 0)
                    if CPB <= n < NCH - 1:
                        third = LOADS // 3
                        load_round(sp, g, 0, 0, (n - CPB) * third, (n - CPB + 1) * third)

            @block.vector
            def _(v):
                def link(ins):
                    link.n += 1
                    ins.then_inc(dve, 1)
                    v.wait_ge(dve, link.n)
                link.n = 0

                def norm(n):
                    v.wait_ge(x_in[n % 2], 16 * (n // 2 + 1))
                    for t in range(TPC):
                        last = nc.vector.bn_stats(st[:, t, :], xt[:, n % 2, t, :])
                    link(last)
                    for t in range(TPC):
                        last = nc.vector.bn_aggr(mv[:, t, :], st[:, t, :])
                    link(last)
                    nc.vector.tensor_scalar(ve[:], mv[:, :, 1], EPS, None, ALU.add).then_inc(var_done, 1)
                    v.wait_ge(sd_done, n + 1)
                    link(nc.vector.reciprocal(rs[:], sd[:]))
                    if n:
                        v.wait_ge(turned, n)
                    for t in range(TPC):
                        last = nc.vector.tensor_scalar(xn[:, t, :], xt[:, n % 2, t, :], mv[:, t, 0:1],
                                                       rs[:, t:t + 1], ALU.subtract, ALU.mult)
                    last.then_inc(normed, 1)
                    v.wait_ge(normed, n + 1)

                v.wait_ge(exp_done, 1)
                link(nc.vector.tensor_scalar(e1[:], ex[:], 1.0, None, ALU.add))
                link(nc.vector.reciprocal(rc[:], e1[:]))
                nc.vector.tensor_tensor(sc[:], rc[:], cT[:], ALU.mult).then_inc(silu_done, 1)
                v.wait_ge(const_in, 16)
                nc.vector.tensor_copy(g.ident_b[:], g.const[:, C_ID:C_ID + P])
                nc.vector.tensor_copy(g.mask_q[:], g.const[:, C_MQ:C_MQ + P])
                link(nc.vector.tensor_copy(g.mask_k[:], g.const[:, C_MK:C_MK + P]))
                norm(0)
                v.wait_ge(cols_done, 1)
                nc.vector.tensor_copy(shift[:], ps_col[:, 0:KC, :])
                nc.vector.tensor_scalar(gain[:], ps_col[:, KC:2 * KC, :], 1.0, None, ALU.add).then_inc(cols_read, 1)
                v.wait_ge(rows_done, 1)
                nc.vector.tensor_copy(mod[:], ps_row).then_inc(rows_read, 1)
                v.wait_ge(rows_read, 1)
                nc.vector.tensor_scalar(mod[:, 2, :], mod[:, 2, :], 1.0, None, ALU.add)
                for i, row in ((0, 0), (1, 3)):
                    nc.vector.tensor_scalar(sgn[:, i, :], mod[:, row, :], 0.0, 2.0, ALU.is_ge, ALU.mult)
                    last = nc.vector.scalar_tensor_tensor(mag[:, i, :], mod[:, row, :], -1.0, mod[:, row, :],
                                                          ALU.mult, ALU.max)
                link(last)
                link(nc.vector.tensor_scalar(mag[:], mag[:], 0.25, None, ALU.max))
                for i, row in ((0, 0), (1, 3)):
                    last = nc.vector.scalar_tensor_tensor(mod[:, row, :], sgn[:, i, :], 1.0, mag[:, i, :],
                                                          ALU.subtract, ALU.mult)
                last.then_inc(mod_set, 1)
                v.wait_ge(vp_set, 4)
                for n in range(NCH):
                    for f in range(NF):
                        u = n * NF + f
                        v.wait_ge(part1, u + 1)
                        if u >= NREST:
                            v.wait_ge(part3, u - NREST + 1)
                        nc.vector.scalar_tensor_tensor(rest[:, u % NREST, :], ps_q[:, u % NQ, :],
                                                       SCALE if f < 2 else 1.0, parts[:, u % NPARTS, 0, :],
                                                       ALU.mult, ALU.subtract).then_inc(rest_done, 1)
                        if f == 0 and n + 1 < NCH:
                            norm(n + 1)
                    for w in range(2):
                        u = n * 2 + w
                        v.wait_ge(v_done, u + 1)
                        if u >= 2:
                            v.wait_ge(v_out[u % 2], 32 * (u // 2))
                        for i in range(2):
                            last = nc.vector.tensor_copy(vp[:, u % 2, i, :, 0:HD],
                                                         ps_v[:, u % 2, i, :].rearrange("p (h c) -> p h c", c=HD))
                        last.then_inc(v_set, 1)

            @block.scalar
            def _(act):
                def modulate(n):
                    act.wait_ge(turned, n + 1)
                    if n >= 2:
                        act.wait_ge(v_done, 2 * (n - 1))
                    for k in range(KC):
                        last = nc.scalar.activation(hT[:, n % 2, k, :], ps_t[:, k, :], ACT.Identity,
                                                    bias=shift[:, k, n // CPB:n // CPB + 1],
                                                    scale=gain[:, k, n // CPB:n // CPB + 1])
                    last.then_inc(moded, 1)

                def second_part(u):
                    act.wait_ge(rest_done, u + 1)
                    nc.scalar.copy(parts[:, u % NPARTS, 1, :], rest[:, u % NREST, :]).then_inc(part2, 1)

                def deviation(n):
                    act.wait_ge(var_done, n + 1)
                    nc.scalar.activation(sd[:], ve[:], ACT.Sqrt).then_inc(sd_done, 1)

                act.wait_ge(c_in, 16)
                nc.scalar.activation(ex[:], cT[:], ACT.Exp, scale=-1.0).then_inc(exp_done, 1)
                deviation(0)
                act.wait_ge(cols_read, 1)
                modulate(0)
                for n in range(NCH):
                    for f in range(NF):
                        u = n * NF + f
                        if f == 1 and n + 1 < NCH:
                            deviation(n + 1)
                        act.wait_ge(qk_done, u + 1)
                        if u >= NPARTS:
                            act.wait_ge(parts_out[u % NPARTS], 32 * (u // NPARTS))
                        nc.scalar.activation(parts[:, u % NPARTS, 0, :], ps_q[:, u % NQ, :], ACT.Copy,
                                             scale=SCALE if f < 2 else 1.0).then_inc(part1, 1)
                        if u:
                            second_part(u - 1)
                    if n + 1 < NCH:
                        modulate(n + 1)
                second_part(NU - 1)

            @block.gpsimd
            def _(gp):
                def link(ins):
                    link.n += 1
                    ins.then_inc(split, 1)
                    gp.wait_ge(split, link.n)
                link.n = 0
                for i in range(2):
                    nc.gpsimd.memset(vp[:, i, :, :, HD:HW], 0.0).then_inc(vp_set, 1)
                gp.wait_ge(vp_set, 2)
                for i in range(2):
                    nc.gpsimd.memset(vp[:, i, :, :, HD:HD + 1], 1.0).then_inc(vp_set, 1)
                link(nc.gpsimd.memset(one[:], 1.0))
                for src, left, pieces, ready in ((al, alr, alp, al_in), (bb, bbr, bbp, bb_in)):
                    gp.wait_ge(ready, 16 if src is al else 32)
                    link(nc.gpsimd.tensor_copy(pieces[:, 0, :], src[:]))
                    link(nc.gpsimd.tensor_tensor(left[:], src[:], pieces[:, 0, :], ALU.subtract))
                    link(nc.gpsimd.tensor_copy(pieces[:, 1, :], left[:]))
                    link(nc.gpsimd.tensor_tensor(left[:], left[:], pieces[:, 1, :], ALU.subtract))
                    link(nc.gpsimd.tensor_copy(pieces[:, 2, :], left[:]))
                for u in range(NU):
                    gp.wait_ge(part2, u + 1)
                    nc.gpsimd.tensor_tensor(parts[:, u % NPARTS, 2, :], rest[:, u % NREST, :],
                                            parts[:, u % NPARTS, 1, :], ALU.subtract).then_inc(part3, 1)

            @block.tensor
            def _(pe):
                def turn(n):
                    pe.wait_ge(normed, n + 1)
                    if n:
                        pe.wait_ge(moded, n)
                    for k in range(KC):
                        for t in range(TPC):
                            last = nc.tensor.transpose(ps_t[:, k, t * P:(t + 1) * P],
                                                       xn[:, t, k * P:(k + 1) * P], g.const[:, C_ID:C_ID + P])
                    last.then_inc(turned, 1)

                pe.wait_ge(silu_done, 1)
                pe.wait_ge(wcol_in, 16)
                for n in range(2 * KC):
                    for k in range(KC):
                        last = nc.tensor.matmul(ps_col[:, n, :], wmod[:, k, n * P:(n + 1) * P], sc[:, k, :],
                                                start=(k == 0), stop=(k == KC - 1))
                last.then_inc(cols_done, 1)
                turn(0)
                pe.wait_ge(wrow_in, 16)
                for n in range(2):
                    for k in range(KC):
                        last = nc.tensor.matmul(ps_v[0:B, n, :, :].rearrange("b i d -> b (i d)"), sc[:, k, :],
                                                wmod[:, k, 2 * D + n * CH:2 * D + (n + 1) * CH],
                                                start=(k == 0), stop=(k == KC - 1))
                last.then_inc(rows_done, 1)
                pe.wait_ge(wqkv_in, 16)
                for n in range(NCH):
                    pe.wait_ge(moded, n + 1)
                    for f in range(NF):
                        u = n * NF + f
                        if u >= NQ:
                            pe.wait_ge(rest_done, u - NQ + 1)
                        for k in range(KC):
                            last = nc.tensor.matmul(ps_q[:, u % NQ, :], wqkv[:, k, f * P:(f + 1) * P],
                                                    hT[:, n % 2, k, :], start=(k == 0), stop=(k == KC - 1))
                        last.then_inc(qk_done, 1)
                    if n + 1 < NCH:
                        turn(n + 1)
                    if n == 0:
                        pe.wait_ge(rows_read, 1)
                    for w in range(2):
                        u = n * 2 + w
                        if u >= 2:
                            pe.wait_ge(v_set, u - 1)
                        for i in range(2):
                            t = 2 * w + i
                            for k in range(KC):
                                last = nc.tensor.matmul(ps_v[:, u % 2, i, :], hT[:, n % 2, k, t * P:(t + 1) * P],
                                                        wqkv[:, k, 2 * D:3 * D], start=(k == 0), stop=(k == KC - 1))
                        last.then_inc(v_done, 1)


def stage_attention(nc, g):
    with ExitStack() as ctx:
        sb, pb, sem = open_stage(nc, ctx)
        kh, qh, vh, loaded = g.kh, g.qh, g.vh, g.loaded
        pr = sb("pr", [P, 2, G, CH])
        part = sb("part", [P, 2, 2, TPC, G])
        mx = sb("mx", [P, TPC, G])
        ms = sb("ms", [P, TPC, G, 3], bf16)
        none = sb("none", [P, TPC, G])
        mrow = sb("mrow", [G * 3, CH], bf16)
        osb = sb("osb", [P, CH])
        rsum = sb("rsum", [P, TPC, G])
        on = sb("on", [P, 2, TPC, G * HD])
        ps_s = pb("ps_s", [P, 2, PIECE])
        ps_w = pb("ps_w", [P, 2, CH])
        ps_o = pb("ps_o", [P, CH])
        ps_m = pb("ps_m", [P, TPC, P])
        none_set, mx_done = sem("none_set"), sem("mx_done")
        filler_set, filler_out = sem("filler_set"), sem("filler_out")
        s_ready, s_read = sem("s_ready"), sem("s_read")
        w_ready, p_ready, pv_done = sem("w_ready"), sem("p_ready"), sem("pv_done")
        pool, m_turned, m_copied, m_in = sem("pool2"), sem("m_turned"), sem("m_copied"), sem("m_in")
        o_copied, o_turned, r_done, on_ready = sem("o_copied"), sem("o_turned"), sem("r_done"), sem("on_ready")
        o_out = [sem(f"o_out{i}") for i in range(2)]
        MOPS = 5
        before, turn, tail0, tail1 = plan()
        psm_b = ps_m[0:G * 3, 0:TPC // 2, :].rearrange("p t q -> p (t q)").bitcast(bf16)
        sums = ps_m[:].rearrange("p t (j c) -> p t j c", j=G)

        def over(eng, do):
            do(before, 0, 0, True)
            with eng.Fori(0, NIT // 2 - 1) as n:
                for u in range(2):
                    do(turn, n, u, False)
            do(tail0, NIT // 2 - 1, 0, False)
            do(tail1, NIT // 2 - 1, 1, False)

        ROWS0, NORMS0 = (sum(x[0] == kind for x in before) for kind in ("rows", "norm"))

        with nc.Block() as block:
            @block.sync
            def _(sp):
                def do(items, n, u, first):
                    for kind, dr, *a in items:
                        r, ru = n * 2 + u + dr, (u + dr) % 2
                        if kind == "rows":
                            c, = a
                            sp.wait_ge(m_copied, r * CPB + c + 1)
                            for j in range(G):
                                sp.dma_start(qh[ru][R_MAX:R_ALL, j, c * CH:(c + 1) * CH],
                                             mrow[3 * j:3 * j + 3, :]).then_inc(m_in, 16)
                        elif kind == "load":
                            sp.wait_ge(pv_done, (r - 1) * NS + 2)
                            load_round(sp, g, r, ru)
                        elif kind == "norm":
                            c, = a
                            sp.wait_ge(on_ready, r * CPB + c + 2)
                            sp.dma_start(g.att_rows[bass.ds(r, 1), :, c * TPC:(c + 1) * TPC, :]
                                         .rearrange("a p t d -> p (a t) d"), on[:, c % 2, :, :]
                                         ).then_inc(o_out[c % 2], 16)

                for i in range(2):
                    sp.sem_inc(o_out[i], 1)
                load_ones(sp, g, 1)
                load_round(sp, g, 1, 1)
                for i in range(NPARTS):
                    sp.wait_ge(g.parts_out[i], 32 * len(range(i, NU, NPARTS)))
                for i in range(2):
                    sp.wait_ge(g.v_out[i], 32 * NCH)
                sp.dma_start(g.mod[:], g.mod_rows.unsqueeze(0).to_broadcast([P, B, 4, D])).then_inc(g.mix_in, 16)
                sp.dma_start(g.wo_in[:], g.woT.rearrange("(k p) n -> p k n", p=P)).then_inc(g.mix_in, 16)
                sp.dma_start(g.wg_s[:], g.wg.rearrange("(k p) e -> p k e", p=P)).then_inc(g.mix_in, 16)
                sp.dma_start(g.bg_s[:], g.bg.unsqueeze(0).to_broadcast([P, E])).then_inc(g.mix_in, 16)
                for k in range(KC):
                    sp.dma_start(g.w1[:, k, :, :], g.w1_dram[:, k * P:(k + 1) * P, :].rearrange("e p n -> p e n")
                                 ).then_inc(g.w1_in, 16)
                sp.wait_ge(filler_set, 2)
                sp.dma_start(g.sorted_h[FILL:FILL + P, :], g.filler[:]).then_inc(filler_out, 16)
                over(sp, do)
                for i in range(2):
                    sp.wait_ge(o_out[i], 16 * NIT * CPB // 2 + 1)
                sp.wait_ge(filler_out, 16)

            @block.tensor
            def _(pe):
                def maxima(n, u, r, ru, dr, k, i):
                    c, t = PIECES[k][:2]
                    j, at, a, z, diag = products(k)[i]
                    count = r * NP + k
                    if k == 0 and i == 0:
                        pe.wait_ge(loaded[ru], (n + (u + dr) // 2 + 1) * 16 * LOADS)
                        pe.wait_ge(g.ones_in[ru], 16 * 2)
                    if i == 0 and (not isinstance(count, int) or count >= 2):
                        pe.wait_ge(s_read, count - 1)
                    q0 = (c * TPC + t) * P
                    mm = nc.tensor.matmul(ps_s[:, k % 2, at + a:at + z], qh[ru][0:R_MAX, j, q0:q0 + P],
                                          kh[ru][0:R_MAX, j, a:z], start=True, stop=not diag)
                    if diag:
                        mm = nc.tensor.matmul(ps_s[:, k % 2, at + z - P:at + z], g.ident_b[:], g.mask_q[:],
                                              start=False, stop=True)
                    if i == len(products(k)) - 1:
                        mm.then_inc(s_ready, 1)

                def scores(r, ru, s, i):
                    c, kb = STEPS[s]
                    col = step_cols(c, kb)
                    w = CH - col
                    bank = (UNITS[s] + i) % 2
                    heads = step_units(s)[i]
                    pe.wait_ge(p_ready, r * UNITS[NS] + UNITS[s] + i + 1)
                    diag = kb >= c * TPC
                    for j in heads:
                        at = (j - heads[0]) * w
                        mm = nc.tensor.matmul(ps_w[:, bank, at:at + w], kh[ru][0:R_ALL, j, kb * P:(kb + 1) * P],
                                              qh[ru][0:R_ALL, j, c * CH + col:(c + 1) * CH],
                                              start=True, stop=not diag)
                        if diag:
                            mm = nc.tensor.matmul(ps_w[:, bank, at:at + P], g.ident_b[:], g.mask_k[:],
                                                  start=False, stop=True)
                    mm.then_inc(w_ready, 1)

                def values(r, ru, s):
                    c, kb = STEPS[s]
                    col = step_cols(c, kb)
                    q = r * CPB + c
                    if kb == 0 and (not isinstance(q, int) or q >= 1):
                        pe.wait_ge(o_copied, q)
                    pe.wait_ge(p_ready, r * UNITS[NS] + UNITS[s + 1] + 2)
                    for j in range(G):
                        mm = nc.tensor.matmul(ps_o[HW * j:HW * (j + 1), col:CH], vh[ru][:, kb, HW * j:HW * (j + 1)],
                                              pr[:, s % 2, j, col:CH], start=(kb == 0),
                                              stop=(kb == TPC * (c + 1) - 1))
                    mm.then_inc(pv_done, 1)

                def do(items, n, u, first):
                    rows = 0 if first else (n * 2 + u) * CPB + ROWS0
                    norms = 0 if first else (n * 2 + u) * CPB + NORMS0
                    for kind, dr, *a in items:
                        r, ru = n * 2 + u + dr, (u + dr) % 2
                        if kind == "unit":
                            s, i = a
                            c, kb = STEPS[s]
                            if kb == 0 and i == 0:
                                pe.wait_ge(m_in, (r * CPB + c + 1) * 16 * G)
                            scores(r, ru, s, i)
                        elif kind == "values":
                            values(r, ru, a[0])
                        elif kind == "part":
                            maxima(n, u, r, ru, dr, *a)
                        elif kind == "max":
                            maxima(n, u, r, ru, dr, *a, len(products(a[0])) - 1)
                        elif kind == "rows":
                            pe.wait_ge(pool, (r * CPB + a[0] + 1) * MOPS)
                            if not isinstance(rows, int) or rows >= 1:
                                pe.wait_ge(m_copied, rows)
                            pe.wait_ge(on_ready, norms + 1)
                            for t in range(TPC):
                                mm = nc.tensor.transpose(psm_b[:, t * P:(t + 1) * P],
                                                         ms[:, t, :, :].rearrange("p j s -> p (j s)"), g.ident_b[:])
                            mm.then_inc(m_turned, 1)
                            rows = rows + 1
                        elif kind == "norm":
                            pe.wait_ge(o_copied, r * CPB + a[0] + 1)
                            pe.wait_ge(m_copied, rows)
                            pe.wait_ge(on_ready, norms + 1)
                            for t in range(TPC):
                                mm = nc.tensor.transpose(ps_m[:, t, :], osb[:, t * P:(t + 1) * P],
                                                         g.const[:, C_ID:C_ID + P])
                            mm.then_inc(o_turned, 1)
                            norms = norms + 1

                pe.sem_inc(o_turned, 1)
                over(pe, do)

            @block.scalar
            def _(act):
                def weights(r, s, i):
                    col = step_cols(*STEPS[s])
                    w = CH - col
                    heads = step_units(s)[i]
                    j, h = heads[0], len(heads)
                    if i == 0:
                        act.wait_ge(pv_done, r * NS + s + 1)
                    act.wait_ge(w_ready, r * UNITS[NS] + UNITS[s] + i + 1)
                    nc.scalar.activation(pr[:, s % 2, j:j + h, col:CH],
                                         ps_w[:, (UNITS[s] + i) % 2, 0:h * w].rearrange("p (h q) -> p h q", h=h),
                                         ACT.Exp).then_inc(p_ready, 1)

                def do(items, n, u, first):
                    for kind, dr, *a in items:
                        r = n * 2 + u + dr
                        if kind == "unit":
                            weights(r, *a)
                        elif kind == "rows":
                            q = r * CPB + a[0]
                            act.wait_ge(m_turned, q + 1)
                            if not isinstance(q, int) or q >= 1:
                                act.wait_ge(m_in, q * 16 * G)
                            nc.scalar.copy(mrow[:], psm_b).then_inc(m_copied, 1)
                        elif kind == "take":
                            c, = a
                            q = r * CPB + c
                            act.wait_ge(pv_done, r * NS + STEPS.index((c, TPC * (c + 1) - 1)) + 3)
                            act.wait_ge(o_turned, q + 1)
                            nc.scalar.copy(osb[:], ps_o[:]).then_inc(o_copied, 1)

                act.sem_inc(p_ready, 2)
                over(act, do)

            @block.vector
            def _(v):
                def do(items, n, u, first):
                    for kind, dr, *a in items:
                        r = n * 2 + u + dr
                        if kind == "max":
                            k, = a
                            c, t, j, nh, i, k0, k1, last = PIECES[k]
                            w = seat(k1 - k0)
                            v.wait_ge(s_ready, r * NP + k + 1)
                            nc.vector.tensor_reduce(
                                part[:, c % 2, i, t, j:j + nh],
                                ps_s[:, k % 2, 0:nh * w].rearrange("p (h k) -> p h k", h=nh)[:, :, 0:k1 - k0],
                                AX.X, ALU.max).then_inc(s_read, 1)
                            if k in CHUNK_END:
                                q = r * CPB + c
                                v.wait_ge(s_read, r * NP + k + 1)
                                if not isinstance(q, int) or q >= 1:
                                    v.wait_ge(pool, q * MOPS)
                                nc.vector.tensor_reduce(
                                    mx[:], part[:, c % 2, 0:i + 1, :, :].rearrange("p i t j -> p t j i"),
                                    AX.X, ALU.max, negate=True).then_inc(mx_done, 1)
                        elif kind == "norm":
                            c, = a
                            q = r * CPB + c
                            v.wait_ge(o_turned, q + 2)
                            nc.vector.reciprocal(rsum[:], sums[:, :, :, HD]).then_inc(r_done, 1)
                            v.wait_ge(r_done, q + 1)
                            v.wait_ge(o_out[c % 2], (r * (CPB // 2) + c // 2) * 16 + 1)
                            nc.vector.tensor_tensor(on[:, c % 2, :, :].rearrange("p t (j d) -> p t j d", j=G),
                                                    sums[:, :, :, 0:HD],
                                                    rsum[:].unsqueeze(3).to_broadcast([P, TPC, G, HD]),
                                                    ALU.mult).then_inc(on_ready, 1)
                v.sem_inc(on_ready, 1)
                over(v, do)

            @block.gpsimd
            def _(gp):
                def do(items, n, u, first):
                    for kind, dr, *a in items:
                        if kind != "rows":
                            continue
                        q = (n * 2 + u + dr) * CPB + a[0]
                        done = 0
                        gp.wait_ge(mx_done, q + 1)
                        if not isinstance(q, int) or q >= 1:
                            gp.wait_ge(m_turned, q)
                        for i in range(3):
                            nc.gpsimd.tensor_tensor(ms[:, :, :, i], mx[:], none[:], ALU.add).then_inc(pool, 1)
                            done += 1
                            if i < 2:
                                gp.wait_ge(pool, q * MOPS + done)
                                nc.gpsimd.tensor_tensor(mx[:], mx[:], ms[:, :, :, i], ALU.subtract
                                                        ).then_inc(pool, 1)
                                done += 1
                                gp.wait_ge(pool, q * MOPS + done)

                gp.sem_inc(pv_done, 2)
                nc.gpsimd.memset(none[:], 0.0).then_inc(none_set, 1)
                nc.gpsimd.memset(g.filler[:, 0:D], 0.0).then_inc(filler_set, 1)
                nc.gpsimd.memset(g.filler[:, D:ROW], float(NTOK)).then_inc(filler_set, 1)
                gp.wait_ge(none_set, 1)
                over(gp, do)


def stage_mix(nc, g):
    with ExitStack() as ctx:
        sb, pb, sem = open_stage(nc, ctx)
        RING = 4
        NAT, NX = 3, 3
        wo = [sb("wo0", [P, KC, D]), g.wo_in]
        wo_in, wg, bg = g.wo_in, g.wg_s, g.bg_s
        eps = sb("eps3", [P, 1])
        at = sb("at", [P, NAT, TPC, D])
        aT = sb("aT", [P, 2, KC, P])
        x1 = sb("x1", [P, NX, TPC, D])
        st = sb("st3", [P, RING, 6])
        mv = sb("mv3", [P, RING, 2])
        sd, rs = sb("sd3", [P, RING]), sb("rs3", [P, RING])
        hT = sb("hT3", [P, 2, KC, P])
        ps_i = pb("ps_i", [P, 2, CH])
        ps_a = pb("ps_a", [P, 2, CH])
        ps_t = pb("ps_t3", [P, CH])
        ps_l = pb("ps_l", [P, 2, CH])
        ps_c = pb("ps_c", [P, CH])
        before, ones = sb("before", [P, P], bf16), sb("ones3", [P, P], bf16)
        logits, most, key, slot = (sb(n, [P, TPC, E]) for n in ("logits", "most", "key", "slot"))
        hot, hot_b = sb("hot", [P, 2, TPC, E]), sb("hot_b", [P, 2, TPC, E], bf16)
        top, slot_f = sb("top", [P, TPC]), sb("slot_f", [P, TPC])
        counts = ps_c[:, 0:TPC * E].rearrange("p (t e) -> p t e", e=E)
        totals = ps_c[:, TPC * E:(TPC + 1) * E]
        chosen, placed, hot_done, counted, slots_done, scattered = (
            sem("chosen"), sem("placed"), sem("hot_done"), sem("counted"), sem("slots_done"), sem("scattered"))
        at_in = [sem(f"at_in{i}") for i in range(NAT)]
        x_in = [sem(f"x_in3{i}") for i in range(NX)]
        wo_ready, i_turned, i_copied, a_done, x1_ready = (
            sem("wo_ready"), sem("i_turned"), sem("i_copied"), sem("a_done"), sem("x1_ready"))
        st_ready, mv_ready, sd_ready, rs_ready, scaled, h_ready = (
            sem("st_ready"), sem("mv_ready"), sem("sd_ready"), sem("rs_ready"), sem("scaled"), sem("h_ready"))
        rescaled = sem("rescaled")
        turned, h_copied, l_done = sem("turned3"), sem("h_copied"), sem("l_done")
        x1_out = [sem(f"x1_out{i}") for i in range(NX)]
        x_v = g.x.rearrange("b (n t p) d -> (b n) p t d", p=P, t=TPC)
        x1_v = g.x1_rows.rearrange("(n t p) d -> n p t d", p=P, t=TPC)
        MIX, NORM, SCALED, TURN, GATE, SCATTER = 1, 2, 3, 6, 7, 4 * TPC
        W2_IN_MIX = 6
        CHOSEN, PLACED = 6, 4
        COUNT = TPC + GATE + 6

        def at_tile(u):
            return u // TPC, u % TPC

        with nc.Block() as block:
            @block.sync
            def _(sp):
                def load_at(n):
                    b, c = n // CPB, n % CPB
                    for i in range(NG):
                        sp.dma_start(at[:, n % NAT, :, i * G * HD:(i + 1) * G * HD],
                                     g.att_rows[b * NG + i, :, c * TPC:(c + 1) * TPC, :]
                                     ).then_inc(at_in[n % NAT], 16)

                def load_x(n):
                    sp.dma_start(x1[:, n % NX, :, :], x_v[n]).then_inc(x_in[n % NX], 16)

                def load_weights(k):
                    sp.dma_start(g.w2_s[:, k, :, :], g.w2[:, k * P:(k + 1) * P, :].rearrange("e p n -> p e n")
                                 ).then_inc(g.w2_in, 16)

                load_at(0)
                load_x(0)
                for n in range(1, NAT):
                    load_at(n)
                    if n < NX - 1:
                        load_x(n)
                for n in range(NCH):
                    if n + NX - 1 < NCH:
                        if n:
                            sp.wait_ge(x1_out[(n - 1) % NX], 16 * ((n - 1) // NX + 1))
                            sp.wait_ge(scaled, TPC * n)
                        load_x(n + NX - 1)
                    sp.wait_ge(x1_ready, TPC * (n + 1))
                    sp.dma_start(x1_v[n], x1[:, n % NX, :, :]).then_inc(x1_out[n % NX], 16)
                    if n + NAT < NCH:
                        load_at(n + NAT)
                    for k in range(n * W2_IN_MIX // NCH, (n + 1) * W2_IN_MIX // NCH):
                        load_weights(k)
                sp.wait_ge(scattered, 16 * NT)
                for k in range(W2_IN_MIX, FC):
                    load_weights(k)
                for i in range(NX):
                    sp.wait_ge(x1_out[i], 16 * len(range(i, NCH, NX)))

            @block.tensor
            def _(pe):
                def turn_in(u):
                    n, t = at_tile(u)
                    if t == 0:
                        pe.wait_ge(at_in[n % NAT], 16 * NG * (n // NAT + 1))
                    if u >= 2:
                        pe.wait_ge(i_copied, u - 1)
                    for k in range(KC):
                        mm = nc.tensor.transpose(ps_i[:, u % 2, k * P:(k + 1) * P],
                                                 at[:, n % NAT, t, k * P:(k + 1) * P], g.const[:, C_ID:C_ID + P])
                    mm.then_inc(i_turned, 1)

                def mix(u):
                    pe.wait_ge(i_copied, u + 1)
                    if u >= 2:
                        pe.wait_ge(x1_ready, u - 1)
                    for k in range(KC):
                        mm = nc.tensor.matmul(ps_a[:, u % 2, 0:D], aT[:, u % 2, k, :], wo[u // (NT // B)][:, k, :],
                                              start=(k == 0), stop=(k == KC - 1))
                    mm.then_inc(a_done, 1)

                def turn(u):
                    pe.wait_ge(h_ready, u + 1)
                    if u:
                        pe.wait_ge(h_copied, u)
                    for k in range(KC):
                        mm = nc.tensor.transpose(ps_t[:, k * P:(k + 1) * P],
                                                 g.h2[:, u, k * P:(k + 1) * P], g.const[:, C_ID:C_ID + P])
                    mm.then_inc(turned, 1)

                def gate(u):
                    n, t = at_tile(u)
                    pe.wait_ge(h_copied, u + 1)
                    if t == 0 and n >= 2:
                        pe.wait_ge(chosen, (n - 2) * CHOSEN + 1)
                    for k in range(KC):
                        mm = nc.tensor.matmul(ps_l[:, n % 2, t * E:(t + 1) * E], hT[:, u % 2, k, :], wg[:, k, :],
                                              start=(k == 0), stop=(k == KC - 1))
                    mm.then_inc(l_done, 1)

                def count(n):
                    pe.wait_ge(hot_done, n + 1)
                    if n:
                        pe.wait_ge(placed, n * PLACED)
                    nc.tensor.matmul(counts, before[:], hot_b[:, n % 2, :, :], start=True, stop=False)
                    for t in range(1, TPC):
                        nc.tensor.matmul(counts[:, t:, :], ones[:], hot_b[:, n % 2, 0:TPC - t, :],
                                         start=False, stop=(t == TPC - 1))
                    for t in range(TPC):
                        mm = nc.tensor.matmul(totals, ones[:], hot_b[:, n % 2, t, :],
                                              start=(t == 0), stop=(t == TPC - 1))
                    mm.then_inc(counted, 1)

                pe.wait_ge(g.mix_in, 16 * 4)
                pe.wait_ge(wo_ready, 1)
                for u in range(NT - TPC + COUNT + 1):
                    if u < NT:
                        turn_in(u)
                    if 0 <= u - MIX < NT:
                        mix(u - MIX)
                    if 0 <= u - GATE < NT:
                        gate(u - GATE)
                    if 0 <= u - TURN < NT:
                        turn(u - TURN)
                    if u >= COUNT and (u - COUNT) % TPC == 0:
                        count((u - COUNT) // TPC)

            @block.scalar
            def _(act):
                for u in range(NT + TURN):
                    if u < NT:
                        act.wait_ge(i_turned, u + 1)
                        if u >= 2:
                            act.wait_ge(a_done, u - 1)
                        nc.scalar.copy(aT[:, u % 2, :, :], ps_i[:, u % 2, 0:D].rearrange("p (k t) -> p k t", k=KC)
                                       ).then_inc(i_copied, 1)
                    w = u - NORM
                    if 0 <= w < NT:
                        act.wait_ge(mv_ready, w + 1)
                        if w >= RING:
                            act.wait_ge(rs_ready, w - RING + 1)
                        nc.scalar.activation(sd[:, w % RING:w % RING + 1], mv[:, w % RING, 1:2], ACT.Sqrt,
                                             bias=eps[:, 0:1]).then_inc(sd_ready, 1)
                    w = u - SCALED
                    if 0 <= w < NT:
                        act.wait_ge(rs_ready, w + 1)
                        act.wait_ge(scaled, w + 1)
                        nc.scalar.activation(g.h2[:, w, 0:D], g.h2[:, w, 0:D], ACT.Copy,
                                             scale=rs[:, w % RING:w % RING + 1]).then_inc(rescaled, 1)
                    w = u - TURN
                    if 0 <= w < NT:
                        act.wait_ge(turned, w + 1)
                        if w >= 2:
                            act.wait_ge(l_done, w - 1)
                        nc.scalar.copy(hT[:, w % 2, :, :], ps_t[:, 0:D].rearrange("p (k t) -> p k t", k=KC)
                                       ).then_inc(h_copied, 1)

            @block.vector
            def _(v):
                def route(u, place):
                    n, k = divmod((u - TPC - GATE - 1) * 4 + place, 4 * TPC)
                    if k < 7 and 0 <= n < NCH:
                        choose(n, k)
                    if 7 <= k < 12 and 1 <= n <= NCH:
                        put(n - 1, k - 7)

                def choose(n, k):
                    if k:
                        v.wait_ge(chosen, n * CHOSEN + k)
                    rank = g.const[:, C_RANK:C_RANK + E].unsqueeze(1).to_broadcast([P, TPC, E])
                    top_b = top[:].unsqueeze(2).to_broadcast([P, TPC, E])
                    if k == 0:
                        v.wait_ge(l_done, TPC * (n + 1))
                        nc.vector.tensor_tensor(logits[:], ps_l[:, n % 2, 0:TPC * E].rearrange("p (t e) -> p t e", e=E),
                                                bg[:].unsqueeze(1).to_broadcast([P, TPC, E]), ALU.add
                                                ).then_inc(chosen, 1)
                    elif k == 1:
                        nc.vector.tensor_reduce(top[:], logits[:], AX.X, ALU.max).then_inc(chosen, 1)
                    elif k == 2:
                        nc.vector.tensor_tensor(most[:], logits[:], top_b, ALU.is_equal).then_inc(chosen, 1)
                    elif k == 3:
                        nc.vector.tensor_tensor(key[:], most[:], rank, ALU.mult).then_inc(chosen, 1)
                    elif k == 4:
                        nc.vector.tensor_reduce(top[:], key[:], AX.X, ALU.max).then_inc(chosen, 1)
                    elif k == 5:
                        nc.vector.tensor_tensor(hot[:, n % 2, :, :], rank, top_b, ALU.is_equal).then_inc(chosen, 1)
                    else:
                        if n >= 2:
                            v.wait_ge(counted, n - 1)
                        nc.vector.tensor_copy(hot_b[:, n % 2, :, :], hot[:, n % 2, :, :]).then_inc(hot_done, 1)

                def put(n, k):
                    if n or k:
                        v.wait_ge(placed, n * PLACED + min(k, 3))
                    if k == 0:
                        v.wait_ge(counted, n + 1)
                        nc.vector.tensor_tensor(slot[:], counts, g.ends[:].unsqueeze(1).to_broadcast([P, TPC, E]),
                                                ALU.add).then_inc(placed, 1)
                    elif k == 1:
                        nc.vector.tensor_tensor(slot[:], slot[:], hot[:, n % 2, :, :], ALU.mult).then_inc(placed, 1)
                    elif k == 2:
                        if n:
                            v.wait_ge(slots_done, n)
                        nc.vector.tensor_reduce(slot_f[:], slot[:], AX.X, ALU.add).then_inc(placed, 1)
                    elif k == 3:
                        nc.vector.tensor_copy(g.slots[:, n * TPC:(n + 1) * TPC], slot_f[:]).then_inc(slots_done, 1)
                    else:
                        nc.vector.tensor_tensor(g.ends[:], g.ends[:], totals, ALU.add).then_inc(placed, 1)

                v.wait_ge(g.mix_in, 16 * 4)
                nc.vector.memset(eps[:], EPS)
                nc.vector.memset(ones[:], 1.0)
                nc.vector.tensor_copy(before[:], g.const[:, C_TRI:C_TRI + P])
                nc.vector.tensor_copy(g.ends[:], g.const[:, C_REGION:C_REGION + E])
                nc.vector.tensor_copy(g.h2[:, :, D], g.const[:, C_TOKEN:C_TOKEN + NT]).then_inc(g.numbered, 1)
                for b in range(B):
                    for k in range(KC):
                        last = nc.vector.tensor_tensor(wo[b][:, k, :], wo_in[:, k, :], g.mod[:, b, 0, :], ALU.mult)
                last.then_inc(wo_ready, 1)
                for u in range(NT + TPC + GATE + 4):
                    route(u, 0)
                    if u < NT:
                        n, t = at_tile(u)
                        if t == 0:
                            v.wait_ge(x_in[n % NX], 16 * (n // NX + 1))
                        v.wait_ge(a_done, u + 1)
                        nc.vector.tensor_tensor(x1[:, n % NX, t, :], ps_a[:, u % 2, 0:D], x1[:, n % NX, t, :], ALU.add
                                                ).then_inc(x1_ready, 1)
                    w = u - 1
                    if 0 <= w < NT:
                        v.wait_ge(st_ready, w + 1)
                        if w >= RING:
                            v.wait_ge(scaled, w - RING + 1)
                            v.wait_ge(sd_ready, w - RING + 1)
                        nc.vector.bn_aggr(mv[:, w % RING, :], st[:, w % RING, :]).then_inc(mv_ready, 1)
                    w = u - 2
                    if 0 <= w < NT:
                        v.wait_ge(sd_ready, w + 1)
                        if w >= RING:
                            v.wait_ge(rescaled, w - RING + 1)
                        nc.vector.reciprocal(rs[:, w % RING:w % RING + 1], sd[:, w % RING:w % RING + 1]
                                             ).then_inc(rs_ready, 1)
                    route(u, 1)
                    if u < NT:
                        v.wait_ge(x1_ready, u + 1)
                        if u >= RING:
                            v.wait_ge(mv_ready, u - RING + 1)
                        nc.vector.bn_stats(st[:, u % RING, :], x1[:, n % NX, t, :]).then_inc(st_ready, 1)
                    route(u, 2)
                    w = u - 1
                    if 0 <= w < NT:
                        n, t = at_tile(w)
                        v.wait_ge(mv_ready, w + 1)
                        nc.vector.scalar_tensor_tensor(g.h2[:, w, 0:D], x1[:, n % NX, t, :],
                                                       mv[:, w % RING, 0:1], g.mod[:, w // (NT // B), 2, :],
                                                       ALU.subtract, ALU.mult).then_inc(scaled, 1)
                    route(u, 3)

            @block.gpsimd
            def _(gp):
                gp.wait_ge(g.mix_in, 16 * 4)
                gp.wait_ge(g.numbered, 1)
                for u in range(NT + SCATTER):
                    if u < NT:
                        gp.wait_ge(rescaled, u + 1)
                        nc.gpsimd.tensor_tensor(g.h2[:, u, 0:D], g.h2[:, u, 0:D], g.mod[:, u // (NT // B), 1, :],
                                                ALU.add).then_inc(h_ready, 1)
                    t = u - SCATTER
                    if t >= 0:
                        gp.wait_ge(slots_done, t // TPC + 1)
                        gp.wait_ge(h_ready, t + 1)
                        nc.gpsimd.indirect_dma_start(
                            out=g.sorted_h, out_offset=bass.IndirectOffsetOnAxis(ap=g.slots[:, t:t + 1], axis=0),
                            in_=g.h2[:, t, :], in_offset=None).then_inc(scattered, 16)
                gp.wait_ge(scattered, 16 * NT)


def stage_route(nc, g):
    with ExitStack() as ctx:
        sb, pb, sem = open_stage(nc, ctx)
        NS2 = SLOTS + 2
        amount = sb("amount", [P, E])
        over = sb("over", [P, E, NT])
        tiles = sb("tiles", [P, E])
        cum = sb("cum", [P, 2, E])
        first = sb("first", [P, E])
        shift = sb("shift4", [P, E])
        past, come, inside, row = (sb(n, [P, NS2, E]) for n in ("past", "come", "inside", "row"))
        exp_f, some, row_f = (sb(n, [P, NS2]) for n in ("exp_f", "some", "row_f"))
        tails = sb("tails", [P, E], i32)
        dve, tails_set, tails_out = sem("dve4"), sem("tails_set"), sem("tails_out")
        region = g.const[:, C_REGION:C_REGION + E]
        tile = g.const[:, C_TILE:C_END]
        with nc.Block() as block:
            @block.sync
            def _(sp):
                sp.wait_ge(tails_set, 1)
                for e in range(E):
                    r = sp.value_load(tails[0:1, e:e + 1], min_val=e * REGION, max_val=e * REGION + NTOK)
                    sp.dma_start(g.sorted_h[bass.ds(r, P), :], g.filler[:]).then_inc(tails_out, 16)
                sp.wait_ge(tails_out, 16 * E)

            @block.vector
            def _(v):
                def link(ins):
                    link.n += 1
                    ins.then_inc(dve, 1)
                    v.wait_ge(dve, link.n)
                link.n = 0
                nc.vector.tensor_copy(tails[:], g.ends[:]).then_inc(tails_set, 1)
                link(nc.vector.tensor_tensor(amount[:], g.ends[:], region, ALU.subtract))
                link(nc.vector.tensor_tensor(over[:], amount[:].unsqueeze(2).to_broadcast([P, E, NT]),
                                             g.const[:, C_THR:C_THR + NT].unsqueeze(1).to_broadcast([P, E, NT]),
                                             ALU.is_gt))
                link(nc.vector.tensor_reduce(tiles[:], over[:], AX.X, ALU.add))
                link(nc.vector.tensor_copy(cum[:, 0, :], tiles[:]))
                j, d = 0, 1
                while d < E:
                    nc.vector.tensor_copy(cum[:, 1 - j, 0:d], cum[:, j, 0:d])
                    link(nc.vector.tensor_tensor(cum[:, 1 - j, d:E], cum[:, j, d:E], cum[:, j, 0:E - d], ALU.add))
                    j, d = 1 - j, 2 * d
                link(nc.vector.tensor_tensor(first[:], cum[:, j, :], tiles[:], ALU.subtract))
                link(nc.vector.scalar_tensor_tensor(shift[:], first[:], -float(P), region, ALU.mult, ALU.add))
                tile_b = tile.unsqueeze(2).to_broadcast([P, NS2, E])
                nc.vector.tensor_tensor(past[:], cum[:, j, :].unsqueeze(1).to_broadcast([P, NS2, E]), tile_b, ALU.is_le)
                link(nc.vector.tensor_tensor(come[:], first[:].unsqueeze(1).to_broadcast([P, NS2, E]), tile_b,
                                             ALU.is_le))
                link(nc.vector.tensor_reduce(exp_f[:], past[:], AX.X, ALU.add))
                nc.vector.tensor_scalar(g.expert[:], exp_f[:], float(E - 1), None, ALU.min)
                link(nc.vector.tensor_tensor(inside[:], come[:], past[:], ALU.subtract))
                link(nc.vector.tensor_tensor(row[:], inside[:], shift[:].unsqueeze(1).to_broadcast([P, NS2, E]),
                                             ALU.mult))
                nc.vector.tensor_reduce(some[:], inside[:], AX.X, ALU.add)
                link(nc.vector.tensor_reduce(row_f[:], row[:], AX.X, ALU.add))
                link(nc.vector.tensor_scalar(exp_f[:], tile, float(P), -float(FILL), ALU.mult, ALU.add))
                link(nc.vector.tensor_tensor(some[:], some[:], exp_f[:], ALU.mult))
                link(nc.vector.tensor_tensor(some[:], some[:], row_f[:], ALU.add))
                nc.vector.tensor_scalar(g.start[:], some[:], float(FILL), None, ALU.add)


def stage_experts(nc, g):
    with ExitStack() as ctx:
        sb, pb, sem = open_stage(nc, ctx)
        b1s = sb("b1s", [3, E, F], bf16)
        b2s = sb("b2s", [3, E, D], bf16)
        one3 = sb("one3", [3, P], bf16)
        ht = sb("ht", [P, 2, ROW])
        number = sb("number", [P, 2])
        index = sb("index", [P, 2], i32)
        batch = sb("batch", [P, B])
        gate0 = sb("gate0", [P, D])
        gate = sb("gate", [P, 2, D])
        xg = sb("xg", [P, 2, D])
        held = sb("held", [P, 2])
        hT = sb("hT5", [P, 2, KC, P])
        ge = sb("ge", [P, 2, F])
        gT = sb("gT", [P, FC, P])
        ys = sb("ys", [P, 2, D])
        ps_x = pb("ps_x", [P, CH])
        ps_1 = pb("ps_1", [P, 2, CH])
        ps_g = pb("ps_g", [P, 2, CH])
        ps_y = pb("ps_y", [P, CH])
        w_in, set5 = sem("w_in5"), sem("set5")
        h_in = [sem(f"h_in{i}") for i in range(2)]
        x_turned, x_copied, f_done, g_done, g_turned, g_copied, y_done, y_copied = (
            sem("x_turned"), sem("x_copied"), sem("f_done"), sem("g_done"), sem("g_turned"), sem("g_copied"),
            sem("y_done"), sem("y_copied"))
        y_out = [sem(f"y_out{i}") for i in range(2)]
        xg_in = [sem(f"xg_in{i}") for i in range(2)]
        steps, holds = sem("steps5"), sem("holds")
        numbered, prepared, y_ready, xg_set = sem("numbered5"), sem("prepared"), sem("y_ready5"), sem("xg_set")

        def tiles(eng, body):
            assert SLOTS % 2
            for i in range(3):
                body(i, i % 2, i // 2)
            with eng.Fori(0, SLOTS // 2 - 1) as n:
                body(n * 2 + 3, 1, n + 1)
                body(n * 2 + 4, 0, n + 2)

        def reached(i, least):
            return not isinstance(i, int) or i >= least

        with nc.Block() as block:
            @block.sync
            def _(sp):
                sp.dma_start(b1s[:], g.b1_rows.rearrange("s (e n) -> s e n", e=E)).then_inc(w_in, 16)
                sp.dma_start(b2s[:], g.b2_rows.rearrange("s (e n) -> s e n", e=E)).then_inc(w_in, 16)

                def load(i, u):
                    r = sp.value_load(g.start[0:1, bass.ds(i, 1)], min_val=0, max_val=FILL)
                    sp.dma_start(ht[:, u, :], g.sorted_h[bass.ds(r, P), :]).then_inc(h_in[u], 16)

                def body(i, u, half_i):
                    sp.wait_ge(x_copied, i + 1)
                    load(i + 2, u)

                for i in range(2):
                    load(i, i)
                tiles(sp, body)
                sp.wait_ge(h_in[0], 16 * (SLOTS // 2 + 2))
                sp.wait_ge(h_in[1], 16 * (SLOTS // 2 + 1))

            @block.gpsimd
            def _(gp):
                def hold(earlier):
                    if reached(earlier, 1):
                        gp.wait_ge(holds, earlier)
                    nc.gpsimd.tensor_tensor(held[:, 1:2], held[:, 0:1], held[:, 0:1], ALU.add).then_inc(holds, 1)

                def body(i, u, half_i):
                    if reached(i, 1):
                        scatter(i - 1, 1 - u)
                    gp.wait_ge(prepared, i + 1)
                    hold(i * 2)
                    nc.gpsimd.indirect_dma_start(
                        out=xg[:, u, :], out_offset=None, in_=g.x1_rows,
                        in_offset=bass.IndirectOffsetOnAxis(ap=index[:, u:u + 1], axis=0),
                        bounds_check=last, oob_is_err=False).then_inc(xg_in[u], 16)

                def scatter(i, u):
                    gp.wait_ge(y_ready, i + 1)
                    hold(i * 2 + 1)
                    nc.gpsimd.indirect_dma_start(
                        out=g.out.rearrange("b s d -> (b s) d"),
                        out_offset=bass.IndirectOffsetOnAxis(ap=index[:, u:u + 1], axis=0),
                        in_=ys[:, u, :], in_offset=None,
                        bounds_check=last, oob_is_err=False).then_inc(y_out[u], 16)

                last = gp.to_reg(NTOK - 1)
                nc.gpsimd.memset(one3[:], 1.0).then_inc(set5, 1)
                nc.gpsimd.memset(xg[:], 0.0).then_inc(xg_set, 1)
                nc.gpsimd.memset(held[:], 0.0).then_inc(xg_set, 1)
                gp.wait_ge(xg_set, 2)
                tiles(gp, body)
                scatter(SLOTS - 1, 0)
                gp.wait_ge(y_out[0], 16 * (SLOTS // 2 + 1))
                gp.wait_ge(y_out[1], 16 * (SLOTS // 2))

            @block.tensor
            def _(pe):
                def turn_in(i, u, half_i):
                    pe.wait_ge(h_in[u], (half_i + 1) * 16)
                    if reached(i, 1):
                        pe.wait_ge(x_copied, i)
                    for k in range(KC):
                        mm = nc.tensor.transpose(ps_x[:, k * P:(k + 1) * P], ht[:, u, k * P:(k + 1) * P],
                                                 g.const[:, C_ID:C_ID + P])
                    mm.then_inc(x_turned, 1)

                def up(i, u, half, e):
                    pe.wait_ge(x_copied, i + 1)
                    if reached(i, 1):
                        pe.wait_ge(g_done, i * 2 + half - 1)
                    cols = slice(half * CH, (half + 1) * CH)
                    nc.tensor.matmul(ps_1[:, half, :], one3[:], b1s[:, bass.ds(e, 1), cols]
                                     .rearrange("s a n -> s (a n)"), start=True, stop=False)
                    for k in range(KC):
                        mm = nc.tensor.matmul(ps_1[:, half, :], hT[:, u, k, :],
                                              g.w1[:, k, bass.ds(e, 1), cols].rearrange("p a n -> p (a n)"),
                                              start=False, stop=(k == KC - 1))
                    mm.then_inc(f_done, 1)

                def turn_hidden(i, u):
                    for half in range(2):
                        pe.wait_ge(g_done, i * 2 + half + 1)
                        if reached(i, 1):
                            pe.wait_ge(g_copied, i * 2 + half - 1)
                        for k in range(FC // 2):
                            f = half * FC // 2 + k
                            mm = nc.tensor.transpose(ps_g[:, half, k * P:(k + 1) * P], ge[:, u, f * P:(f + 1) * P],
                                                     g.const[:, C_ID:C_ID + P])
                        mm.then_inc(g_turned, 1)

                def down(i):
                    e = pe.value_load(g.expert[0:1, bass.ds(i, 1)], min_val=0, max_val=E - 1)
                    pe.wait_ge(y_copied, i + 1)
                    nc.tensor.matmul(ps_y[:, 0:D], one3[:], b2s[:, bass.ds(e, 1), :].rearrange("s a n -> s (a n)"),
                                     start=True, stop=False)
                    for f in range(FC):
                        if f % (FC // 2) == 0:
                            pe.wait_ge(g_copied, i * 2 + f // (FC // 2) + 1)
                        mm = nc.tensor.matmul(ps_y[:, 0:D], gT[:, f, :],
                                              g.w2_s[:, f, bass.ds(e, 1), :].rearrange("p a n -> p (a n)"),
                                              start=False, stop=(f == FC - 1))
                    mm.then_inc(y_done, 1)

                def body(i, u, half_i):
                    e = pe.value_load(g.expert[0:1, bass.ds(i, 1)], min_val=0, max_val=E - 1)
                    up(i, u, 0, e)
                    up(i, u, 1, e)
                    turn_in(i + 1, 1 - u, half_i + u)
                    if reached(i, 1):
                        down(i - 1)
                    turn_hidden(i, u)

                pe.wait_ge(set5, 1)
                pe.wait_ge(w_in, 32)
                turn_in(0, 0, 0)
                pe.wait_ge(g.w1_in, 16 * KC)
                pe.wait_ge(g.w2_in, 16 * FC)
                tiles(pe, body)
                down(SLOTS - 1)

            @block.scalar
            def _(act):
                def body(i, u, half_i):
                    for half in range(2):
                        act.wait_ge(f_done, i * 2 + half + 1)
                        nc.scalar.activation(ge[:, u, half * CH:(half + 1) * CH], ps_1[:, half, :], ACT.Gelu
                                             ).then_inc(g_done, 1)

                tiles(act, body)

            @block.vector
            def _(v):
                def turned_in(i, u):
                    v.wait_ge(x_turned, i + 1)
                    nc.vector.tensor_copy(number[:, u:u + 1], ht[:, u, D:ROW]).then_inc(numbered, 1)
                    nc.vector.tensor_copy(hT[:, u, :, :], ps_x[:, 0:D].rearrange("p (k t) -> p k t", k=KC)
                                          ).then_inc(x_copied, 1)

                def prepare(i, u, half_i):
                    v.wait_ge(numbered, i + 1)
                    if reached(i, 2):
                        v.wait_ge(y_out[u], half_i * 16)
                    nc.vector.tensor_scalar(batch[:, 0:1], number[:, u:u + 1], float(S), None, ALU.is_lt)
                    nc.vector.tensor_scalar(batch[:, 1:2], number[:, u:u + 1], float(S), None, ALU.is_ge)
                    nc.vector.tensor_copy(index[:, u:u + 1], number[:, u:u + 1]).then_inc(steps, 1)
                    v.wait_ge(steps, i * 2 + 1)
                    nc.vector.tensor_scalar(gate0[:], g.mod[:, 0, 3, :], batch[:, 0:1], None, ALU.mult
                                            ).then_inc(steps, 1)
                    v.wait_ge(steps, i * 2 + 2)
                    nc.vector.scalar_tensor_tensor(gate[:, u, :], g.mod[:, 1, 3, :], batch[:, 1:2], gate0[:],
                                                   ALU.mult, ALU.add).then_inc(prepared, 1)

                def output(i, u, half_i):
                    v.wait_ge(y_done, i + 1)
                    v.wait_ge(prepared, i + 1)
                    nc.vector.tensor_tensor(ys[:, u, :], ps_y[:, 0:D], gate[:, u, :], ALU.mult).then_inc(y_copied, 1)
                    v.wait_ge(y_copied, i + 2)
                    v.wait_ge(xg_in[u], half_i * 16 + 16)
                    nc.vector.tensor_tensor(ys[:, u, :], ys[:, u, :], xg[:, u, :], ALU.add).then_inc(y_ready, 1)

                def body(i, u, half_i):
                    turned_in(i + 1, 1 - u)
                    if reached(i, 1):
                        output(i - 1, 1 - u, half_i + u - 1)
                    for half in range(2):
                        v.wait_ge(g_turned, i * 2 + half + 1)
                        nc.vector.tensor_copy(gT[:, half * FC // 2:(half + 1) * FC // 2, :],
                                              ps_g[:, half, :].rearrange("p (k t) -> p k t", t=P)
                                              ).then_inc(g_copied, 1)
                    prepare(i, u, half_i)

                v.sem_inc(y_copied, 1)
                turned_in(0, 0)
                tiles(v, body)
                output(SLOTS - 1, 0, SLOTS // 2)


def build(nc, g, stages=(1, 2, 3, 4, 5)):
    def dram(name, shape, dt):
        return nc.dram_tensor(name, shape, dt, kind="Internal").ap()

    g.qk_rows = dram("qk_rows", (NIT, 2, 3, G * HD, S), bf16)
    g.v_rows = dram("v_rows", (NIT, S, P), fp32)
    g.pos_rows = dram("pos_rows", (NIT, 3, G * S), bf16)
    g.one_rows = dram("one_rows", (3, G * S), bf16)
    g.mod_rows = dram("mod_rows", (B, 4, D), fp32)
    g.att_rows = dram("att_rows", (NIT, P, S // P, G * HD), fp32)
    g.b1_rows = dram("b1_rows", (3, E * F), bf16)
    g.b2_rows = dram("b2_rows", (3, E * D), bf16)
    g.x1_rows = dram("x1_rows", (NTOK, D), fp32)
    g.sorted_h = dram("sorted_h", (FILL + P, ROW), fp32)
    with ExitStack() as ctx:
        sb, pb, sem = open_stage(nc, ctx)
        g.const = sb("const", [P, C_END])
        g.ident_b = sb("ident_b", [P, P], bf16)
        g.mask_q = sb("mask_q", [P, P], bf16)
        g.mask_k = sb("mask_k", [P, P], bf16)
        g.mod = sb("mod", [P, B, 4, D])
        g.wo_in = sb("wo_in", [P, KC, D])
        g.wg_s = sb("wg_s", [P, KC, E])
        g.bg_s = sb("bg_s", [P, E])
        g.filler = sb("filler", [P, ROW])
        g.ends = sb("ends", [P, E])
        g.slots = sb("slots", [P, NT], i32)
        g.expert = sb("expert", [P, SLOTS + 2], i32)
        g.start = sb("start", [P, SLOTS + 2], i32)
        g.numbered = sem("numbered")
        g.parts_out = [sem(f"parts_out{i}") for i in range(NPARTS)]
        g.v_out = [sem(f"v_out{i}") for i in range(2)]
        g.mix_in, g.w1_in, g.w2_in = sem("mix_in"), sem("w1_in"), sem("w2_in")
        g.ones_in = [sem(f"ones_in{i}") for i in range(2)]
        g.loaded = [sem(f"loaded{i}") for i in range(2)]
        g.w1 = sb("w1", [P, KC, E, F])
        with ExitStack() as rounds:
            def buffer(name, shape, dt):
                return rounds.enter_context(nc.sbuf_tensor(name, shape, dt))

            g.kh, g.qh, g.vh = [], [], []

            def round_buffers(u):
                g.kh.append(buffer(f"kh{u}", [P, G, S], bf16))
                g.qh.append(buffer(f"qh{u}", [P, G, S], bf16))
                g.vh.append(buffer(f"vh{u}", [P, S // P, P], fp32))

            round_buffers(0)
            g.parts = buffer("parts", [P, NPARTS, 3, CH], bf16)
            g.vp = buffer("vp", [P, 2, 2, H, HW], fp32)
            if 1 in stages: stage_qkv(nc, g)
            round_buffers(1)
            if 2 in stages: stage_attention(nc, g)
        g.w2_s = sb("w2_s", [P, FC, E, D])
        with ExitStack() as mid:
            g.h2 = mid.enter_context(nc.sbuf_tensor("h2", [P, NT, ROW], fp32))
            if 3 in stages: stage_mix(nc, g)
            if 4 in stages: stage_route(nc, g)
        if 5 in stages: stage_experts(nc, g)


def constants():
    c = np.zeros((P, C_END), np.float32)
    i, j = np.arange(P)[:, None], np.arange(P)[None, :]
    c[:, C_ID:C_ID + P] = i == j
    c[:, C_MQ:C_MQ + P] = np.where(j > i, -1e30, 0.0)
    c[:, C_MK:C_MK + P] = np.where(j < i, -1e30, 0.0)
    c[:, C_TRI:C_TRI + P] = i < j
    c[:, C_RANK:C_RANK + E] = E - np.arange(E)
    c[:, C_THR:C_THR + NT] = P * np.arange(NT)
    c[:, C_TOKEN:C_TOKEN + NT] = P * np.arange(NT) + i
    c[:, C_REGION:C_REGION + E] = REGION * np.arange(E)
    c[:, C_TILE:C_END] = np.arange(SLOTS + 2)
    start = 2.0 ** (-2.0 ** -(np.log2(H) - 3))
    slopes = np.array([start * start ** i for i in range(H)], np.float32)
    alibi = -slopes[:, None] * np.arange(S, dtype=np.float32)[None, :]
    return c, alibi.astype(np.float32)


def laid_out(inputs):
    a = {k: np.ascontiguousarray(np.asarray(v)) for k, v in inputs.items()}
    const, alibi = constants()
    return {
        "x": a["L0_attn_x"],
        "wqkvT": np.ascontiguousarray(a["L0_attn_W_qkv"].T),
        "woT": np.ascontiguousarray(a["L0_attn_W_o"].T),
        "wg": a["L0_ffn_Wg"], "bg": a["L0_ffn_bg"],
        "w1_dram": a["L0_ffn_W1"], "b1": a["L0_ffn_b1"], "w2": a["L0_ffn_W2"], "b2": a["L0_ffn_b2"],
        "cT": np.ascontiguousarray(a["L0_c"].T.reshape(KC, P, B).transpose(1, 0, 2)),
        "wmod": a["L0_wmod"],
        "const_dram": const, "alibi": alibi,
    }


def kernel(**inputs):
    import concourse.bacc as _bacc
    from concourse.bass_utils import run_bass_kernel_spmd as _run

    nc = _bacc.Bacc("TRN2", target_bir_lowering=False, num_devices=1)
    g, arrays = Tensors(), {}
    for name, a in laid_out(inputs).items():
        arrays["in_" + name] = a
        g.__dict__[name] = nc.dram_tensor("in_" + name, a.shape, mybir.dt.from_np(a.dtype), kind="ExternalInput").ap()
    g.out = nc.dram_tensor("out_0", (B, S, D), fp32, kind="ExternalOutput").ap()
    build(nc, g)
    r = _run(nc, [arrays], core_ids=[0])
    return r.results[0]["out_0"]
```
